# Optimizing a Trainium2 kernel written in Bass

```python
import numpy as np
import jax
import jax.numpy as jnp

def _softmax(x, axis=-1):
    return jax.nn.softmax(x, axis=axis)

def _gelu(x):
    return jax.nn.gelu(x, approximate=True)

def _silu(x):
    return jax.nn.silu(x)

def _sigmoid(x):
    return jax.nn.sigmoid(x)

def _layernorm(x, axis=-1, eps=1e-05):
    m = jnp.mean(x, axis=axis, keepdims=True)
    v = jnp.var(x, axis=axis, keepdims=True)
    return (x - m) / jnp.sqrt(v + eps)

def _scatter_add(tgt, idx, src, axis=0):
    return tgt.at[idx].add(src)

def _segment_sum(src, seg, n):
    return jax.ops.segment_sum(src, seg, n)
kernel_name = 'mk_seq_preln_d2_jaxref_r8_3d6d4e'

def setup_inputs(seed: int=0):
    np.random.seed(seed)
    _w = jnp.asarray

    def _L0_attn_setup():
        import jax, jax.numpy as jnp
        import numpy as np
        DIM = 128
        N_HEADS = 16
        HEAD_DIM = DIM // N_HEADS
        B, T = (2, 256)
        ROPE_THETA = 32.0
        EPS = 1e-06

        def precompute_freqs_1d(dim, seq_len, theta):
            freqs = theta ** (-jnp.arange(0, dim, 2, dtype=jnp.float32) / dim)
            t = jnp.arange(seq_len, dtype=jnp.float32)
            ang = t[:, None] * freqs[None, :]
            return (jnp.cos(ang), jnp.sin(ang))

        def _rms_norm(t, w):
            var = jnp.mean(t * t, axis=-1, keepdims=True)
            return t * jax.lax.rsqrt(var + EPS) * w

        def _rope(q, k, cos, sin):
            cos = cos[None, None]
            sin = sin[None, None]
            q1, q2 = jnp.split(q, 2, axis=-1)
            k1, k2 = jnp.split(k, 2, axis=-1)
            q_out = jnp.concatenate([q1 * cos - q2 * sin, q2 * cos + q1 * sin], axis=-1)
            k_out = jnp.concatenate([k1 * cos - k2 * sin, k2 * cos + k1 * sin], axis=-1)
            return (q_out, k_out)
        key = jax.random.key(seed)
        k1, k2, k3, k4, k5 = jax.random.split(key, 5)
        x = jax.random.normal(k1, (B, T, DIM), dtype=jnp.float32)
        w_qkv = jax.random.normal(k2, (3 * DIM, DIM), dtype=jnp.float32) * DIM ** (-0.5)
        w_proj = jax.random.normal(k3, (DIM, DIM), dtype=jnp.float32) * DIM ** (-0.5)
        q_norm_w = 1.0 + 0.1 * jax.random.normal(k4, (HEAD_DIM,), dtype=jnp.float32)
        k_norm_w = 1.0 + 0.1 * jax.random.normal(k5, (HEAD_DIM,), dtype=jnp.float32)
        return {'x': x, 'w_qkv': w_qkv, 'w_proj': w_proj, 'q_norm_w': q_norm_w, 'k_norm_w': k_norm_w}
    _L0_attn_in = _L0_attn_setup()

    def _L0_ffn_setup():
        import jax, jax.numpy as jnp
        import numpy as np
        B, N, D = (4, 256, 128)
        SPARSITY = 0.01
        key = jax.random.key(seed)
        k1, k2, k3 = jax.random.split(key, 3)
        x = jax.random.normal(k1, (B, N, D), dtype=jnp.float32)
        spatial = jax.random.normal(k2, (D, D), dtype=jnp.float32) * 0.02
        freq = jnp.fft.fft(spatial, axis=-1)
        k = int(D * SPARSITY)
        mag = jnp.abs(freq)
        kth = jax.lax.top_k(mag, k)[0][:, -1:]
        w_sparse = jnp.where(mag >= kth, freq, 0.0 + 0j)
        bias = jax.random.normal(k3, (D,), dtype=jnp.float32) * 0.01
        return {'x': x, 'w_freq_real': jnp.real(w_sparse).astype(jnp.float32), 'w_freq_imag': jnp.imag(w_sparse).astype(jnp.float32), 'bias': bias}
    _L0_ffn_in = _L0_ffn_setup()

    def _L1_attn_setup():
        import jax, jax.numpy as jnp
        import numpy as np
        DIM = 128
        HEADS = 16
        HEAD_DIM = DIM // HEADS
        B, N = (4, 512)

        def _reference_tuple_inner(x, Wq, bq, Wk, bk, Wv, bv, Wo, bo, stdp):
            b, n, d = x.shape
            h, dh = (HEADS, HEAD_DIM)

            def proj(W, bias):
                return (x @ W.T + bias).reshape(b, n, h, dh).transpose(0, 2, 1, 3)
            Q = jax.nn.elu(proj(Wq, bq)) + 1.0
            K = jax.nn.elu(proj(Wk, bk)) + 1.0
            V = proj(Wv, bv)
            stdp_w = jax.nn.sigmoid(stdp).reshape(1, h, 1, 1)
            KV = jnp.einsum('bhnd,bhnv->bhdv', K, V)
            K_sum = K.sum(axis=2)
            numerator = jnp.einsum('bhnd,bhdv->bhnv', Q, KV)
            denominator = jnp.einsum('bhnd,bhd->bhn', Q, K_sum)[..., None] + 1e-06
            attn_out = numerator / denominator * stdp_w
            out = attn_out.transpose(0, 2, 1, 3).reshape(b, n, d)
            out = out @ Wo.T + bo
            return (out, jax.lax.stop_gradient(stdp))
        key = jax.random.key(seed)
        ks = jax.random.split(key, 10)
        s = 1.0 / np.sqrt(DIM)
        return {'x': jax.random.normal(ks[0], (B, N, DIM), dtype=jnp.float32), 'Wq': jax.random.uniform(ks[1], (DIM, DIM), jnp.float32, -s, s), 'bq': jax.random.uniform(ks[2], (DIM,), jnp.float32, -s, s), 'Wk': jax.random.uniform(ks[3], (DIM, DIM), jnp.float32, -s, s), 'bk': jax.random.uniform(ks[4], (DIM,), jnp.float32, -s, s), 'Wv': jax.random.uniform(ks[5], (DIM, DIM), jnp.float32, -s, s), 'bv': jax.random.uniform(ks[6], (DIM,), jnp.float32, -s, s), 'Wo': jax.random.uniform(ks[7], (DIM, DIM), jnp.float32, -s, s), 'bo': jax.random.uniform(ks[8], (DIM,), jnp.float32, -s, s), 'stdp': jnp.ones((HEADS,), dtype=jnp.float32)}
    _L1_attn_in = _L1_attn_setup()

    def _L1_ffn_setup():
        import jax, jax.numpy as jnp
        import numpy as np
        B, T, DIM = (4, 128, 128)
        H, E, DH, K = (8, 5, 64, 3)

        def _topk_mask(s, k):
            idx = jax.lax.top_k(s, k)[1]
            return jnp.sum(jax.nn.one_hot(idx, s.shape[-1], dtype=s.dtype), axis=-2)
        key = jax.random.key(seed)
        ks = jax.random.split(key, 6)
        w = lambda k, shape: jax.random.normal(k, shape, jnp.float32) * 0.02
        return {'x': jax.random.normal(ks[0], (B, T, DIM), jnp.float32), 'Wq': w(ks[1], (DIM, H * E * DH)), 'Wkv': w(ks[2], (DIM, 2 * H * E * DH)), 'Ws': w(ks[3], (DIM, H * E)), 'Wd': w(ks[4], (DIM, H * E)), 'Wo': w(ks[5], (DH, E * DIM))}
    _L1_ffn_in = _L1_ffn_setup()
    _d = {'L0_attn_x': _L0_attn_in['x'], 'L0_attn_w_qkv': _L0_attn_in['w_qkv'], 'L0_attn_w_proj': _L0_attn_in['w_proj'], 'L0_attn_q_norm_w': _L0_attn_in['q_norm_w'], 'L0_attn_k_norm_w': _L0_attn_in['k_norm_w'], 'L0_ffn_w_freq_real': _L0_ffn_in['w_freq_real'], 'L0_ffn_w_freq_imag': _L0_ffn_in['w_freq_imag'], 'L0_ffn_bias': _L0_ffn_in['bias'], 'L1_attn_Wq': _L1_attn_in['Wq'], 'L1_attn_bq': _L1_attn_in['bq'], 'L1_attn_Wk': _L1_attn_in['Wk'], 'L1_attn_bk': _L1_attn_in['bk'], 'L1_attn_Wv': _L1_attn_in['Wv'], 'L1_attn_bv': _L1_attn_in['bv'], 'L1_attn_Wo': _L1_attn_in['Wo'], 'L1_attn_bo': _L1_attn_in['bo'], 'L1_attn_stdp': _L1_attn_in['stdp'], 'L1_ffn_Wq': _L1_ffn_in['Wq'], 'L1_ffn_Wkv': _L1_ffn_in['Wkv'], 'L1_ffn_Ws': _L1_ffn_in['Ws'], 'L1_ffn_Wd': _L1_ffn_in['Wd'], 'L1_ffn_Wo': _L1_ffn_in['Wo']}
    _x0 = _d['L0_attn_x']
    _d['L0_attn_x'] = jax.random.normal(jax.random.fold_in(jax.random.key(seed), 1), (1, 2048, 128), dtype=_x0.dtype)
    del _x0
    return _d

def reference(L0_attn_x, L0_attn_w_qkv, L0_attn_w_proj, L0_attn_q_norm_w, L0_attn_k_norm_w, L0_ffn_w_freq_real, L0_ffn_w_freq_imag, L0_ffn_bias, L1_attn_Wq, L1_attn_bq, L1_attn_Wk, L1_attn_bk, L1_attn_Wv, L1_attn_bv, L1_attn_Wo, L1_attn_bo, L1_attn_stdp, L1_ffn_Wq, L1_ffn_Wkv, L1_ffn_Ws, L1_ffn_Wd, L1_ffn_Wo):

    def _L0_attn_ref(x, w_qkv, w_proj, q_norm_w, k_norm_w):
        import jax, jax.numpy as jnp
        import numpy as np
        DIM = 128
        N_HEADS = 16
        HEAD_DIM = DIM // N_HEADS
        B, T = (2, 256)
        ROPE_THETA = 32.0
        EPS = 1e-06

        def precompute_freqs_1d(dim, seq_len, theta):
            freqs = theta ** (-jnp.arange(0, dim, 2, dtype=jnp.float32) / dim)
            t = jnp.arange(seq_len, dtype=jnp.float32)
            ang = t[:, None] * freqs[None, :]
            return (jnp.cos(ang), jnp.sin(ang))

        def _rms_norm(t, w):
            var = jnp.mean(t * t, axis=-1, keepdims=True)
            return t * jax.lax.rsqrt(var + EPS) * w

        def _rope(q, k, cos, sin):
            cos = cos[None, None]
            sin = sin[None, None]
            q1, q2 = jnp.split(q, 2, axis=-1)
            k1, k2 = jnp.split(k, 2, axis=-1)
            q_out = jnp.concatenate([q1 * cos - q2 * sin, q2 * cos + q1 * sin], axis=-1)
            k_out = jnp.concatenate([k1 * cos - k2 * sin, k2 * cos + k1 * sin], axis=-1)
            return (q_out, k_out)
        Bc, Tc, C = x.shape
        scale = HEAD_DIM ** (-0.5)
        qkv = x @ w_qkv.T
        qkv = qkv.reshape(Bc, Tc, 3, N_HEADS, HEAD_DIM).transpose(2, 0, 3, 1, 4)
        q, k, v = (qkv[0], qkv[1], qkv[2])
        q = _rms_norm(q, q_norm_w)
        k = _rms_norm(k, k_norm_w)
        cos, sin = precompute_freqs_1d(HEAD_DIM, Tc, ROPE_THETA)
        q, k = _rope(q, k, cos, sin)
        attn = jnp.einsum('bhqd,bhkd->bhqk', q, k) * scale
        causal = jnp.triu(jnp.ones((Tc, Tc), dtype=bool), k=1)
        attn = jnp.where(causal, -jnp.inf, attn)
        attn = jax.nn.softmax(attn, axis=-1)
        out = jnp.einsum('bhqk,bhkd->bhqd', attn, v)
        out = out.transpose(0, 2, 1, 3).reshape(Bc, Tc, C)
        return out @ w_proj.T

    def _L0_ffn_ref(x, w_freq_real, w_freq_imag, bias):
        import jax, jax.numpy as jnp
        import numpy as np
        B, N, D = (4, 256, 128)
        SPARSITY = 0.01
        w = jax.lax.complex(w_freq_real, w_freq_imag)
        x_freq = jnp.fft.fft(x, axis=-1)
        y_freq = jnp.einsum('bnd,do->bno', x_freq, w)
        y = jnp.real(jnp.fft.ifft(y_freq, axis=-1))
        return y + bias

    def _L1_attn_ref(x, Wq, bq, Wk, bk, Wv, bv, Wo, bo, stdp):
        import jax, jax.numpy as jnp
        import numpy as np
        DIM = 128
        HEADS = 16
        HEAD_DIM = DIM // HEADS
        B, N = (4, 512)

        def _reference_tuple_inner(x, Wq, bq, Wk, bk, Wv, bv, Wo, bo, stdp):
            b, n, d = x.shape
            h, dh = (HEADS, HEAD_DIM)

            def proj(W, bias):
                return (x @ W.T + bias).reshape(b, n, h, dh).transpose(0, 2, 1, 3)
            Q = jax.nn.elu(proj(Wq, bq)) + 1.0
            K = jax.nn.elu(proj(Wk, bk)) + 1.0
            V = proj(Wv, bv)
            stdp_w = jax.nn.sigmoid(stdp).reshape(1, h, 1, 1)
            KV = jnp.einsum('bhnd,bhnv->bhdv', K, V)
            K_sum = K.sum(axis=2)
            numerator = jnp.einsum('bhnd,bhdv->bhnv', Q, KV)
            denominator = jnp.einsum('bhnd,bhd->bhn', Q, K_sum)[..., None] + 1e-06
            attn_out = numerator / denominator * stdp_w
            out = attn_out.transpose(0, 2, 1, 3).reshape(b, n, d)
            out = out @ Wo.T + bo
            return (out, jax.lax.stop_gradient(stdp))
        return _reference_tuple_inner(x, Wq, bq, Wk, bk, Wv, bv, Wo, bo, stdp)[0]

    def _L1_ffn_ref(x, Wq, Wkv, Ws, Wd, Wo):
        import jax, jax.numpy as jnp
        import numpy as np
        B, T, DIM = (4, 128, 128)
        H, E, DH, K = (8, 5, 64, 3)

        def _topk_mask(s, k):
            idx = jax.lax.top_k(s, k)[1]
            return jnp.sum(jax.nn.one_hot(idx, s.shape[-1], dtype=s.dtype), axis=-2)
        b, t, _ = x.shape
        scale = DH ** (-0.5)
        ss = jax.nn.sigmoid(x @ Ws).reshape(b, t, H, E)
        sd = jax.nn.sigmoid(x @ Wd).reshape(b, t, H, E)
        ms = _topk_mask(ss, K)
        md = _topk_mask(sd, K)
        ss_g = ss * ms
        sd_g = sd * md
        q5 = (x @ Wq).reshape(b, t, H, E, DH)
        kv = (x @ Wkv).reshape(b, t, 2, H, E, DH)
        k5, v5 = (kv[:, :, 0], kv[:, :, 1])
        q = jnp.einsum('bthed,bthe->bhtd', q5, sd_g)
        k = jnp.einsum('bthed,bthe->bhtd', k5, ss_g)
        v = jnp.einsum('bthed,bthe->bhtd', v5, ss_g)
        attn = jax.nn.softmax(jnp.einsum('bhid,bhjd->bhij', q * scale, k), axis=-1)
        out = jnp.einsum('bhij,bhjd->bihd', attn, v)
        o5 = jnp.einsum('bthd,dm->bthm', out, Wo).reshape(b, t, H, E, DIM)
        return jnp.einsum('bthem,bthe->btm', o5, md)
    x = L0_attn_x
    x = x + _L0_attn_ref(_layernorm(x, axis=-1), L0_attn_w_qkv, L0_attn_w_proj, L0_attn_q_norm_w, L0_attn_k_norm_w)
    x = x + _L0_ffn_ref(_layernorm(x, axis=-1), L0_ffn_w_freq_real, L0_ffn_w_freq_imag, L0_ffn_bias)
    x = x + _L1_attn_ref(_layernorm(x, axis=-1), L1_attn_Wq, L1_attn_bq, L1_attn_Wk, L1_attn_bk, L1_attn_Wv, L1_attn_bv, L1_attn_Wo, L1_attn_bo, L1_attn_stdp)
    x = x + _L1_ffn_ref(_layernorm(x, axis=-1), L1_ffn_Wq, L1_ffn_Wkv, L1_ffn_Ws, L1_ffn_Wd, L1_ffn_Wo)
    return x

_drawn_inputs = setup_inputs


def setup_inputs(seed=0):
    import zlib

    import numpy as np

    out = dict(_drawn_inputs(seed))
    spreads = {'L1_attn_stdp': (1.0, 0.6)}
    factors = {'L0_attn_q_norm_w': 6.809,
     'L0_attn_k_norm_w': 5.752,
     'L0_ffn_bias': 6.107,
     'L1_attn_Wq': 8.0,
     'L1_attn_bq': 8.0,
     'L1_attn_Wk': 8.0,
     'L1_attn_bk': 8.0,
     'L1_attn_Wv': 6.994,
     'L1_attn_bv': 2.702,
     'L1_attn_Wo': 2.815,
     'L1_ffn_Wq': 8.0,
     'L1_ffn_Wkv': 4.627,
     'L1_ffn_Ws': 6.115,
     'L1_ffn_Wd': 8.0,
     'L1_ffn_Wo': 5.313}
    for name, (base, spread) in spreads.items():
        noise = np.random.default_rng([zlib.crc32(name.encode()), seed]).standard_normal(out[name].shape)
        drawn = base * np.exp(spread * noise) if base else spread * noise
        out[name] = jnp.asarray(drawn.astype(out[name].dtype))
    for name, factor in factors.items():
        out[name] = (out[name] * factor).astype(out[name].dtype)
    return out
```

```python
from contextlib import ExitStack

import numpy as np

import concourse.bass as bass
from concourse import mybir

F32 = mybir.dt.float32
F32R = mybir.dt.float32r
BF16 = mybir.dt.bfloat16
ALU = mybir.AluOpType
ACT = mybir.ActivationFunctionType
AX = mybir.AxisListType

P = 128
T = 2048
NT = T // P
D = 128
CH = 512
NC = T // CH
TPC = CH // P
H0, D0 = 16, 8
GH = 4
NG = H0 // GH
H1, E1, D1 = 8, 5, 64
TOP = 3
LN_EPS = 1e-5
RMS_EPS = 1e-6
NEG = -1e30
NP = 6
NS = 3
ACC, AUX = 6, 7


def build(nc, A):
    ctx = ExitStack()
    with ctx:
        def sem(name):
            return ctx.enter_context(nc.semaphore(name))

        def sbuf(stack, name, shape, dt=F32):
            return stack.enter_context(nc.sbuf_tensor(name, shape, dt))

        ps = ctx.enter_context(nc.psum_tensor("ps", [P, 8, CH], F32))

        x = sbuf(ctx, "x", [P, NT, D])
        ident = sbuf(ctx, "ident", [P, P])
        eps = sbuf(ctx, "eps", [P, 2])
        stats = sbuf(ctx, "stats", [P, NT, 6])
        meanvar = sbuf(ctx, "meanvar", [P, NT, 2])
        std = sbuf(ctx, "std", [P, NT])
        rstd = sbuf(ctx, "rstd", [P, NT])
        pbuf = sbuf(ctx, "pbuf", [P, NP, 2, CH])
        oT = sbuf(ctx, "oT", [P, 2, CH])

        l0 = ExitStack()
        s0 = lambda name, shape, dt=F32: sbuf(l0, name, shape, dt)
        identb = s0("identb", [P, P], BF16)
        masks = s0("masks", [P, 2, P])
        masksb = s0("masksb", [P, 2, P], BF16)
        wqkv = s0("wqkv", [P, 3 * D])
        wproj = s0("wproj", [P, D])
        normw = s0("normw", [P, 2, D0])
        rope = s0("rope", [P, NT, 2, D0 // 2])
        dft = s0("dft", [P, 2, P])
        ndft = s0("ndft", [P, P])
        wfreq = s0("wfreq", [P, 2, P])
        ab = s0("ab", [P, 2, P])
        mix = s0("mix", [P, P])
        bias0 = s0("bias0", [P, D])
        xn = s0("xn", [P, NT, D])
        xnT = s0("xnT", [P, T])
        qkv = s0("qkv", [P, NT, 3 * D])
        ms = s0("ms", [P, NT, 2 * H0])
        tmp = s0("tmp", [P, NT, 2 * H0, D0])
        stageq = s0("stageq", [P, NT, GH, 32])
        stagek = s0("stagek", [P, NT, GH, 32])
        stagev = s0("stagev", [P, 2, NT, GH, 32])
        qT = s0("qT", [P, 2, T], F32R)
        kT = s0("kT", [P, 2, T], F32R)
        kM = s0("kM", [P, GH, T], F32R)
        mx = s0("mx", [P, NT, GH])
        rden = s0("rden", [P, TPC, GH])
        l0.close()

        l1 = ExitStack()
        s1 = lambda name, shape, dt=F32: sbuf(l1, name, shape, dt)
        fold = s1("fold", [P, D1])
        ones = s1("ones", [P, 1])
        wgate = s1("wgate", [P, 2, H1 * E1])
        wout = s1("wout", [P, 3, D])
        lin = ExitStack()
        sl = lambda name, shape, dt=F32: sbuf(lin, name, shape, dt)
        wlin = sl("wlin", [P, 4, D])
        blin = sl("blin", [P, 3, D])
        bqcol = sl("bqcol", [P, 1])
        stdp = sl("stdp", [P, 3, H0])
        blockm = sl("blockm", [P, D])
        bd = sl("bd", [P, 3, D])
        qfT = sl("qfT", [P, T])
        lt = sl("lt", [P, 2, 2, CH])
        kf = sl("kf", [P, NT, D])
        vf = sl("vf", [P, NT, D + 2])
        aT = sl("aT", [P, T])
        lin.close()
        z = s1("z", [P, NT, E1, D1])
        zT = s1("zT", [P, 3, P])
        xh = s1("xh", [P, T], F32R)
        xl = s1("xl", [P, T], F32R)
        sig = s1("sig", [P, NT, 2, H1, E1])
        rank = s1("rank", [P, NT, 2, H1, E1])
        gate = s1("gate", [P, NT, 3, H1, E1])
        wraw = s1("wraw", [P, 3, E1 * D1])
        wh = s1("wh", [P, 3, E1 * D1], F32R)
        wl = s1("wl", [P, 3, E1 * D1], F32R)
        gt = s1("gt", [P, 2, 3, E1, D1])
        gs = s1("gs", [P, 3, 2, D1])
        gsum = s1("gsum", [P, 3, D1])
        h_qkv = s1("h_qkv", [P, 3, NT, D1])
        den = s1("den", [P, 2, 2, CH])
        on = s1("on", [P, TPC, D1])
        onm = s1("onm", [P, TPC, E1, D1])
        rd1 = s1("rd1", [P, TPC])
        mx1 = s1("mx1", [P, NT])
        ranking = ExitStack()
        y_n = sbuf(ranking, "y_n", [P, NT, D])
        y_nT = sbuf(ranking, "y_nT", [P, T])
        beats = sbuf(ranking, "beats", [P, 2, 2 * NT * H1, E1 - 1])
        ranking.close()
        sq1 = s1("sq1", [P, NT, P])
        sq2 = s1("sq2", [P, NT, P])
        sk1 = s1("sk1", [P, NT, P])
        sk2 = s1("sk2", [P, NT, P])
        q1T = s1("q1T", [P, T], F32R)
        q2T = s1("q2T", [P, T], F32R)
        k1T = s1("k1T", [P, T], F32R)
        k2T = s1("k2T", [P, T], F32R)
        l1.close()

        s_load = sem("s_load")
        s_load1 = sem("s_load1")
        s_w = sem("s_w")
        s_out = sem("s_out")
        s_const = sem("s_const")
        s_pconst = sem("s_pconst")
        s_dve = sem("s_dve")
        s_pool = sem("s_pool")
        s_act = sem("s_act")
        s_mv = sem("s_mv")
        s_std = sem("s_std")
        s_xn = sem("s_xn")
        s_tp = sem("s_tp")
        s_xnT = sem("s_xnT")
        s_qkv = sem("s_qkv")
        s_qkvev = sem("s_qkvev")
        s_ms = sem("s_ms")
        s_rms = sem("s_rms")
        s_roped = sem("s_roped")
        s_stage = sem("s_stage")
        s_stagev = sem("s_stagev")
        s_gt = sem("s_gt")
        s_gev = sem("s_gev")
        s_kM = sem("s_kM")
        s_mxmm = sem("s_mxmm")
        s_mx = sem("s_mx")
        s_sc = sem("s_sc")
        s_exp = sem("s_exp")
        s_av = sem("s_av")
        s_oT = sem("s_oT")
        s_ot = sem("s_ot")
        s_attn = sem("s_attn")
        s_pj = sem("s_pj")
        s_res = sem("s_res")
        s_mixw = sem("s_mixw")
        s_mixc = sem("s_mixc")
        s_lin = sem("s_lin")
        s_lind = sem("s_lind")
        s_lina = sem("s_lina")
        s_lq = sem("s_lq")
        s_g1 = sem("s_g1")
        s_g2 = sem("s_g2")
        s_gate = sem("s_gate")
        s_wh = sem("s_wh")
        s_proj = sem("s_proj")
        s_gated = sem("s_gated")
        s_gadd = sem("s_gadd")
        s_st1 = sem("s_st1")
        s_t1 = sem("s_t1")
        s_t1ev = sem("s_t1ev")
        s_mm1 = sem("s_mm1")
        s_mx1 = sem("s_mx1")
        s_sc1 = sem("s_sc1")
        s_exp1 = sem("s_exp1")
        s_av1 = sem("s_av1")
        s_den1 = sem("s_den1")
        s_oT1 = sem("s_oT1")
        s_fin1 = sem("s_fin1")
        s_on1 = sem("s_on1")
        s_z = sem("s_z")
        s_zt = sem("s_zt")
        s_zT = sem("s_zT")
        s_y = sem("s_y")

        STEPS0 = [(c, jt) for c in range(NC) for jt in range(TPC * (c + 1))]
        N0 = len(STEPS0)
        LAST0 = [TPC * (c + 1) * (c + 2) // 2 for c in range(NC)]
        M1 = NT // 2
        U1 = NC * M1
        LN_FFN0, LN_LIN, LN_FFN1 = 1, 2, 3
        TP_LN = [0, 2, 3, 4]
        TP_ATTN = 1

        def n0(off):
            return slice(off, CH)

        def diag(c, jt):
            return max(0, P * (jt - TPC * c))

        block = ctx.enter_context(nc.Block())

        @block.sync
        def _(sp):
            sp.dma_start(x[:], A["x"].rearrange("(n p) d -> p n d", p=P)).then_inc(s_load, 16)
            sp.dma_start(ident[:], A["ident"]).then_inc(s_load, 16)
            sp.dma_start(wqkv[:], A["wqkvT"]).then_inc(s_load, 16)
            sp.dma_start(normw[:, 0, :], A["qnw"].partition_broadcast(P)).then_inc(s_load, 16)
            sp.dma_start(normw[:, 1, :], A["knw"].partition_broadcast(P)).then_inc(s_load, 16)
            sp.dma_start(rope[:], A["rope"].rearrange("(n p) a f -> p n a f", p=P)).then_inc(s_load, 16)
            sp.dma_start(masks[:], A["masks"].rearrange("a p q -> p a q")).then_inc(s_load, 16)
            sp.dma_start(wproj[:], A["wprojT"]).then_inc(s_load, 16)
            sp.dma_start(dft[:], A["dft"].rearrange("a p q -> p a q")).then_inc(s_load, 16)
            sp.dma_start(wfreq[:, 0, :], A["wre"]).then_inc(s_load, 16)
            sp.dma_start(wfreq[:, 1, :], A["wim"]).then_inc(s_load, 16)
            sp.dma_start(bias0[:], A["bias0"].partition_broadcast(P)).then_inc(s_load, 16)
            sp.wait_ge(s_res, 2 * NC)
            for i, name in enumerate(["lWq", "lWk", "lWv", "lWo"]):
                sp.dma_start(wlin[:, i, :], A[name]).then_inc(s_load1, 16)
            for i, name in enumerate(["lbk", "lbv", "lbo"]):
                sp.dma_start(blin[:, i, :], A[name].partition_broadcast(P)).then_inc(s_load1, 16)
            sp.dma_start(bqcol[:], A["lbq"].rearrange("(p a) -> p a", a=1)).then_inc(s_load1, 16)
            sp.dma_start(stdp[:, 0, :], A["stdp"].partition_broadcast(P)).then_inc(s_load1, 16)
            sp.dma_start(blockm[:], A["blockm"]).then_inc(s_load1, 16)
            sp.dma_start(wgate[:, 0, :], A["Ws"]).then_inc(s_load1, 16)
            sp.dma_start(wgate[:, 1, :], A["Wd"]).then_inc(s_load1, 16)
            for i in range(3):
                r = min(P, E1 * D1 - P * i)
                sp.dma_start(wout[0:r, i, :], A["Wo"][P * i:P * i + r, :]).then_inc(s_load1, 16)
            sp.dma_start(fold[:], A["fold"]).then_inc(s_load1, 16)
            sp.wait_ge(s_res, 3 * NC)
            for h in range(H1):
                if h:
                    sp.wait_ge(s_wh, h)
                c0 = h * E1 * D1
                sp.dma_start(wraw[:, 0, :], A["Wq"][:, c0:c0 + E1 * D1]).then_inc(s_w, 16)
                for i in range(2):
                    c1 = i * H1 * E1 * D1 + c0
                    sp.dma_start(wraw[:, 1 + i, :], A["Wkv"][:, c1:c1 + E1 * D1]).then_inc(s_w, 16)
            out_v = A["out"].rearrange("(n p) d -> p n d", p=P)
            for c in range(NC):
                sp.wait_ge(s_res, 3 * NC + c + 1)
                sp.dma_start(out_v[:, TPC * c:TPC * (c + 1), :], x[:, TPC * c:TPC * (c + 1), :]).then_inc(s_out, 16)
            sp.wait_ge(s_out, 16 * NC)

        @block.tensor
        def _(pe):
            def transpose_tiles(src, k, ready, count):
                for c in range(NC):
                    pe.wait_ge(ready, count(c))
                    for i in range(TPC):
                        n = TPC * c + i
                        mm = pe.transpose(ps[:, c, P * i:P * (i + 1)], src[:, n, :], ident[:])
                    mm.then_inc(s_tp, 1)

            pe.wait_ge(s_load, 16 * 12)
            transpose_tiles(xn, 0, s_xn, lambda c: c + 1)
            for n in range(NT):
                pe.wait_ge(s_xnT, n // TPC + 1)
                if n >= 4:
                    pe.wait_ge(s_qkvev, n - 3)
                pe.matmul(ps[:, 4 + n % 4, 0:3 * D], xnT[:, P * n:P * (n + 1)], wqkv[:],
                          start=True, stop=True).then_inc(s_qkv, 1)
            pe.wait_ge(s_qkvev, NT)

            pe.wait_ge(s_const, 1)
            pe.matmul(ps[:, 0, 0:P], wfreq[:, 0, :], dft[:, 0, :], start=True, stop=False)
            pe.matmul(ps[:, 0, 0:P], wfreq[:, 1, :], dft[:, 1, :], start=False, stop=True)
            pe.matmul(ps[:, 1, 0:P], wfreq[:, 1, :], dft[:, 0, :], start=True, stop=False)
            pe.matmul(ps[:, 1, 0:P], wfreq[:, 0, :], ndft[:], start=False, stop=True).then_inc(s_mixw, 1)
            pe.wait_ge(s_mixc, 1)
            pe.matmul(ps[:, 2, 0:P], ab[:, 0, :], dft[:, 0, :], start=True, stop=False)
            pe.matmul(ps[:, 2, 0:P], ab[:, 1, :], ndft[:], start=False, stop=True).then_inc(s_mixw, 1)
            pe.wait_ge(s_mixc, 2)

            for g in range(NG):
                pe.wait_ge(s_stage, 2 * g + 1)
                if g:
                    pe.wait_ge(s_attn, NC * g)
                for w, stage in enumerate((stagek, stageq)):
                    for c in range(NC):
                        for i in range(TPC):
                            mm = pe.transpose(ps[:, 4 * w + c, P * i:P * (i + 1)],
                                              stage[:, TPC * c + i, :, :].rearrange("p h r -> p (h r)"), ident[:])
                        mm.then_inc(s_gt, 1)
                pe.wait_ge(s_gev, 12 * g + 8)
                for h in range(GH):
                    rows = slice(32 * h, 32 * h + 32)
                    for it in range(NT):
                        m = (g * GH + h) * NT + it
                        b0 = 4 * (m % 2)
                        if m >= 2:
                            pe.wait_ge(s_mx, m - 1)
                        nk = P * (it + 1)
                        for b in range((nk + CH - 1) // CH):
                            w = min(CH, nk - CH * b)
                            last = nk - CH * b <= CH
                            mm = pe.matmul(ps[:, b0 + b, 0:w], qT[rows, g % 2, P * it:P * (it + 1)],
                                           kT[rows, g % 2, CH * b:CH * b + w], start=True, stop=not last,
                                           tile_position=(32 * h, 0))
                            if last:
                                mm = pe.matmul(ps[:, b0 + b, w - P:w], identb[:], masksb[:, 0, :],
                                               start=False, stop=True)
                        mm.then_inc(s_mxmm, 1)
                pe.wait_ge(s_stage, 2 * g + 2)
                for c in range(NC):
                    for i in range(TPC):
                        mm = pe.transpose(ps[:, 4 + c, P * i:P * (i + 1)],
                                          stageq[:, TPC * c + i, :, :].rearrange("p h r -> p (h r)"), ident[:])
                    mm.then_inc(s_gt, 1)
                pe.wait_ge(s_gev, 12 * g + 12)
                pe.wait_ge(s_kM, GH * (g + 1))
                pe.wait_ge(s_stagev, g + 1)

                def scores(u):
                    c, jt = STEPS0[u // 2]
                    off = diag(c, jt)
                    ug = 2 * N0 * g + u
                    if ug >= NS:
                        pe.wait_ge(s_exp, ug - NS + 1)
                    for i in range(2):
                        h = 2 * (u % 2) + i
                        b = 2 * (ug % NS) + i
                        mm = pe.matmul(ps[:, b, off:CH], kM[:, h, P * jt:P * (jt + 1)],
                                       qT[:, g % 2, CH * c + off:CH * (c + 1)], start=True, stop=jt < TPC * c)
                        if jt >= TPC * c:
                            mm = pe.matmul(ps[:, b, off:off + P], identb[:], masksb[:, 1, :], start=False, stop=True)
                    mm.then_inc(s_sc, 1)

                def values(k):
                    c, jt = STEPS0[k]
                    off = diag(c, jt)
                    kg = N0 * g + k
                    pe.wait_ge(s_exp, 2 * kg + 2)
                    if jt == 0 and g * NC + c:
                        pe.wait_ge(s_oT, g * NC + c)
                    for h in range(GH):
                        u = 2 * kg + h // 2
                        mm = pe.matmul(ps[32 * h:32 * h + 32, ACC, off:CH], stagev[:, g % 2, jt, h, :],
                                       pbuf[:, u % NP, h % 2, off:CH], start=jt == 0, stop=jt == TPC * (c + 1) - 1,
                                       tile_position=(0, 32 * h))
                    mm.then_inc(s_av, 1)

                def token_major(c):
                    m = g * NC + c
                    pe.wait_ge(s_oT, m + 1)
                    if m:
                        pe.wait_ge(s_attn, m)
                    for i in range(TPC):
                        mm = pe.transpose(ps[:, AUX, P * i:P * (i + 1)], oT[:, m % 2, P * i:P * (i + 1)], ident[:])
                    mm.then_inc(s_ot, 1)

                for k in range(N0 + 1):
                    if k < N0:
                        scores(2 * k)
                        scores(2 * k + 1)
                    if k:
                        values(k - 1)
                    if k - 3 in LAST0:
                        token_major(LAST0.index(k - 3))
                token_major(NC - 1)

            transpose_tiles(xn, TP_ATTN, s_attn, lambda c: NC * NG)
            for c in range(NC):
                pe.wait_ge(s_xnT, NC * TP_ATTN + c + 1)
                for i in range(TPC):
                    n = TPC * c + i
                    mm = pe.matmul(ps[:, 4 + c, P * i:P * (i + 1)], xnT[:, P * n:P * (n + 1)], wproj[:],
                                   start=True, stop=True)
                mm.then_inc(s_pj, 1)
            transpose_tiles(xn, TP_LN[LN_FFN0], s_xn, lambda c: NC * LN_FFN0 + c + 1)
            for c in range(NC):
                pe.wait_ge(s_xnT, NC * TP_LN[LN_FFN0] + c + 1)
                for i in range(TPC):
                    n = TPC * c + i
                    mm = pe.matmul(ps[:, 4 + c, P * i:P * (i + 1)], xnT[:, P * n:P * (n + 1)], mix[:],
                                   start=True, stop=True)
                mm.then_inc(s_pj, 1)

            pe.wait_ge(s_load1, 16 * 16)
            transpose_tiles(y_n, TP_LN[LN_LIN], s_xn, lambda c: NC * LN_LIN + c + 1)
            for c in range(NC):
                pe.wait_ge(s_xnT, NC * TP_LN[LN_LIN] + c + 1)
                pe.matmul(ps[:, 4 + c, :], wlin[:, 0, :], y_nT[:, CH * c:CH * (c + 1)],
                          start=True, stop=True).then_inc(s_lin, 1)
            for m in range(NT // 2):
                b = m % 4
                if m >= 4:
                    pe.wait_ge(s_lq, NC + m - 3)
                for i in range(2):
                    n = 2 * m + i
                    mm = pe.matmul(ps[:, b, 2 * D * i:2 * D * (i + 1)], y_nT[:, P * n:P * (n + 1)],
                                   wlin[:, 1:3, :].rearrange("p a d -> p (a d)"), start=True, stop=True)
                mm.then_inc(s_lin, 1)
            pe.wait_ge(s_lind, NC + NT // 2)
            for n in range(NT):
                mm = pe.matmul(ps[:, 4, 0:D + 2], kf[:, n, :], vf[:, n, :], start=n == 0, stop=n == NT - 1)
            mm.then_inc(s_lin, 1)
            pe.wait_ge(s_lind, NC + NT // 2 + 1)
            for c in range(NC):
                b = 2 * (c % 2)
                if c >= 2:
                    pe.wait_ge(s_lind, NC + NT // 2 + c)
                pe.matmul(ps[:, b, :], bd[:, 0, :], qfT[:, CH * c:CH * (c + 1)], start=True, stop=True)
                pe.matmul(ps[:, b + 1, :], bd[:, 1, :], qfT[:, CH * c:CH * (c + 1)],
                          start=True, stop=True).then_inc(s_lin, 1)
            for c in range(NC):
                pe.wait_ge(s_lind, NC + NT // 2 + 2 + c)
                for i in range(TPC):
                    n = TPC * c + i
                    mm = pe.matmul(ps[:, 4 + c, P * i:P * (i + 1)], aT[:, P * n:P * (n + 1)], wlin[:, 3, :],
                                   start=True, stop=True)
                mm.then_inc(s_pj, 1)

            transpose_tiles(y_n, TP_LN[LN_FFN1], s_xn, lambda c: NC * LN_FFN1 + c + 1)
            for n in range(NT):
                pe.wait_ge(s_xnT, NC * TP_LN[LN_FFN1] + n // TPC + 1)
                b, i = 4 + n // 6, n % 6
                mm = pe.matmul(ps[:, b, 80 * i:80 * (i + 1)], y_nT[:, P * n:P * (n + 1)],
                               wgate[:, :, :].rearrange("p a f -> p (a f)"), start=True, stop=True)
                if i == 5 or n == NT - 1:
                    mm.then_inc(s_g1, 1)
            pe.wait_ge(s_g2, 3)
            for h in range(H1):
                pe.wait_ge(s_wh, h + 1)
                for n in range(NT):
                    m = NT * h + n
                    if m >= 2:
                        pe.wait_ge(s_gated, m - 1)
                    if n < 2 and h:
                        pe.wait_ge(s_exp1, U1 * h)
                    for j in range(3):
                        o = ps[:, 3 * (m % 2) + j, 0:E1 * D1]
                        t = slice(P * n, P * (n + 1))
                        pe.matmul(o, xh[:, t], wh[:, j, :], start=True, stop=False)
                        pe.matmul(o, xh[:, t], wl[:, j, :], start=False, stop=False)
                        mm = pe.matmul(o, xl[:, t], wh[:, j, :], start=False, stop=True)
                    mm.then_inc(s_proj, 1)
                pe.wait_ge(s_gated, NT * (h + 1))
                pe.wait_ge(s_st1, 2 * h + 1)
                if h:
                    pe.wait_ge(s_on1, NC * h)

                def tr1(src, b0, k):
                    for c in range(NC):
                        if k >= 8:
                            pe.wait_ge(s_t1ev, 16 * h + k - 8 + c + 1)
                        for i in range(TPC):
                            mm = pe.transpose(ps[:, b0 + c, P * i:P * (i + 1)], src[:, TPC * c + i, :], ident[:])
                        mm.then_inc(s_t1, 1)

                tr1(sk1, 0, 0)
                tr1(sq1, 4, 4)
                tr1(sk2, 0, 8)
                pe.wait_ge(s_t1ev, 16 * h + 12)
                for it in range(NT):
                    m = NT * h + it
                    if m >= 2:
                        pe.wait_ge(s_mx1, m - 1)
                    for b in range(NC):
                        mm = pe.matmul(ps[:, 4 * (m % 2) + b, :], q1T[:, P * it:P * (it + 1)],
                                       k1T[:, CH * b:CH * (b + 1)], start=True, stop=True)
                    mm.then_inc(s_mm1, 1)
                pe.wait_ge(s_st1, 2 * h + 2)
                tr1(sq2, 4, 0)
                pe.wait_ge(s_t1ev, 16 * h + 16)

                def scores1(u):
                    c, m = u // M1, u % M1
                    ug = U1 * h + u
                    if ug >= NS:
                        pe.wait_ge(s_exp1, ug - NS + 1)
                    for i in range(2):
                        b = 2 * (ug % NS) + i
                        t = slice(P * (2 * m + i), P * (2 * m + i + 1))
                        q = slice(CH * c, CH * (c + 1))
                        pe.matmul(ps[:, b, :], k1T[:, t], q1T[:, q], start=True, stop=False)
                        mm = pe.matmul(ps[:, b, :], k2T[:, t], q2T[:, q], start=False, stop=True)
                    mm.then_inc(s_sc1, 1)

                def values1(u):
                    c, m = u // M1, u % M1
                    ug = U1 * h + u
                    pe.wait_ge(s_exp1, ug + 1)
                    if m == 0 and h * NC + c:
                        pe.wait_ge(s_oT1, h * NC + c)
                    for i in range(2):
                        mm = pe.matmul(ps[64 * i:64 * i + 64, ACC, :], h_qkv[:, 2, 2 * m + i, :],
                                       pbuf[:, ug % NP, i, :], start=m == 0, stop=m == M1 - 1,
                                       tile_position=(0, 64 * i))
                    mm.then_inc(s_av1, 1)

                def finish1(c):
                    m = h * NC + c
                    pe.wait_ge(s_oT1, m + 1)
                    pe.wait_ge(s_den1, U1 * h + M1 * (c + 1))
                    if m:
                        pe.wait_ge(s_on1, m)
                    for i in range(TPC):
                        t = slice(P * i, P * (i + 1))
                        pe.matmul(ps[:, AUX, D1 * i:D1 * (i + 1)], oT[:, m % 2, t], fold[:],
                                  start=i == 0, stop=True, skip_group_check=True)
                    for i in range(TPC):
                        t = slice(P * i, P * (i + 1))
                        o = ps[:, AUX, TPC * D1 + i:TPC * D1 + i + 1]
                        pe.matmul(o, den[:, m % 2, 0, t], ones[:], start=False, stop=False, skip_group_check=True)
                        mm = pe.matmul(o, den[:, m % 2, 1, t], ones[:], start=False, stop=True, skip_group_check=True)
                    mm.then_inc(s_fin1, 1)

                for u in range(U1 + 2):
                    if u < U1:
                        scores1(u)
                    if u >= 2:
                        values1(u - 2)
                    if u >= M1 + 3 and (u - 3) % M1 == 0:
                        finish1((u - 3) // M1 - 1)
                finish1(NC - 1)

            pe.wait_ge(s_z, 2 * H1 * NC)
            for n in range(NT):
                b = n % 2
                if n >= 2:
                    pe.wait_ge(s_zT, n - 1)
                for i in range(3):
                    r = min(P, E1 * D1 - P * i)
                    mm = pe.transpose(ps[0:r, b, P * i:P * (i + 1)],
                                      z[:, n, :, :].rearrange("p e d -> p (e d)")[:, P * i:P * i + r], ident[:])
                mm.then_inc(s_zt, 1)
                pe.wait_ge(s_zT, n + 1)
                for i in range(3):
                    r = min(P, E1 * D1 - P * i)
                    mm = pe.matmul(ps[:, 2 + n // TPC, P * (n % TPC):P * (n % TPC + 1)], zT[0:r, i, :], wout[0:r, i, :],
                                   start=i == 0, stop=i == 2)
                if n % TPC == TPC - 1:
                    mm.then_inc(s_pj, 1)

        @block.scalar
        def _(act):
            def norm_std(k):
                act.wait_ge(s_mv, k + 1)
                nc.scalar.activation(std[:], meanvar[:, :, 1], ACT.Sqrt, bias=eps[:, 0:1]).then_inc(s_std, 1)

            def copy_chunks(dst, k):
                for c in range(NC):
                    act.wait_ge(s_tp, NC * k + c + 1)
                    nc.scalar.activation(dst[:, CH * c:CH * (c + 1)], ps[:, c, :], ACT.Copy).then_inc(s_xnT, 1)

            norm_std(0)
            copy_chunks(xnT, 0)
            for n in range(NT):
                act.wait_ge(s_qkv, n + 1)
                nc.scalar.activation(qkv[:, n, :], ps[:, 4 + n % 4, 0:3 * D], ACT.Copy).then_inc(s_qkvev, 1)
            act.wait_ge(s_ms, 1)
            nc.scalar.activation(ms[:], ms[:], ACT.Sqrt, bias=eps[:, 1:2], scale=1.0 / D0).then_inc(s_rms, 1)
            act.wait_ge(s_mixw, 1)
            nc.scalar.activation(ab[:], ps[:, 0:2, 0:P], ACT.Copy).then_inc(s_mixc, 1)
            act.wait_ge(s_mixw, 2)
            nc.scalar.activation(mix[:], ps[:, 2, 0:P], ACT.Copy, scale=1.0 / D).then_inc(s_mixc, 1)

            for g in range(NG):
                for w, dst in enumerate((kT, qT)):
                    for c in range(NC):
                        act.wait_ge(s_gt, 12 * g + 4 * w + c + 1)
                        nc.scalar.activation(dst[:, g % 2, CH * c:CH * (c + 1)], ps[:, 4 * w + c, :],
                                             ACT.Copy).then_inc(s_gev, 1)
                for c in range(NC):
                    act.wait_ge(s_gt, 12 * g + 8 + c + 1)
                    nc.scalar.activation(qT[:, g % 2, CH * c:CH * (c + 1)], ps[:, 4 + c, :],
                                         ACT.Copy).then_inc(s_gev, 1)
                for u in range(2 * N0):
                    c, jt = STEPS0[u // 2]
                    off = diag(c, jt)
                    ug = 2 * N0 * g + u
                    act.wait_ge(s_sc, ug + 1)
                    if ug >= NP:
                        act.wait_ge(s_av, (ug - NP) // 2 + 1)
                    b = 2 * (ug % NS)
                    nc.scalar.activation(pbuf[:, ug % NP, :, off:CH], ps[:, b:b + 2, off:CH], ACT.Exp,
                                         scale=float(D0) ** -0.5).then_inc(s_exp, 1)
            copy_chunks(xnT, TP_ATTN)
            norm_std(LN_FFN0)
            copy_chunks(xnT, TP_LN[LN_FFN0])
            norm_std(LN_LIN)
            copy_chunks(y_nT, TP_LN[LN_LIN])
            act.wait_ge(s_load1, 16 * 16)
            nc.scalar.activation(stdp[:, 1, :], stdp[:, 0, :], ACT.Exp, scale=-1.0).then_inc(s_lina, 1)
            for m in range(NC + NT // 2):
                act.wait_ge(s_lq, m + 1)
                w = CH if m < NC else 2 * D
                nc.scalar.activation(lt[:, m % 2, 0, 0:w], lt[:, m % 2, 0, 0:w], ACT.Exp).then_inc(s_lina, 1)
            norm_std(LN_FFN1)
            copy_chunks(y_nT, TP_LN[LN_FFN1])
            for b in range(3):
                act.wait_ge(s_g1, b + 1)
                w = min(6, NT - 6 * b)
                nc.scalar.activation(sig[:, 6 * b:6 * b + w, :, :, :].rearrange("p n a h e -> p (n a h e)"),
                                     ps[:, 4 + b, 0:80 * w], ACT.Exp, scale=-1.0).then_inc(s_g2, 1)
            for h in range(H1):
                for k, (dst, b0) in enumerate(((k1T, 0), (q1T, 4), (k2T, 0), (q2T, 4))):
                    for c in range(NC):
                        act.wait_ge(s_t1, 16 * h + 4 * k + c + 1)
                        nc.scalar.activation(dst[:, CH * c:CH * (c + 1)], ps[:, b0 + c, :],
                                             ACT.Copy).then_inc(s_t1ev, 1)
                for u in range(U1):
                    ug = U1 * h + u
                    act.wait_ge(s_sc1, ug + 1)
                    if ug >= NP:
                        act.wait_ge(s_av1, ug - NP + 1)
                        act.wait_ge(s_den1, ug - NP + 1)
                    b = 2 * (ug % NS)
                    nc.scalar.activation(pbuf[:, ug % NP, :, :], ps[:, b:b + 2, :], ACT.Exp,
                                         scale=float(D1) ** -0.5).then_inc(s_exp1, 1)
            for n in range(NT):
                act.wait_ge(s_zt, n + 1)
                nc.scalar.activation(zT[:, 0:2, :].rearrange("p a t -> p (a t)"), ps[:, n % 2, 0:2 * P], ACT.Copy)
                nc.scalar.activation(zT[0:64, 2, :], ps[0:64, n % 2, 2 * P:3 * P], ACT.Copy).then_inc(s_zT, 1)

        @block.vector
        def _(dve):
            v = nc.vector
            order = [0]

            def link(ins):
                order[0] += 1
                ins.then_inc(s_dve, 1)
                dve.wait_ge(s_dve, order[0])

            def norm(k, dst):
                for n in range(NT):
                    ins = v.bn_stats(stats[:, n, :], x[:, n, :])
                link(ins)
                for n in range(NT):
                    ins = v.bn_aggr(meanvar[:, n, :], stats[:, n, :])
                ins.then_inc(s_mv, 1)
                dve.wait_ge(s_std, k + 1)
                link(v.reciprocal(rstd[:], std[:]))
                for n in range(NT):
                    ins = v.tensor_scalar(dst[:, n, :], x[:, n, :], meanvar[:, n, 0:1], rstd[:, n:n + 1],
                                          ALU.subtract, ALU.mult)
                    if n % TPC == TPC - 1:
                        ins.then_inc(s_xn, 1)

            def residual(bank, k, bias=None):
                for c in range(NC):
                    dve.wait_ge(s_pj, NC * k + c + 1)
                    xc = x[:, TPC * c:TPC * (c + 1), :]
                    ins = v.tensor_tensor(xc, ps[:, bank + c, :].rearrange("p (n d) -> p n d", n=TPC), xc, ALU.add)
                    if bias is not None:
                        link(ins)
                        ins = v.tensor_tensor(xc, xc, bias.unsqueeze(1).to_broadcast([P, TPC, D]), ALU.add)
                    ins.then_inc(s_res, 1)
                dve.wait_ge(s_res, NC * (k + 1))

            v.memset(eps[:, 0:1], LN_EPS)
            v.memset(eps[:, 1:2], RMS_EPS)
            dve.wait_ge(s_load, 16 * 12)
            norm(0, xn)
            v.tensor_copy(identb[:], ident[:])
            v.tensor_copy(masksb[:], masks[:])
            v.tensor_scalar(ndft[:], dft[:, 1, :], -1.0, None, ALU.mult).then_inc(s_const, 1)

            dve.wait_ge(s_qkvev, NT)
            qk = qkv[:, :, 0:2 * D]
            qkh = qk.rearrange("p n (h d) -> p n h d", d=D0)
            link(v.tensor_tensor(tmp[:].rearrange("p n h d -> p n (h d)"), qk, qk, ALU.mult))
            v.tensor_reduce(ms[:], tmp[:], AX.X, ALU.add).then_inc(s_ms, 1)
            dve.wait_ge(s_rms, 1)
            link(v.reciprocal(ms[:], ms[:]))
            link(v.tensor_tensor(qkh, qkh, ms[:].unsqueeze(3).to_broadcast([P, NT, 2 * H0, D0]), ALU.mult))
            for i in range(2):
                q = qkh[:, :, H0 * i:H0 * (i + 1), :]
                w = normw[:, i, :].unsqueeze(1).unsqueeze(1).to_broadcast([P, NT, H0, D0])
                link(v.tensor_tensor(q, q, w, ALU.mult))
            half = D0 // 2
            qa, qb = qkh[:, :, :, 0:half], qkh[:, :, :, half:D0]
            ta, tb = tmp[:, :, :, 0:half], tmp[:, :, :, half:D0]
            cos, sin = (rope[:, :, i, :].unsqueeze(2).to_broadcast([P, NT, 2 * H0, half]) for i in range(2))
            v.tensor_tensor(ta, qa, sin, ALU.mult)
            link(v.tensor_tensor(tb, qb, sin, ALU.mult))
            v.tensor_tensor(qa, qa, cos, ALU.mult)
            link(v.tensor_tensor(qb, qb, cos, ALU.mult))
            v.tensor_tensor(qa, qa, tb, ALU.subtract)
            link(v.tensor_tensor(qb, qb, ta, ALU.add))
            dve.wait_ge(s_pconst, 1)

            for g in range(NG):
                if g:
                    dve.wait_ge(s_gt, 12 * g)
                gq = qkv[:, :, 32 * g:32 * (g + 1)].rearrange("p n (h d) -> p n h d", d=D0)
                gk = qkv[:, :, D + 32 * g:D + 32 * (g + 1)].rearrange("p n (h d) -> p n h d", d=D0)
                for o in (0, 2 * D0):
                    v.tensor_copy(stageq[:, :, :, o:o + D0].bitcast(F32R), gq)
                for o in (0, D0):
                    v.tensor_copy(stagek[:, :, :, o:o + D0].bitcast(F32R), gk)
                link(v.memset(stageq[:, :, :, 24:25], 0.0))
                v.tensor_tensor(stageq[:, :, :, D0:2 * D0], gq, stageq[:, :, :, 0:D0], ALU.subtract)
                v.tensor_tensor(stagek[:, :, :, 2 * D0:3 * D0], gk, stagek[:, :, :, 0:D0],
                                ALU.subtract).then_inc(s_stage, 1)
                for h in range(GH):
                    for it in range(NT):
                        m = (g * GH + h) * NT + it
                        dve.wait_ge(s_mxmm, m + 1)
                        b0 = 4 * (m % 2)
                        v.tensor_reduce(mx[:, it, h:h + 1],
                                        ps[:, b0:b0 + 4, :].rearrange("p b c -> p (b c)")[:, 0:P * (it + 1)],
                                        AX.X, ALU.max).then_inc(s_mx, 1)
                dve.wait_ge(s_mx, GH * NT * (g + 1))
                v.tensor_scalar(stageq[:, :, :, 24:25].bitcast(F32R), mx[:].unsqueeze(3), -1.0, None,
                                ALU.mult).then_inc(s_stage, 1)
                for c in range(NC):
                    m = g * NC + c
                    dve.wait_ge(s_av, N0 * g + LAST0[c])
                    if m >= 2:
                        dve.wait_ge(s_ot, m - 1)
                    v.tensor_copy(oT[:, m % 2, :], ps[:, ACC, :]).then_inc(s_oT, 1)
                    dve.wait_ge(s_ot, m + 1)
                    o = ps[:, AUX, :].rearrange("p (n h r) -> p n h r", n=TPC, h=GH)
                    link(v.reciprocal(rden[:].unsqueeze(3), o[:, :, :, D0:D0 + 1]))
                    dst = xn[:, TPC * c:TPC * (c + 1), 32 * g:32 * (g + 1)].rearrange("p n (h d) -> p n h d", d=D0)
                    v.tensor_tensor(dst, o[:, :, :, 0:D0], rden[:].unsqueeze(3).to_broadcast([P, TPC, GH, D0]),
                                    ALU.mult).then_inc(s_attn, 1)
            residual(4, 0)
            norm(LN_FFN0, xn)
            residual(4, 1, bias0[:])

            norm(LN_LIN, y_n)
            v.memset(vf[:, :, D:D + 1], 1.0)
            v.memset(vf[:, :, D + 1:D + 2], 0.0)
            v.memset(ones[:], 1.0)
            dve.wait_ge(s_lina, 1)
            link(v.tensor_scalar(stdp[:, 1, :], stdp[:, 1, :], 1.0, None, ALU.add))
            link(v.reciprocal(stdp[:, 2, :], stdp[:, 1, :]))
            link(v.tensor_tensor(bd[:, 2, :].rearrange("p (h d) -> p h d", d=D0),
                                 blockm[:].rearrange("p (h d) -> p h d", d=D0),
                                 stdp[:, 2, :].unsqueeze(2).to_broadcast([P, H0, D0]), ALU.mult))

            def split_sign(m):
                dve.wait_ge(s_lin, m + 1)
                if m >= 2:
                    dve.wait_ge(s_lind, m - 1)
                if m < NC:
                    z0, z1 = lt[:, m % 2, 0, :], lt[:, m % 2, 1, :]
                    v.tensor_scalar(z0, ps[:, 4 + m, :], bqcol[:, 0:1], 0.0, ALU.add, ALU.min)
                    v.tensor_scalar(z1, ps[:, 4 + m, :], bqcol[:, 0:1], 0.0, ALU.add, ALU.max).then_inc(s_lq, 1)
                    return
                j = m - NC
                kv = ps[:, j % 4, :].rearrange("p (n a d) -> p n a d", n=2, a=2)
                z0, z1 = (lt[:, m % 2, i, 0:2 * D].rearrange("p (n d) -> p n d", n=2) for i in range(2))
                bk, bv = (blin[:, i, :].unsqueeze(1).to_broadcast([P, 2, D]) for i in range(2))
                link(v.tensor_tensor(z1, kv[:, :, 0, :], bk, ALU.add))
                v.tensor_tensor(vf[:, 2 * j:2 * j + 2, 0:D], kv[:, :, 1, :], bv, ALU.add)
                link(v.tensor_scalar(z0, z1, 0.0, None, ALU.min))
                v.tensor_scalar(z1, z1, 0.0, None, ALU.max).then_inc(s_lq, 1)

            def elu1(m):
                dve.wait_ge(s_lina, m + 2)
                dve.wait_ge(s_lq, m + 1)
                if m < NC:
                    out, z0, z1 = qfT[:, CH * m:CH * (m + 1)], lt[:, m % 2, 0, :], lt[:, m % 2, 1, :]
                else:
                    out = kf[:, 2 * (m - NC):2 * (m - NC) + 2, :]
                    z0, z1 = (lt[:, m % 2, i, 0:2 * D].rearrange("p (n d) -> p n d", n=2) for i in range(2))
                v.tensor_tensor(out, z0, z1, ALU.add).then_inc(s_lind, 1)

            items = NC + NT // 2
            for m in range(items + 1):
                if m < items:
                    split_sign(m)
                if m:
                    elu1(m - 1)
            dve.wait_ge(s_lin, items + 1)
            v.tensor_tensor(bd[:, 0, :], ps[:, 4, 0:D], bd[:, 2, :], ALU.mult)
            v.tensor_scalar(bd[:, 1, :], blockm[:], ps[:, 4, D:D + 1], None, ALU.mult).then_inc(s_lind, 1)
            dve.wait_ge(s_lind, items + 1)
            for c in range(NC):
                dve.wait_ge(s_lin, items + 2 + c)
                b = 2 * (c % 2)
                z0, z1 = lt[:, c % 2, 0, :], lt[:, c % 2, 1, :]
                link(v.tensor_scalar(z0, ps[:, b + 1, :], 1e-6, None, ALU.add))
                link(v.reciprocal(z1, z0))
                v.tensor_tensor(aT[:, CH * c:CH * (c + 1)], ps[:, b, :], z1, ALU.mult).then_inc(s_lind, 1)
            residual(4, 2, blin[:, 2, :])

            norm(LN_FFN1, y_n)
            dve.wait_ge(s_xnT, NC * (TP_LN[LN_FFN1] + 1))
            link(v.tensor_copy(xh[:], y_nT[:]))
            link(v.tensor_tensor(xl[:], y_nT[:], xh[:].bitcast(F32), ALU.subtract))
            dve.wait_ge(s_g2, 3)
            link(v.tensor_scalar(sig[:], sig[:], 1.0, None, ALU.add))
            link(v.reciprocal(sig[:], sig[:]))
            sg = sig[:].rearrange("p n a h e -> p (n a h) e")
            rk = rank[:].rearrange("p n a h e -> p (n a h) e")
            link(v.memset(rank[:], 0.0))
            for r in range(1, E1):
                lo, hi = slice(0, E1 - r), slice(r, E1)
                v.tensor_tensor(beats[:, 0, :, 0:E1 - r], sg[:, :, hi], sg[:, :, lo], ALU.is_gt)
                link(v.tensor_tensor(beats[:, 1, :, 0:E1 - r], sg[:, :, lo], sg[:, :, hi], ALU.is_ge))
                link(v.tensor_tensor(rk[:, :, lo], rk[:, :, lo], beats[:, 0, :, 0:E1 - r], ALU.add))
                link(v.tensor_tensor(rk[:, :, hi], rk[:, :, hi], beats[:, 1, :, 0:E1 - r], ALU.add))
            link(v.tensor_scalar(rank[:], rank[:], TOP - 0.5, None, ALU.is_lt))
            for i, a in enumerate((1, 0, 0)):
                ins = v.tensor_tensor(gate[:, :, i, :, :], sig[:, :, a, :, :], rank[:, :, a, :, :], ALU.mult)
            link(ins)
            v.memset(sq2[:, :, D1:P], 0.0)
            v.memset(sk2[:, :, D1:D1 + 1], 1.0)
            link(v.memset(sk2[:, :, D1 + 1:P], 0.0))

            for h in range(H1):
                dve.wait_ge(s_w, 48 * (h + 1))
                if h:
                    dve.wait_ge(s_proj, NT * h)
                link(v.tensor_copy(wh[:], wraw[:]))
                v.tensor_tensor(wl[:], wraw[:], wh[:].bitcast(F32), ALU.subtract).then_inc(s_wh, 1)
                for n in range(NT):
                    m = NT * h + n
                    dve.wait_ge(s_proj, m + 1)
                    if m >= 2:
                        dve.wait_ge(s_gadd, m - 1)
                    b = 3 * (m % 2)
                    v.tensor_tensor(gt[:, m % 2], ps[:, b:b + 3, 0:E1 * D1].rearrange("p j (e d) -> p j e d", e=E1),
                                    gate[:, n, :, h, :].unsqueeze(3).to_broadcast([P, 3, E1, D1]),
                                    ALU.mult).then_inc(s_gated, 1)
                dve.wait_ge(s_gadd, NT * (h + 1))
                q, k = h_qkv[:, 0], h_qkv[:, 1]
                if h:
                    dve.wait_ge(s_t1, 16 * h)
                v.tensor_copy(sk1[:, :, 0:D1].bitcast(F32R), k)
                v.tensor_copy(sk1[:, :, D1:P].bitcast(F32R), k)
                v.tensor_copy(sq1[:, :, 0:D1].bitcast(F32R), q)
                link(v.tensor_copy(sq2[:, :, 0:D1].bitcast(F32R), q))
                v.tensor_tensor(sq1[:, :, D1:P], q, sq1[:, :, 0:D1], ALU.subtract)
                v.tensor_tensor(sk2[:, :, 0:D1], k, sk1[:, :, 0:D1], ALU.subtract).then_inc(s_st1, 1)
                for it in range(NT):
                    m = NT * h + it
                    dve.wait_ge(s_mm1, m + 1)
                    b = 4 * (m % 2)
                    v.tensor_reduce(mx1[:, it:it + 1], ps[:, b:b + 4, :].rearrange("p b c -> p (b c)"),
                                    AX.X, ALU.max).then_inc(s_mx1, 1)
                dve.wait_ge(s_mx1, NT * (h + 1))
                v.tensor_scalar(sq2[:, :, D1:D1 + 1].bitcast(F32R), mx1[:].unsqueeze(2), -1.0, None,
                                ALU.mult).then_inc(s_st1, 1)
                for u in range(U1):
                    c, m = u // M1, u % M1
                    ug, mc = U1 * h + u, NC * h + c
                    dve.wait_ge(s_exp1, ug + 1)
                    w, dn = pbuf[:, ug % NP, :, :], den[:, mc % 2, :, :]
                    if m == 0:
                        if mc >= 2:
                            dve.wait_ge(s_fin1, mc - 1)
                        v.tensor_copy(dn, w).then_inc(s_den1, 1)
                    else:
                        dve.wait_ge(s_den1, ug)
                        v.tensor_tensor(dn, dn, w, ALU.add).then_inc(s_den1, 1)
                    if m == M1 - 1:
                        dve.wait_ge(s_av1, ug + 1)
                        v.tensor_copy(oT[:, mc % 2, :], ps[:, ACC, :]).then_inc(s_oT1, 1)
                        dve.wait_ge(s_fin1, mc + 1)
                        if mc:
                            dve.wait_ge(s_z, 2 * mc - 1)
                        link(v.reciprocal(rd1[:], ps[:, AUX, TPC * D1:TPC * (D1 + 1)]))
                        v.tensor_tensor(on[:], ps[:, AUX, 0:TPC * D1].rearrange("p (n d) -> p n d", n=TPC),
                                        rd1[:].unsqueeze(2).to_broadcast([P, TPC, D1]), ALU.mult).then_inc(s_on1, 1)
            residual(2, 3)

        @block.gpsimd
        def _(pool):
            g_ = nc.gpsimd
            order = [0]

            def link(ins):
                order[0] += 1
                ins.then_inc(s_pool, 1)
                pool.wait_ge(s_pool, order[0])

            g_.memset(stageq[:, :, :, 24:32], 0.0)
            g_.memset(stagek[:, :, :, 24:25], 1.0)
            g_.memset(stagek[:, :, :, 25:32], 0.0)
            g_.memset(stagev[:, :, :, :, D0:D0 + 1].rearrange("p b n h r -> p (b n h) r"), 1.0)
            g_.memset(stagev[:, :, :, :, D0 + 1:32].rearrange("p b n h r -> p (b n h) r"), 0.0)
            g_.memset(kM[:].bitcast(F32), 0.0).then_inc(s_pconst, 1)
            pool.wait_ge(s_pconst, 1)
            pool.wait_ge(s_qkvev, NT)
            for g in range(NG):
                if g >= 2:
                    pool.wait_ge(s_av, N0 * (g - 1))
                gv = qkv[:, :, 2 * D + 32 * g:2 * D + 32 * (g + 1)].rearrange("p n (h d) -> p n h d", d=D0)
                g_.tensor_copy(stagev[:, g % 2, :, :, 0:D0], gv).then_inc(s_stagev, 1)
                pool.wait_ge(s_stagev, g + 1)
                pool.wait_ge(s_gev, 12 * g + 4)
                if g:
                    pool.wait_ge(s_sc, 2 * N0 * g)
                for h in range(GH):
                    rows = slice(32 * h, 32 * h + 32)
                    g_.tensor_copy(kM[rows, h, :], kT[rows, g % 2, :]).then_inc(s_kM, 1)
                    pool.wait_ge(s_kM, GH * g + h + 1)
            pool.wait_ge(s_g1, 3)
            link(g_.memset(z[:], 0.0))
            for h in range(H1):
                for n in range(NT):
                    m = NT * h + n
                    pool.wait_ge(s_gated, m + 1)
                    if h and n == 0:
                        pool.wait_ge(s_av1, U1 * h)
                    t = gt[:, m % 2]
                    link(g_.tensor_tensor(gs[:], t[:, :, 0:2, :], t[:, :, 2:4, :], ALU.add))
                    link(g_.tensor_tensor(gsum[:], gs[:, :, 0, :], gs[:, :, 1, :], ALU.add))
                    g_.tensor_tensor(h_qkv[:, :, n, :], gsum[:], t[:, :, 4, :], ALU.add).then_inc(s_gadd, 1)
                for c in range(NC):
                    mc = NC * h + c
                    pool.wait_ge(s_on1, mc + 1)
                    tiles = slice(TPC * c, TPC * (c + 1))
                    g_.tensor_tensor(onm[:], on[:].unsqueeze(2).to_broadcast([P, TPC, E1, D1]),
                                     rank[:, tiles, 1, h, :].unsqueeze(3).to_broadcast([P, TPC, E1, D1]),
                                     ALU.mult).then_inc(s_z, 1)
                    pool.wait_ge(s_z, 2 * mc + 1)
                    g_.tensor_tensor(z[:, tiles], z[:, tiles], onm[:], ALU.add).then_inc(s_z, 1)
                    pool.wait_ge(s_z, 2 * mc + 2)


_INPUTS = {
    "x": "L0_attn_x", "qnw": "L0_attn_q_norm_w", "knw": "L0_attn_k_norm_w", "wre": "L0_ffn_w_freq_real",
    "wim": "L0_ffn_w_freq_imag", "bias0": "L0_ffn_bias", "lbq": "L1_attn_bq", "lbk": "L1_attn_bk",
    "lbv": "L1_attn_bv", "lbo": "L1_attn_bo", "stdp": "L1_attn_stdp", "Ws": "L1_ffn_Ws", "Wd": "L1_ffn_Wd",
    "Wq": "L1_ffn_Wq", "Wkv": "L1_ffn_Wkv",
}
_TRANSPOSED = {"wqkvT": "L0_attn_w_qkv", "wprojT": "L0_attn_w_proj", "lWq": "L1_attn_Wq", "lWk": "L1_attn_Wk",
               "lWv": "L1_attn_Wv", "lWo": "L1_attn_Wo"}


def constants():
    f32 = np.float32
    freqs = (f32(32.0) ** (-np.arange(0, D0, 2, dtype=f32) / f32(D0))).astype(f32)
    ang = (np.arange(T, dtype=f32)[:, None] * freqs[None, :]).astype(f32).astype(np.float64)
    a = 2 * np.pi * (np.outer(np.arange(D), np.arange(D)) % D) / D
    i, j = np.arange(P)[:, None], np.arange(P)[None, :]
    return {
        "ident": np.eye(P, dtype=f32),
        "rope": np.stack([np.cos(ang), np.sin(ang)], 1).astype(f32),
        "masks": np.stack([np.where(j > i, NEG, 0.0), np.where(i > j, NEG, 0.0)]).astype(f32),
        "dft": np.stack([np.cos(a), np.sin(a)]).astype(f32),
        "blockm": (i // D0 == j // D0).astype(f32),
        "fold": np.concatenate([np.eye(D1), np.eye(D1)]).astype(f32),
    }


def kernel(**inputs):
    import concourse.bacc as _bacc
    from concourse.bass_utils import run_bass_kernel_spmd as _run

    arrays = {k: np.ascontiguousarray(inputs[v]) for k, v in _INPUTS.items()}
    arrays["x"] = arrays["x"].reshape(T, D)
    arrays |= {k: np.ascontiguousarray(np.asarray(inputs[v]).T) for k, v in _TRANSPOSED.items()}
    wo = np.asarray(inputs["L1_ffn_Wo"]).reshape(D1, E1, D).transpose(1, 0, 2)
    arrays["Wo"] = np.ascontiguousarray(wo).reshape(E1 * D1, D)
    arrays |= constants()
    nc = _bacc.Bacc("TRN2", target_bir_lowering=False, num_devices=1)
    aps = {k: nc.dram_tensor(f"in_{k}", a.shape, mybir.dt.from_np(a.dtype), kind="ExternalInput").ap()
           for k, a in arrays.items()}
    aps["out"] = nc.dram_tensor("out_0", (T, D), F32, kind="ExternalOutput").ap()
    build(nc, aps)
    r = _run(nc, [{f"in_{k}": a for k, a in arrays.items()}], core_ids=[0])
    return r.results[0]["out_0"].reshape(1, T, D)
```

```python
from contextlib import ExitStack

import numpy as np

import concourse.bass as bass
from concourse import mybir

F32 = mybir.dt.float32
F32R = mybir.dt.float32r
BF16 = mybir.dt.bfloat16
ALU = mybir.AluOpType
ACT = mybir.ActivationFunctionType
AX = mybir.AxisListType

P = 128
T = 2048
NT = T // P
D = 128
CH = 512
NC = T // CH
TPC = CH // P
H0, D0 = 16, 8
GH = 4
NG = H0 // GH
H1, E1, D1 = 8, 5, 64
TOP = 3
LN_EPS = 1e-5
RMS_EPS = 1e-6
NEG = -1e30
NP0, NP1 = 6, 5
NS = 2
ACC = 6
RING = (4, 5, 7)
LEAD0 = 42
LEAD1 = 23


def preparation0():
    out, late = [], None
    for g in range(NG):
        out += [(("stagek", g), 3), (("k", g, 0), 1), (("k", g, 1), 1)]
        if late:
            out.append((late, 1))
        out += [(("stageq", g), 3), (("q", g, 0), 1)]
        late = None
        for c in range(NC):
            if c + 1 < NC:
                out.append((("q", g, c + 1), 1))
            if c + 2 < NC:
                out.append((("k", g, c + 2), 1))
            items = []
            for i in range(TPC):
                for b in range(c + 1):
                    n = min(GH, TPC // (i + 1)) if b == c else 1
                    items += [(("max", g, c, i, b, h, n), 1) for h in range(0, GH, n)]
            if late:
                items.insert(5, (late, 1))
            out += items + [(("m", g, c), 0.5)]
            late = ("q2", g, c)
    return out + [(late, 1)]


def preparation1():
    out, late = [(("w", 0), 1)], None
    for h in range(H1):
        staged = 0
        for n in range(NT + 2):
            if n < NT:
                out += [(("proj", h, n, j), 0.8) for j in range(3)]
            if late and n == 1:
                out.append((late, 0.6))
            while staged < NC and (TPC * staged + TPC + 1 <= n or n == NT + 1):
                out += [(("stage", h, staged), 1.5)] + [(("t", h, staged, w), 0.6) for w in range(3)]
                staged += 1
        late = None
        for c in range(NC):
            items = [(("max", h, TPC * c + i, b), 1) for i in range(TPC) for b in range(NC)]
            if late:
                items.insert(5, (late, 0.6))
            out += items + [(("m", h, c), 0.8)]
            late = ("q2", h, c)
            if c == 1 and h + 1 < H1:
                out.append((("w", h + 1), 2))
    return out + [(late, 0.6)]


def merge(preparation, lead, per, units, foreground, tail):
    total, done, i, seq = sum(c for _, c in preparation), 0.0, 0, []
    rate = total / units
    for u in range(units + tail):
        while i < len(preparation) and done < (u + lead) * rate:
            seq.append(preparation[i][0])
            done += preparation[i][1]
            i += 1
        seq += foreground(u)
    assert i == len(preparation)
    return seq


class Ring:

    def __init__(self, seq, by_dve, by_act):
        self.turn, self.read, self.by_act, self.order = {}, {}, by_act, []
        counts = {True: 0, False: 0}
        for step in seq:
            if step[0] in by_dve + by_act:
                a = step[0] in by_act
                counts[a] += 1
                self.turn[step], self.read[step] = len(self.order), counts[a]
                self.order.append(step)

    def bank(self, step):
        return RING[self.turn[step] % len(RING)]


def build(nc, A):
    ctx = ExitStack()
    with ctx:
        def sem(name):
            return ctx.enter_context(nc.semaphore(name))

        def sbuf(stack, name, shape, dt=F32):
            return stack.enter_context(nc.sbuf_tensor(name, shape, dt))

        ps = ctx.enter_context(nc.psum_tensor("ps", [P, 8, CH], F32))

        x = sbuf(ctx, "x", [P, NT, D])
        ident = sbuf(ctx, "ident", [P, P])
        eps = sbuf(ctx, "eps", [P, 2])
        stats = sbuf(ctx, "stats", [P, NT, 6])
        meanvar = sbuf(ctx, "meanvar", [P, NT, 2])
        std = sbuf(ctx, "std", [P, NT])
        rstd = sbuf(ctx, "rstd", [P, NT])
        oT = sbuf(ctx, "oT", [P, 2, CH])

        l0 = ExitStack()
        s0 = lambda name, shape, dt=F32: sbuf(l0, name, shape, dt)
        identb = s0("identb", [P, P], BF16)
        masksb = s0("masksb", [P, 2, P], BF16)
        wqkv = s0("wqkv", [P, 3 * D])
        wproj = s0("wproj", [P, D])
        normw = s0("normw", [P, 2, D0])
        rope = s0("rope", [P, NT, 2, D0 // 2])
        mix = s0("mix", [P, P])
        bias0 = s0("bias0", [P, D])
        xn = s0("xn", [P, NT, D])
        xnT = s0("xnT", [P, T])
        qkv = s0("qkv", [P, NT, 3 * D])
        ms = s0("ms", [P, NT, 2 * H0])
        stageq = s0("stageq", [P, NT, GH, 32])
        stagek = s0("stagek", [P, NT, GH, 32])
        stagev = s0("stagev", [P, 2, NT, GH, 32])
        qT = s0("qT", [P, 2, T], F32R)
        kT = s0("kT", [P, T], F32R)
        mxp = s0("mxp", [P, TPC, GH, NC])
        mx = s0("mx", [P, TPC, GH])
        rden = s0("rden", [P, TPC, GH])
        rotating = ExitStack()
        sp_ = lambda name, shape, dt=F32: sbuf(rotating, name, shape, dt)
        tmp = sp_("tmp", [P, NT, 2 * H0, D0])
        masks = sp_("masks", [P, 2, P])
        dft = sp_("dft", [P, 2, P])
        ndft = sp_("ndft", [P, P])
        wfreq = sp_("wfreq", [P, 2, P])
        ab = sp_("ab", [P, 2, P])
        rotating.close()
        pbuf0 = s0("pbuf0", [P, NP0, 2, CH])
        kM = s0("kM", [P, 2, GH, T], F32R)
        l0.close()

        l1 = ExitStack()
        s1 = lambda name, shape, dt=F32: sbuf(l1, name, shape, dt)
        fold = s1("fold", [P, D1])
        ones = s1("ones", [P, 1])
        wgate = s1("wgate", [P, 2, H1 * E1])
        wout = s1("wout", [P, 3, D])
        lin = ExitStack()
        sl = lambda name, shape, dt=F32: sbuf(lin, name, shape, dt)
        wlin = sl("wlin", [P, 4, D])
        blin = sl("blin", [P, 3, D])
        bqcol = sl("bqcol", [P, 1])
        stdp = sl("stdp", [P, 3, H0])
        blockm = sl("blockm", [P, D])
        bd = sl("bd", [P, 3, D])
        qfT = sl("qfT", [P, T])
        lt = sl("lt", [P, 2, 2, CH])
        kf = sl("kf", [P, NT, D])
        vf = sl("vf", [P, NT, D + 2])
        aT = sl("aT", [P, T])
        lin.close()
        z = s1("z", [P, NT, E1, D1])
        xh = s1("xh", [P, T], F32R)
        xl = s1("xl", [P, T], F32R)
        gate = s1("gate", [P, NT, 2, H1, E1])
        maskd = s1("maskd", [P, NT, H1, E1])
        wraw = s1("wraw", [P, 3, E1 * D1])
        wh = s1("wh", [P, 3, E1 * D1], F32R)
        wl = s1("wl", [P, 3, E1 * D1], F32R)
        ranking = ExitStack()
        sr = lambda name, shape, dt=F32: sbuf(ranking, name, shape, dt)
        y_n = sr("y_n", [P, NT, D])
        y_nT = sr("y_nT", [P, T])
        beats = sr("beats", [P, 2, 2 * NT * H1, E1 - 1])
        sig = sr("sig", [P, NT, 2, H1, E1])
        rank = sr("rank", [P, NT, 2, H1, E1])
        ranking.close()
        final = ExitStack()
        zT = sbuf(final, "zT", [P, 3, P])
        final.close()
        gt = s1("gt", [P, 2, 3, E1, D1])
        gs = s1("gs", [P, 3, 2, D1])
        gsum = s1("gsum", [P, 3, D1])
        h_qk = s1("h_qk", [P, 2, NT, D1])
        h_v = s1("h_v", [P, 2, NT, D1])
        pbuf1 = s1("pbuf1", [P, NP1, 2, CH])
        den = s1("den", [P, 2, 2, CH])
        on = s1("on", [P, TPC, D1])
        onm = s1("onm", [P, TPC, E1, D1])
        rd1 = s1("rd1", [P, TPC])
        mxp1 = s1("mxp1", [P, TPC, NC])
        mx1 = s1("mx1", [P, TPC])
        sk1 = s1("sk1", [P, TPC, P])
        sk2 = s1("sk2", [P, TPC, P])
        sq1 = s1("sq1", [P, TPC, P])
        sq2 = s1("sq2", [P, TPC, P])
        k1T = s1("k1T", [P, 2, T], F32R)
        k2T = s1("k2T", [P, 2, T], F32R)
        q1T = s1("q1T", [P, 2, T], F32R)
        q2T = s1("q2T", [P, 2, T], F32R)
        l1.close()

        s_load = sem("s_load")
        s_load1 = sem("s_load1")
        s_w = sem("s_w")
        s_out = sem("s_out")
        s_const = sem("s_const")
        s_pconst = sem("s_pconst")
        s_dve = sem("s_dve")
        s_pool = sem("s_pool")
        s_act = sem("s_act")
        s_mv = sem("s_mv")
        s_std = sem("s_std")
        s_xn = sem("s_xn")
        s_tp = sem("s_tp")
        s_xnT = sem("s_xnT")
        s_qkv = sem("s_qkv")
        s_qkvev = sem("s_qkvev")
        s_ms = sem("s_ms")
        s_rms = sem("s_rms")
        s_roped = sem("s_roped")
        s_stagek = sem("s_stagek")
        s_stageq = sem("s_stageq")
        s_stagev = sem("s_stagev")
        s_turn0 = sem("s_turn0")
        s_read0d = sem("s_read0d")
        s_read0a = sem("s_read0a")
        s_turn1 = sem("s_turn1")
        s_read1d = sem("s_read1d")
        s_read1a = sem("s_read1a")
        s_kM = sem("s_kM")
        s_m = sem("s_m")
        s_sc = sem("s_sc")
        s_exp = sem("s_exp")
        s_av = sem("s_av")
        s_oT = sem("s_oT")
        s_pj = sem("s_pj")
        s_res = sem("s_res")
        s_mixw = sem("s_mixw")
        s_mixc = sem("s_mixc")
        s_lin = sem("s_lin")
        s_lind = sem("s_lind")
        s_lina = sem("s_lina")
        s_lq = sem("s_lq")
        s_g1 = sem("s_g1")
        s_g2 = sem("s_g2")
        s_gate = sem("s_gate")
        s_wh = sem("s_wh")
        s_gadd = sem("s_gadd")
        s_hi1 = sem("s_hi1")
        s_st1 = sem("s_st1")
        s_m1 = sem("s_m1")
        s_sc1 = sem("s_sc1")
        s_exp1 = sem("s_exp1")
        s_av1 = sem("s_av1")
        s_den1 = sem("s_den1")
        s_oT1 = sem("s_oT1")
        s_z = sem("s_z")
        s_zt = sem("s_zt")
        s_zT = sem("s_zT")

        STEPS0 = [(c, jt) for c in range(NC) for jt in range(TPC * (c + 1))]
        N0 = len(STEPS0)
        LAST0 = [TPC * (c + 1) * (c + 2) // 2 for c in range(NC)]
        M1 = NT // 2
        U1 = NC * M1
        LN_FFN0, LN_LIN, LN_FFN1 = 1, 2, 3
        TP_LN = [0, 2, 3, 4]
        TP_ATTN = 1

        def foreground0(u):
            seq, k = [], u // 2 - 2
            if u < 2 * N0 * NG:
                seq.append(("S", u))
            if u % 2 == 0 and 0 <= k < N0 * NG:
                seq.append(("V", k))
                if k % N0 + 1 in LAST0:
                    seq.append(("O", k // N0, LAST0.index(k % N0 + 1)))
            k = u // 2 - 4
            if u % 2 and 0 <= k < N0 * NG and k % N0 + 1 in LAST0:
                seq.append(("F", k // N0, LAST0.index(k % N0 + 1)))
            return seq

        def foreground1(u):
            seq = [("S", u)] if u < U1 * H1 else []
            if 0 <= u - 2 < U1 * H1:
                seq += [("V", u - 2), ("D", u - 2)]
                if (u - 1) % M1 == 0:
                    seq.append(("O", (u - 1) // M1 - 1))
            if 0 <= u - 4 < U1 * H1 and (u - 3) % M1 == 0:
                seq.append(("F", (u - 3) // M1 - 1))
            return seq

        SEQ0 = merge(preparation0(), LEAD0, 2 * N0, 2 * N0 * NG, foreground0, 10)
        SEQ1 = merge(preparation1(), LEAD1, U1, U1 * H1, foreground1, 5)
        ring0 = Ring(SEQ0, ("max", "F"), ("k", "q", "q2"))
        ring1 = Ring(SEQ1, ("proj", "max", "F"), ("t", "q2"))

        def wait_read(eng, ring, step):
            a, d = (s_read0a, s_read0d) if ring is ring0 else (s_read1a, s_read1d)
            eng.wait_ge(a if step[0] in ring.by_act else d, ring.read[step])

        def wait_turn(eng, ring, step):
            eng.wait_ge(s_turn0 if ring is ring0 else s_turn1, ring.turn[step] + 1)

        def diag(c, jt):
            return max(0, P * (jt - TPC * c))

        block = ctx.enter_context(nc.Block())

        @block.sync
        def _(sp):
            sp.dma_start(x[:], A["x"].rearrange("(n p) d -> p n d", p=P)).then_inc(s_load, 16)
            sp.dma_start(ident[:], A["ident"]).then_inc(s_load, 16)
            sp.dma_start(wqkv[:], A["wqkvT"]).then_inc(s_load, 16)
            sp.dma_start(normw[:, 0, :], A["qnw"].partition_broadcast(P)).then_inc(s_load, 16)
            sp.dma_start(normw[:, 1, :], A["knw"].partition_broadcast(P)).then_inc(s_load, 16)
            sp.dma_start(rope[:], A["rope"].rearrange("(n p) a f -> p n a f", p=P)).then_inc(s_load, 16)
            sp.dma_start(masks[:], A["masks"].rearrange("a p q -> p a q")).then_inc(s_load, 16)
            sp.dma_start(wproj[:], A["wprojT"]).then_inc(s_load, 16)
            sp.dma_start(dft[:], A["dft"].rearrange("a p q -> p a q")).then_inc(s_load, 16)
            sp.dma_start(wfreq[:, 0, :], A["wre"]).then_inc(s_load, 16)
            sp.dma_start(wfreq[:, 1, :], A["wim"]).then_inc(s_load, 16)
            sp.dma_start(bias0[:], A["bias0"].partition_broadcast(P)).then_inc(s_load, 16)
            sp.wait_ge(s_res, 2 * NC)
            for i, name in enumerate(["lWq", "lWk", "lWv", "lWo"]):
                sp.dma_start(wlin[:, i, :], A[name]).then_inc(s_load1, 16)
            for i, name in enumerate(["lbk", "lbv", "lbo"]):
                sp.dma_start(blin[:, i, :], A[name].partition_broadcast(P)).then_inc(s_load1, 16)
            sp.dma_start(bqcol[:], A["lbq"].rearrange("(p a) -> p a", a=1)).then_inc(s_load1, 16)
            sp.dma_start(stdp[:, 0, :], A["stdp"].partition_broadcast(P)).then_inc(s_load1, 16)
            sp.dma_start(blockm[:], A["blockm"]).then_inc(s_load1, 16)
            sp.dma_start(wgate[:, 0, :], A["Ws"]).then_inc(s_load1, 16)
            sp.dma_start(wgate[:, 1, :], A["Wd"]).then_inc(s_load1, 16)
            for i in range(3):
                r = min(P, E1 * D1 - P * i)
                sp.dma_start(wout[0:r, i, :], A["Wo"][P * i:P * i + r, :]).then_inc(s_load1, 16)
            sp.dma_start(fold[:], A["fold"]).then_inc(s_load1, 16)
            sp.wait_ge(s_res, 3 * NC)
            for h in range(H1):
                if h:
                    sp.wait_ge(s_wh, h)
                c0 = h * E1 * D1
                sp.dma_start(wraw[:, 0, :], A["Wq"][:, c0:c0 + E1 * D1]).then_inc(s_w, 16)
                for i in range(2):
                    c1 = i * H1 * E1 * D1 + c0
                    sp.dma_start(wraw[:, 1 + i, :], A["Wkv"][:, c1:c1 + E1 * D1]).then_inc(s_w, 16)
            out_v = A["out"].rearrange("(n p) d -> p n d", p=P)
            for c in range(NC):
                sp.wait_ge(s_res, 3 * NC + c + 1)
                sp.dma_start(out_v[:, TPC * c:TPC * (c + 1), :], x[:, TPC * c:TPC * (c + 1), :]).then_inc(s_out, 16)
            sp.wait_ge(s_out, 16 * NC)

        @block.tensor
        def _(pe):
            def transpose_tiles(src, k, ready, count):
                for c in range(NC):
                    pe.wait_ge(ready, count(c))
                    for i in range(TPC):
                        n = TPC * c + i
                        mm = pe.transpose(ps[:, c, P * i:P * (i + 1)], src[:, n, :], ident[:])
                    mm.then_inc(s_tp, 1)

            pe.wait_ge(s_load, 16 * 12)
            transpose_tiles(xn, 0, s_xn, lambda c: c + 1)
            for n in range(NT):
                pe.wait_ge(s_xnT, n // TPC + 1)
                if n >= 4:
                    pe.wait_ge(s_qkvev, n - 3)
                pe.matmul(ps[:, 4 + n % 4, 0:3 * D], xnT[:, P * n:P * (n + 1)], wqkv[:],
                          start=True, stop=True).then_inc(s_qkv, 1)
            pe.wait_ge(s_qkvev, NT)

            pe.wait_ge(s_const, 1)
            pe.matmul(ps[:, 0, 0:P], wfreq[:, 0, :], dft[:, 0, :], start=True, stop=False)
            pe.matmul(ps[:, 0, 0:P], wfreq[:, 1, :], dft[:, 1, :], start=False, stop=True)
            pe.matmul(ps[:, 1, 0:P], wfreq[:, 1, :], dft[:, 0, :], start=True, stop=False)
            pe.matmul(ps[:, 1, 0:P], wfreq[:, 0, :], ndft[:], start=False, stop=True).then_inc(s_mixw, 1)
            pe.wait_ge(s_mixc, 1)
            pe.matmul(ps[:, 2, 0:P], ab[:, 0, :], dft[:, 0, :], start=True, stop=False)
            pe.matmul(ps[:, 2, 0:P], ab[:, 1, :], ndft[:], start=False, stop=True).then_inc(s_mixw, 1)
            pe.wait_ge(s_mixc, 2)

            def take(ring, step):
                turn = ring.turn[step]
                if turn >= len(RING):
                    wait_read(pe, ring, ring.order[turn - len(RING)])
                return ring.bank(step)

            def chunk_transposes(ring, step, src):
                b = take(ring, step)
                for i in range(TPC):
                    mm = pe.transpose(ps[:, b, P * i:P * (i + 1)], src(i), ident[:])
                return mm

            for step in SEQ0:
                kind = step[0]
                if kind == "k":
                    _, g, c = step
                    pe.wait_ge(s_stagek, g + 1)
                    chunk_transposes(ring0, step, lambda i: stagek[:, TPC * c + i, :, :].rearrange(
                        "p h r -> p (h r)")).then_inc(s_turn0, 1)
                elif kind in ("q", "q2"):
                    _, g, c = step
                    pe.wait_ge(s_stageq, g + 1)
                    if kind == "q2":
                        pe.wait_ge(s_m, NC * g + c + 1)
                    chunk_transposes(ring0, step, lambda i: stageq[:, TPC * c + i, :, :].rearrange(
                        "p h r -> p (h r)")).then_inc(s_turn0, 1)
                elif kind == "max":
                    _, g, c, i, b, h, n = step
                    bank = take(ring0, step)
                    wait_read(pe, ring0, ("q", g, c))
                    pe.wait_ge(s_kM, NC * GH * g + GH * (b + 1))
                    w = P * (i + 1) if b == c else CH
                    for a in range(n):
                        it = TPC * c + i
                        mm = pe.matmul(ps[:, bank, w * a:w * (a + 1)], qT[:, g % 2, P * it:P * (it + 1)],
                                       kM[:, g % 2, h + a, CH * b:CH * b + w], start=True, stop=b < c)
                        if b == c:
                            mm = pe.matmul(ps[:, bank, w * (a + 1) - P:w * (a + 1)], identb[:], masksb[:, 0, :],
                                           start=False, stop=True)
                    mm.then_inc(s_turn0, 1)
                elif kind == "S":
                    u = step[1]
                    g, (c, jt) = u // (2 * N0), STEPS0[u // 2 % N0]
                    off = diag(c, jt)
                    if u >= NS:
                        pe.wait_ge(s_exp, u - NS + 1)
                    wait_read(pe, ring0, ("q2", g, c))
                    pe.wait_ge(s_kM, NC * GH * g + GH * (c + 1))
                    for i in range(2):
                        h = 2 * (u % 2) + i
                        b = 2 * (u % NS) + i
                        mm = pe.matmul(ps[:, b, off:CH], kM[:, g % 2, h, P * jt:P * (jt + 1)],
                                       qT[:, g % 2, CH * c + off:CH * (c + 1)], start=True, stop=jt < TPC * c)
                        if jt >= TPC * c:
                            mm = pe.matmul(ps[:, b, off:off + P], identb[:], masksb[:, 1, :], start=False, stop=True)
                    mm.then_inc(s_sc, 1)
                elif kind == "V":
                    k = step[1]
                    g, (c, jt) = k // N0, STEPS0[k % N0]
                    off = diag(c, jt)
                    pe.wait_ge(s_stagev, g + 1)
                    pe.wait_ge(s_exp, 2 * k + 2)
                    if jt == 0 and g * NC + c:
                        pe.wait_ge(s_oT, g * NC + c)
                    for h in range(GH):
                        u = 2 * k + h // 2
                        mm = pe.matmul(ps[32 * h:32 * h + 32, ACC, off:CH], stagev[:, g % 2, jt, h, :],
                                       pbuf0[:, u % NP0, h % 2, off:CH], start=jt == 0, stop=jt == TPC * (c + 1) - 1,
                                       tile_position=(0, 32 * h))
                    mm.then_inc(s_av, 1)
                elif kind == "F":
                    _, g, c = step
                    m = g * NC + c
                    pe.wait_ge(s_oT, m + 1)
                    chunk_transposes(ring0, step,
                                     lambda i: oT[:, m % 2, P * i:P * (i + 1)]).then_inc(s_turn0, 1)
            wait_read(pe, ring0, ("F", NG - 1, NC - 1))

            transpose_tiles(xn, TP_ATTN, s_read0d, lambda c: ring0.read["F", NG - 1, NC - 1])
            for c in range(NC):
                pe.wait_ge(s_xnT, NC * TP_ATTN + c + 1)
                for i in range(TPC):
                    n = TPC * c + i
                    mm = pe.matmul(ps[:, 4 + c, P * i:P * (i + 1)], xnT[:, P * n:P * (n + 1)], wproj[:],
                                   start=True, stop=True)
                mm.then_inc(s_pj, 1)
            transpose_tiles(xn, TP_LN[LN_FFN0], s_xn, lambda c: NC * LN_FFN0 + c + 1)
            for c in range(NC):
                pe.wait_ge(s_xnT, NC * TP_LN[LN_FFN0] + c + 1)
                for i in range(TPC):
                    n = TPC * c + i
                    mm = pe.matmul(ps[:, 4 + c, P * i:P * (i + 1)], xnT[:, P * n:P * (n + 1)], mix[:],
                                   start=True, stop=True)
                mm.then_inc(s_pj, 1)

            pe.wait_ge(s_load1, 16 * 16)
            transpose_tiles(y_n, TP_LN[LN_LIN], s_xn, lambda c: NC * LN_LIN + c + 1)
            for c in range(NC):
                pe.wait_ge(s_xnT, NC * TP_LN[LN_LIN] + c + 1)
                pe.matmul(ps[:, 4 + c, :], wlin[:, 0, :], y_nT[:, CH * c:CH * (c + 1)],
                          start=True, stop=True).then_inc(s_lin, 1)
            for m in range(NT // 2):
                b = m % 4
                if m >= 4:
                    pe.wait_ge(s_lq, NC + m - 3)
                for i in range(2):
                    n = 2 * m + i
                    mm = pe.matmul(ps[:, b, 2 * D * i:2 * D * (i + 1)], y_nT[:, P * n:P * (n + 1)],
                                   wlin[:, 1:3, :].rearrange("p a d -> p (a d)"), start=True, stop=True)
                mm.then_inc(s_lin, 1)
            pe.wait_ge(s_lind, NC + NT // 2)
            for n in range(NT):
                mm = pe.matmul(ps[:, 4, 0:D + 2], kf[:, n, :], vf[:, n, :], start=n == 0, stop=n == NT - 1)
            mm.then_inc(s_lin, 1)
            pe.wait_ge(s_lind, NC + NT // 2 + 1)
            for c in range(NC):
                b = 2 * (c % 2)
                if c >= 2:
                    pe.wait_ge(s_lind, NC + NT // 2 + c)
                pe.matmul(ps[:, b, :], bd[:, 0, :], qfT[:, CH * c:CH * (c + 1)], start=True, stop=True)
                pe.matmul(ps[:, b + 1, :], bd[:, 1, :], qfT[:, CH * c:CH * (c + 1)],
                          start=True, stop=True).then_inc(s_lin, 1)
            for c in range(NC):
                pe.wait_ge(s_lind, NC + NT // 2 + 2 + c)
                for i in range(TPC):
                    n = TPC * c + i
                    mm = pe.matmul(ps[:, 4 + c, P * i:P * (i + 1)], aT[:, P * n:P * (n + 1)], wlin[:, 3, :],
                                   start=True, stop=True)
                mm.then_inc(s_pj, 1)

            transpose_tiles(y_n, TP_LN[LN_FFN1], s_xn, lambda c: NC * LN_FFN1 + c + 1)
            for n in range(NT):
                pe.wait_ge(s_xnT, NC * TP_LN[LN_FFN1] + n // TPC + 1)
                b, i = 4 + n // 6, n % 6
                mm = pe.matmul(ps[:, b, 80 * i:80 * (i + 1)], y_nT[:, P * n:P * (n + 1)],
                               wgate[:, :, :].rearrange("p a f -> p (a f)"), start=True, stop=True)
                if i == 5 or n == NT - 1:
                    mm.then_inc(s_g1, 1)
            pe.wait_ge(s_g2, 3)
            for step in SEQ1:
                kind = step[0]
                if kind == "proj":
                    _, h, n, j = step
                    bank = take(ring1, step)
                    pe.wait_ge(s_wh, h + 1)
                    o, t = ps[:, bank, 0:E1 * D1], slice(P * n, P * (n + 1))
                    pe.matmul(o, xh[:, t], wh[:, j, :], start=True, stop=False)
                    pe.matmul(o, xh[:, t], wl[:, j, :], start=False, stop=False)
                    pe.matmul(o, xl[:, t], wh[:, j, :], start=False, stop=True).then_inc(s_turn1, 1)
                elif kind == "t":
                    _, h, c, w = step
                    pe.wait_ge(s_st1, NC * h + c + 1)
                    src = (sk1, sk2, sq1)[w]
                    chunk_transposes(ring1, step, lambda i: src[:, i, :]).then_inc(s_turn1, 1)
                elif kind == "max":
                    _, h, it, b = step
                    bank = take(ring1, step)
                    wait_read(pe, ring1, ("t", h, NC - 1, 2))
                    pe.matmul(ps[:, bank, :], q1T[:, h % 2, P * it:P * (it + 1)],
                              k1T[:, h % 2, CH * b:CH * (b + 1)], start=True, stop=True).then_inc(s_turn1, 1)
                elif kind == "q2":
                    _, h, c = step
                    pe.wait_ge(s_m1, NC * h + c + 1)
                    chunk_transposes(ring1, step, lambda i: sq2[:, i, :]).then_inc(s_turn1, 1)
                elif kind == "S":
                    u = step[1]
                    h, c, m = u // U1, u % U1 // M1, u % M1
                    if u >= NS:
                        pe.wait_ge(s_exp1, u - NS + 1)
                    wait_read(pe, ring1, ("q2", h, c))
                    for i in range(2):
                        b = 2 * (u % NS) + i
                        t = slice(P * (2 * m + i), P * (2 * m + i + 1))
                        q = slice(CH * c, CH * (c + 1))
                        pe.matmul(ps[:, b, :], k1T[:, h % 2, t], q1T[:, h % 2, q], start=True, stop=False)
                        mm = pe.matmul(ps[:, b, :], k2T[:, h % 2, t], q2T[:, h % 2, q], start=False, stop=True)
                    mm.then_inc(s_sc1, 1)
                elif kind == "V":
                    u = step[1]
                    h, c, m = u // U1, u % U1 // M1, u % M1
                    pe.wait_ge(s_exp1, u + 1)
                    if m == 0 and h * NC + c:
                        pe.wait_ge(s_oT1, h * NC + c)
                    for i in range(2):
                        mm = pe.matmul(ps[64 * i:64 * i + 64, ACC, :], h_v[:, h % 2, 2 * m + i, :],
                                       pbuf1[:, u % NP1, i, :], start=m == 0, stop=m == M1 - 1,
                                       tile_position=(0, 64 * i))
                    mm.then_inc(s_av1, 1)
                elif kind == "F":
                    m = step[1]
                    bank = take(ring1, step)
                    pe.wait_ge(s_oT1, m + 1)
                    pe.wait_ge(s_den1, M1 * (m + 1))
                    for i in range(TPC):
                        t = slice(P * i, P * (i + 1))
                        pe.matmul(ps[:, bank, D1 * i:D1 * (i + 1)], oT[:, m % 2, t], fold[:],
                                  start=i == 0, stop=True, skip_group_check=True)
                    for i in range(TPC):
                        t = slice(P * i, P * (i + 1))
                        o = ps[:, bank, TPC * D1 + i:TPC * D1 + i + 1]
                        pe.matmul(o, den[:, m % 2, 0, t], ones[:], start=False, stop=False, skip_group_check=True)
                        mm = pe.matmul(o, den[:, m % 2, 1, t], ones[:], start=False, stop=True, skip_group_check=True)
                    mm.then_inc(s_turn1, 1)

            pe.wait_ge(s_z, 2 * H1 * NC)
            for n in range(NT):
                b = n % 2
                if n >= 2:
                    pe.wait_ge(s_zT, n - 1)
                for i in range(3):
                    r = min(P, E1 * D1 - P * i)
                    mm = pe.transpose(ps[0:r, b, P * i:P * (i + 1)],
                                      z[:, n, :, :].rearrange("p e d -> p (e d)")[:, P * i:P * i + r], ident[:])
                mm.then_inc(s_zt, 1)
                pe.wait_ge(s_zT, n + 1)
                for i in range(3):
                    r = min(P, E1 * D1 - P * i)
                    mm = pe.matmul(ps[:, 2 + n // TPC, P * (n % TPC):P * (n % TPC + 1)], zT[0:r, i, :], wout[0:r, i, :],
                                   start=i == 0, stop=i == 2)
                if n % TPC == TPC - 1:
                    mm.then_inc(s_pj, 1)

        @block.scalar
        def _(act):
            def norm_std(k):
                act.wait_ge(s_mv, k + 1)
                nc.scalar.activation(std[:], meanvar[:, :, 1], ACT.Sqrt, bias=eps[:, 0:1]).then_inc(s_std, 1)

            def copy_chunks(dst, k):
                for c in range(NC):
                    act.wait_ge(s_tp, NC * k + c + 1)
                    nc.scalar.activation(dst[:, CH * c:CH * (c + 1)], ps[:, c, :], ACT.Copy).then_inc(s_xnT, 1)

            norm_std(0)
            copy_chunks(xnT, 0)
            for n in range(NT):
                act.wait_ge(s_qkv, n + 1)
                nc.scalar.activation(qkv[:, n, :], ps[:, 4 + n % 4, 0:3 * D], ACT.Copy).then_inc(s_qkvev, 1)
            act.wait_ge(s_ms, 1)
            nc.scalar.activation(ms[:], ms[:], ACT.Sqrt, bias=eps[:, 1:2], scale=1.0 / D0).then_inc(s_rms, 1)
            act.wait_ge(s_mixw, 1)
            nc.scalar.activation(ab[:], ps[:, 0:2, 0:P], ACT.Copy).then_inc(s_mixc, 1)
            act.wait_ge(s_mixw, 2)
            nc.scalar.activation(mix[:], ps[:, 2, 0:P], ACT.Copy, scale=1.0 / D).then_inc(s_mixc, 1)

            for step in SEQ0:
                kind = step[0]
                if kind in ("k", "q", "q2"):
                    _, g, c = step
                    wait_turn(act, ring0, step)
                    if kind == "k":
                        dst = kT[:, CH * c:CH * (c + 1)]
                        if g:
                            act.wait_ge(s_kM, NC * GH * (g - 1) + GH * (c + 1))
                    else:
                        dst = qT[:, g % 2, CH * c:CH * (c + 1)]
                        if g >= 2:
                            act.wait_ge(s_sc, 2 * N0 * (g - 1))
                    nc.scalar.activation(dst, ps[:, ring0.bank(step), :], ACT.Copy).then_inc(s_read0a, 1)
                elif kind == "S":
                    u = step[1]
                    off = diag(*STEPS0[u // 2 % N0])
                    act.wait_ge(s_sc, u + 1)
                    if u >= NP0:
                        act.wait_ge(s_av, (u - NP0) // 2 + 1)
                    b = 2 * (u % NS)
                    nc.scalar.activation(pbuf0[:, u % NP0, :, off:CH], ps[:, b:b + 2, off:CH], ACT.Exp,
                                         scale=float(D0) ** -0.5).then_inc(s_exp, 1)
                elif kind == "O":
                    _, g, c = step
                    m = g * NC + c
                    act.wait_ge(s_av, N0 * g + LAST0[c])
                    if m >= 2:
                        wait_turn(act, ring0, ("F", (m - 2) // NC, (m - 2) % NC))
                    nc.scalar.activation(oT[:, m % 2, :], ps[:, ACC, :], ACT.Copy).then_inc(s_oT, 1)
            copy_chunks(xnT, TP_ATTN)
            norm_std(LN_FFN0)
            copy_chunks(xnT, TP_LN[LN_FFN0])
            norm_std(LN_LIN)
            copy_chunks(y_nT, TP_LN[LN_LIN])
            act.wait_ge(s_load1, 16 * 16)
            nc.scalar.activation(stdp[:, 1, :], stdp[:, 0, :], ACT.Exp, scale=-1.0).then_inc(s_lina, 1)
            for m in range(NC + NT // 2):
                act.wait_ge(s_lq, m + 1)
                w = CH if m < NC else 2 * D
                nc.scalar.activation(lt[:, m % 2, 0, 0:w], lt[:, m % 2, 0, 0:w], ACT.Exp).then_inc(s_lina, 1)
            norm_std(LN_FFN1)
            copy_chunks(y_nT, TP_LN[LN_FFN1])
            for b in range(3):
                act.wait_ge(s_g1, b + 1)
                w = min(6, NT - 6 * b)
                nc.scalar.activation(sig[:, 6 * b:6 * b + w, :, :, :].rearrange("p n a h e -> p (n a h e)"),
                                     ps[:, 4 + b, 0:80 * w], ACT.Exp, scale=-1.0).then_inc(s_g2, 1)
            for step in SEQ1:
                kind = step[0]
                if kind == "stage":
                    _, h, c = step
                    tiles = slice(TPC * c, TPC * (c + 1))
                    act.wait_ge(s_gadd, NT * h + TPC * (c + 1))
                    if h or c:
                        wait_turn(act, ring1, ("t", h, c - 1, 2) if c else ("t", h - 1, NC - 1, 2))
                    nc.scalar.activation(sk1[:].rearrange("p n (a d) -> p n a d", a=2).bitcast(F32R),
                                         h_qk[:, 1, tiles, :].unsqueeze(2).to_broadcast([P, TPC, 2, D1]), ACT.Copy)
                    nc.scalar.activation(sq1[:, :, 0:D1].bitcast(F32R), h_qk[:, 0, tiles, :],
                                         ACT.Copy).then_inc(s_hi1, 1)
                elif kind == "t":
                    _, h, c, w = step
                    wait_turn(act, ring1, step)
                    if h >= 2:
                        act.wait_ge(s_sc1, U1 * (h - 1))
                    nc.scalar.activation((k1T, k2T, q1T)[w][:, h % 2, CH * c:CH * (c + 1)],
                                         ps[:, ring1.bank(step), :], ACT.Copy).then_inc(s_read1a, 1)
                elif kind == "q2":
                    _, h, c = step
                    wait_turn(act, ring1, step)
                    nc.scalar.activation(q2T[:, h % 2, CH * c:CH * (c + 1)],
                                         ps[:, ring1.bank(step), :], ACT.Copy).then_inc(s_read1a, 1)
                elif kind == "S":
                    u = step[1]
                    act.wait_ge(s_sc1, u + 1)
                    if u >= NP1:
                        act.wait_ge(s_av1, u - NP1 + 1)
                        act.wait_ge(s_den1, u - NP1 + 1)
                    b = 2 * (u % NS)
                    nc.scalar.activation(pbuf1[:, u % NP1, :, :], ps[:, b:b + 2, :], ACT.Exp,
                                         scale=float(D1) ** -0.5).then_inc(s_exp1, 1)
                elif kind == "O":
                    m = step[1]
                    act.wait_ge(s_av1, M1 * (m + 1))
                    if m >= 2:
                        wait_turn(act, ring1, ("F", m - 2))
                    nc.scalar.activation(oT[:, m % 2, :], ps[:, ACC, :], ACT.Copy).then_inc(s_oT1, 1)
            for n in range(NT):
                act.wait_ge(s_zt, n + 1)
                nc.scalar.activation(zT[:, 0:2, :].rearrange("p a t -> p (a t)"), ps[:, n % 2, 0:2 * P], ACT.Copy)
                nc.scalar.activation(zT[0:64, 2, :], ps[0:64, n % 2, 2 * P:3 * P], ACT.Copy).then_inc(s_zT, 1)

        @block.vector
        def _(dve):
            v = nc.vector
            order = [0]

            def link(ins):
                order[0] += 1
                ins.then_inc(s_dve, 1)
                dve.wait_ge(s_dve, order[0])

            def norm(k, dst):
                for n in range(NT):
                    ins = v.bn_stats(stats[:, n, :], x[:, n, :])
                link(ins)
                for n in range(NT):
                    ins = v.bn_aggr(meanvar[:, n, :], stats[:, n, :])
                ins.then_inc(s_mv, 1)
                dve.wait_ge(s_std, k + 1)
                link(v.reciprocal(rstd[:], std[:]))
                for n in range(NT):
                    ins = v.tensor_scalar(dst[:, n, :], x[:, n, :], meanvar[:, n, 0:1], rstd[:, n:n + 1],
                                          ALU.subtract, ALU.mult)
                    if n % TPC == TPC - 1:
                        ins.then_inc(s_xn, 1)

            def residual(bank, k, bias=None):
                for c in range(NC):
                    dve.wait_ge(s_pj, NC * k + c + 1)
                    xc = x[:, TPC * c:TPC * (c + 1), :]
                    ins = v.tensor_tensor(xc, ps[:, bank + c, :].rearrange("p (n d) -> p n d", n=TPC), xc, ALU.add)
                    if bias is not None:
                        link(ins)
                        ins = v.tensor_tensor(xc, xc, bias.unsqueeze(1).to_broadcast([P, TPC, D]), ALU.add)
                    ins.then_inc(s_res, 1)
                dve.wait_ge(s_res, NC * (k + 1))

            v.memset(eps[:, 0:1], LN_EPS)
            v.memset(eps[:, 1:2], RMS_EPS)
            dve.wait_ge(s_load, 16 * 12)
            norm(0, xn)
            v.tensor_copy(identb[:], ident[:])
            v.tensor_copy(masksb[:], masks[:])
            v.tensor_scalar(ndft[:], dft[:, 1, :], -1.0, None, ALU.mult).then_inc(s_const, 1)

            dve.wait_ge(s_qkvev, NT)
            qk = qkv[:, :, 0:2 * D]
            qkh = qk.rearrange("p n (h d) -> p n h d", d=D0)
            link(v.tensor_tensor(tmp[:].rearrange("p n h d -> p n (h d)"), qk, qk, ALU.mult))
            v.tensor_reduce(ms[:], tmp[:], AX.X, ALU.add).then_inc(s_ms, 1)
            dve.wait_ge(s_rms, 1)
            link(v.reciprocal(ms[:], ms[:]))
            link(v.tensor_tensor(qkh, qkh, ms[:].unsqueeze(3).to_broadcast([P, NT, 2 * H0, D0]), ALU.mult))
            for i in range(2):
                q = qkh[:, :, H0 * i:H0 * (i + 1), :]
                w = normw[:, i, :].unsqueeze(1).unsqueeze(1).to_broadcast([P, NT, H0, D0])
                link(v.tensor_tensor(q, q, w, ALU.mult))
            half = D0 // 2
            qa, qb = qkh[:, :, :, 0:half], qkh[:, :, :, half:D0]
            ta, tb = tmp[:, :, :, 0:half], tmp[:, :, :, half:D0]
            cos, sin = (rope[:, :, i, :].unsqueeze(2).to_broadcast([P, NT, 2 * H0, half]) for i in range(2))
            v.tensor_tensor(ta, qa, sin, ALU.mult)
            link(v.tensor_tensor(tb, qb, sin, ALU.mult))
            v.tensor_tensor(qa, qa, cos, ALU.mult)
            link(v.tensor_tensor(qb, qb, cos, ALU.mult))
            v.tensor_tensor(qa, qa, tb, ALU.subtract)
            link(v.tensor_tensor(qb, qb, ta, ALU.add))
            dve.wait_ge(s_pconst, 1)

            for step in SEQ0:
                kind = step[0]
                if kind == "stagek":
                    g = step[1]
                    if g:
                        wait_turn(dve, ring0, ("k", g - 1, NC - 1))
                    gk = qkv[:, :, D + 32 * g:D + 32 * (g + 1)].rearrange("p n (h d) -> p n h d", d=D0)
                    v.tensor_copy(stagek[:, :, :, D0:2 * D0].bitcast(F32R), gk)
                    link(v.tensor_copy(stagek[:, :, :, 0:D0].bitcast(F32R), gk))
                    v.tensor_tensor(stagek[:, :, :, 2 * D0:3 * D0], gk, stagek[:, :, :, 0:D0],
                                    ALU.subtract).then_inc(s_stagek, 1)
                elif kind == "stageq":
                    g = step[1]
                    if g:
                        wait_turn(dve, ring0, ("q2", g - 1, NC - 1))
                    gq = qkv[:, :, 32 * g:32 * (g + 1)].rearrange("p n (h d) -> p n h d", d=D0)
                    v.tensor_copy(stageq[:, :, :, 2 * D0:3 * D0].bitcast(F32R), gq)
                    v.tensor_copy(stageq[:, :, :, 0:D0].bitcast(F32R), gq)
                    link(v.memset(stageq[:, :, :, 24:25], 0.0))
                    v.tensor_tensor(stageq[:, :, :, D0:2 * D0], gq, stageq[:, :, :, 0:D0],
                                    ALU.subtract).then_inc(s_stageq, 1)
                elif kind == "max":
                    _, g, c, i, b, h, n = step
                    wait_turn(dve, ring0, step)
                    w = P * (i + 1) if b == c else CH
                    v.tensor_reduce(mxp[:, i, h:h + n, b],
                                    ps[:, ring0.bank(step), 0:w * n].rearrange("p (h k) -> p h k", h=n),
                                    AX.X, ALU.max).then_inc(s_read0d, 1)
                    last = step
                elif kind == "m":
                    _, g, c = step
                    wait_read(dve, ring0, last)
                    if g or c:
                        dve.wait_ge(s_m, NC * g + c)
                    link(v.tensor_reduce(mx[:], mxp[:, :, :, 0:c + 1], AX.X, ALU.max))
                    v.tensor_scalar(stageq[:, TPC * c:TPC * (c + 1), :, 24:25].bitcast(F32R), mx[:].unsqueeze(3),
                                    -1.0, None, ALU.mult).then_inc(s_m, 1)
                elif kind == "F":
                    _, g, c = step
                    wait_turn(dve, ring0, step)
                    if g or c:
                        wait_read(dve, ring0, ("F", g, c - 1) if c else ("F", g - 1, NC - 1))
                    o = ps[:, ring0.bank(step), :].rearrange("p (n h r) -> p n h r", n=TPC, h=GH)
                    link(v.reciprocal(rden[:].unsqueeze(3), o[:, :, :, D0:D0 + 1]))
                    dst = xn[:, TPC * c:TPC * (c + 1), 32 * g:32 * (g + 1)].rearrange("p n (h d) -> p n h d", d=D0)
                    v.tensor_tensor(dst, o[:, :, :, 0:D0], rden[:].unsqueeze(3).to_broadcast([P, TPC, GH, D0]),
                                    ALU.mult).then_inc(s_read0d, 1)
            residual(4, 0)
            norm(LN_FFN0, xn)
            residual(4, 1, bias0[:])

            norm(LN_LIN, y_n)
            v.memset(vf[:, :, D:D + 1], 1.0)
            v.memset(vf[:, :, D + 1:D + 2], 0.0)
            v.memset(ones[:], 1.0)
            dve.wait_ge(s_lina, 1)
            link(v.tensor_scalar(stdp[:, 1, :], stdp[:, 1, :], 1.0, None, ALU.add))
            link(v.reciprocal(stdp[:, 2, :], stdp[:, 1, :]))
            link(v.tensor_tensor(bd[:, 2, :].rearrange("p (h d) -> p h d", d=D0),
                                 blockm[:].rearrange("p (h d) -> p h d", d=D0),
                                 stdp[:, 2, :].unsqueeze(2).to_broadcast([P, H0, D0]), ALU.mult))

            def split_sign(m):
                dve.wait_ge(s_lin, m + 1)
                if m >= 2:
                    dve.wait_ge(s_lind, m - 1)
                if m < NC:
                    z0, z1 = lt[:, m % 2, 0, :], lt[:, m % 2, 1, :]
                    v.tensor_scalar(z0, ps[:, 4 + m, :], bqcol[:, 0:1], 0.0, ALU.add, ALU.min)
                    v.tensor_scalar(z1, ps[:, 4 + m, :], bqcol[:, 0:1], 0.0, ALU.add, ALU.max).then_inc(s_lq, 1)
                    return
                j = m - NC
                kv = ps[:, j % 4, :].rearrange("p (n a d) -> p n a d", n=2, a=2)
                z0, z1 = (lt[:, m % 2, i, 0:2 * D].rearrange("p (n d) -> p n d", n=2) for i in range(2))
                bk, bv = (blin[:, i, :].unsqueeze(1).to_broadcast([P, 2, D]) for i in range(2))
                link(v.tensor_tensor(z1, kv[:, :, 0, :], bk, ALU.add))
                v.tensor_tensor(vf[:, 2 * j:2 * j + 2, 0:D], kv[:, :, 1, :], bv, ALU.add)
                link(v.tensor_scalar(z0, z1, 0.0, None, ALU.min))
                v.tensor_scalar(z1, z1, 0.0, None, ALU.max).then_inc(s_lq, 1)

            def elu1(m):
                dve.wait_ge(s_lina, m + 2)
                dve.wait_ge(s_lq, m + 1)
                if m < NC:
                    out, z0, z1 = qfT[:, CH * m:CH * (m + 1)], lt[:, m % 2, 0, :], lt[:, m % 2, 1, :]
                else:
                    out = kf[:, 2 * (m - NC):2 * (m - NC) + 2, :]
                    z0, z1 = (lt[:, m % 2, i, 0:2 * D].rearrange("p (n d) -> p n d", n=2) for i in range(2))
                v.tensor_tensor(out, z0, z1, ALU.add).then_inc(s_lind, 1)

            items = NC + NT // 2
            for m in range(items + 1):
                if m < items:
                    split_sign(m)
                if m:
                    elu1(m - 1)
            dve.wait_ge(s_lin, items + 1)
            v.tensor_tensor(bd[:, 0, :], ps[:, 4, 0:D], bd[:, 2, :], ALU.mult)
            v.tensor_scalar(bd[:, 1, :], blockm[:], ps[:, 4, D:D + 1], None, ALU.mult).then_inc(s_lind, 1)
            dve.wait_ge(s_lind, items + 1)
            for c in range(NC):
                dve.wait_ge(s_lin, items + 2 + c)
                b = 2 * (c % 2)
                z0, z1 = lt[:, c % 2, 0, :], lt[:, c % 2, 1, :]
                link(v.tensor_scalar(z0, ps[:, b + 1, :], 1e-6, None, ALU.add))
                link(v.reciprocal(z1, z0))
                v.tensor_tensor(aT[:, CH * c:CH * (c + 1)], ps[:, b, :], z1, ALU.mult).then_inc(s_lind, 1)
            residual(4, 2, blin[:, 2, :])

            norm(LN_FFN1, y_n)
            dve.wait_ge(s_xnT, NC * (TP_LN[LN_FFN1] + 1))
            link(v.tensor_copy(xh[:], y_nT[:]))
            link(v.tensor_tensor(xl[:], y_nT[:], xh[:].bitcast(F32), ALU.subtract))
            dve.wait_ge(s_g2, 3)
            link(v.tensor_scalar(sig[:], sig[:], 1.0, None, ALU.add))
            link(v.reciprocal(sig[:], sig[:]))
            sg = sig[:].rearrange("p n a h e -> p (n a h) e")
            rk = rank[:].rearrange("p n a h e -> p (n a h) e")
            link(v.memset(rank[:], 0.0))
            for r in range(1, E1):
                lo, hi = slice(0, E1 - r), slice(r, E1)
                v.tensor_tensor(beats[:, 0, :, 0:E1 - r], sg[:, :, hi], sg[:, :, lo], ALU.is_gt)
                link(v.tensor_tensor(beats[:, 1, :, 0:E1 - r], sg[:, :, lo], sg[:, :, hi], ALU.is_ge))
                link(v.tensor_tensor(rk[:, :, lo], rk[:, :, lo], beats[:, 0, :, 0:E1 - r], ALU.add))
                link(v.tensor_tensor(rk[:, :, hi], rk[:, :, hi], beats[:, 1, :, 0:E1 - r], ALU.add))
            link(v.tensor_scalar(rank[:], rank[:], TOP - 0.5, None, ALU.is_lt))
            v.tensor_copy(maskd[:], rank[:, :, 1, :, :])
            for i, a in enumerate((1, 0)):
                ins = v.tensor_tensor(gate[:, :, i, :, :], sig[:, :, a, :, :], rank[:, :, a, :, :], ALU.mult)
            link(ins)
            v.memset(sq2[:, :, D1:P], 0.0)
            v.memset(sk2[:, :, D1:D1 + 1], 1.0)
            link(v.memset(sk2[:, :, D1 + 1:P], 0.0))

            for step in SEQ1:
                kind = step[0]
                if kind == "w":
                    h = step[1]
                    dve.wait_ge(s_w, 48 * (h + 1))
                    if h:
                        wait_turn(dve, ring1, ("proj", h - 1, NT - 1, 2))
                    link(v.tensor_copy(wh[:], wraw[:]))
                    v.tensor_tensor(wl[:], wraw[:], wh[:].bitcast(F32), ALU.subtract).then_inc(s_wh, 1)
                elif kind == "proj":
                    _, h, n, j = step
                    m = NT * h + n
                    wait_turn(dve, ring1, step)
                    if m >= 2:
                        dve.wait_ge(s_gadd, m - 1)
                    v.tensor_tensor(gt[:, m % 2, j], ps[:, ring1.bank(step), 0:E1 * D1].rearrange(
                        "p (e d) -> p e d", e=E1), gate[:, n, min(j, 1), h, :].unsqueeze(2).to_broadcast([P, E1, D1]),
                        ALU.mult).then_inc(s_read1d, 1)
                elif kind == "stage":
                    _, h, c = step
                    tiles = slice(TPC * c, TPC * (c + 1))
                    dve.wait_ge(s_hi1, NC * h + c + 1)
                    v.tensor_tensor(sk2[:, :, 0:D1], h_qk[:, 1, tiles, :], sk1[:, :, 0:D1], ALU.subtract)
                    v.tensor_tensor(sq1[:, :, D1:P], h_qk[:, 0, tiles, :], sq1[:, :, 0:D1],
                                    ALU.subtract).then_inc(s_st1, 1)
                elif kind == "max":
                    _, h, it, b = step
                    wait_turn(dve, ring1, step)
                    v.tensor_reduce(mxp1[:, it % TPC, b:b + 1], ps[:, ring1.bank(step), :],
                                    AX.X, ALU.max).then_inc(s_read1d, 1)
                    last = step
                elif kind == "m":
                    _, h, c = step
                    wait_read(dve, ring1, last)
                    if h or c:
                        dve.wait_ge(s_m1, NC * h + c)
                    if c:
                        wait_turn(dve, ring1, ("q2", h, c - 1))
                    elif h:
                        wait_turn(dve, ring1, ("q2", h - 1, NC - 1))
                    link(v.tensor_reduce(mx1[:], mxp1[:], AX.X, ALU.max))
                    v.tensor_copy(sq2[:, :, 0:D1].bitcast(F32R), h_qk[:, 0, TPC * c:TPC * (c + 1), :])
                    v.tensor_scalar(sq2[:, :, D1:D1 + 1].bitcast(F32R), mx1[:].unsqueeze(2), -1.0, None,
                                    ALU.mult).then_inc(s_m1, 1)
                elif kind == "D":
                    u = step[1]
                    mc, m = u // M1, u % M1
                    dve.wait_ge(s_exp1, u + 1)
                    w, dn = pbuf1[:, u % NP1, :, :], den[:, mc % 2, :, :]
                    if m == 0:
                        if mc >= 2:
                            wait_turn(dve, ring1, ("F", mc - 2))
                        v.tensor_copy(dn, w).then_inc(s_den1, 1)
                    else:
                        dve.wait_ge(s_den1, u)
                        v.tensor_tensor(dn, dn, w, ALU.add).then_inc(s_den1, 1)
                elif kind == "F":
                    m = step[1]
                    wait_turn(dve, ring1, step)
                    if m:
                        dve.wait_ge(s_z, 2 * m - 1)
                        wait_read(dve, ring1, ("F", m - 1))
                    b = ring1.bank(step)
                    link(v.reciprocal(rd1[:], ps[:, b, TPC * D1:TPC * (D1 + 1)]))
                    v.tensor_tensor(on[:], ps[:, b, 0:TPC * D1].rearrange("p (n d) -> p n d", n=TPC),
                                    rd1[:].unsqueeze(2).to_broadcast([P, TPC, D1]), ALU.mult).then_inc(s_read1d, 1)
            residual(2, 3)

        @block.gpsimd
        def _(pool):
            g_ = nc.gpsimd
            order = [0]

            def link(ins):
                order[0] += 1
                ins.then_inc(s_pool, 1)
                pool.wait_ge(s_pool, order[0])

            g_.memset(stageq[:, :, :, 24:32], 0.0)
            g_.memset(stagek[:, :, :, 24:25], 1.0)
            g_.memset(stagek[:, :, :, 25:32], 0.0)
            g_.memset(stagev[:, :, :, :, D0:D0 + 1].rearrange("p b n h r -> p (b n h) r"), 1.0)
            g_.memset(stagev[:, :, :, :, D0 + 1:32].rearrange("p b n h r -> p (b n h) r"), 0.0)
            g_.memset(kM[:, 0].bitcast(F32), 0.0)
            g_.memset(kM[:, 1].bitcast(F32), 0.0).then_inc(s_pconst, 1)
            pool.wait_ge(s_pconst, 1)
            pool.wait_ge(s_qkvev, NT)
            done = 0
            for step in SEQ0:
                if step[0] == "k":
                    _, g, c = step
                    wait_read(pool, ring0, step)
                    if g >= 2:
                        pool.wait_ge(s_sc, 2 * N0 * (g - 1))
                    for h in range(GH):
                        rows = slice(32 * h, 32 * h + 32)
                        g_.tensor_copy(kM[rows, g % 2, h, CH * c:CH * (c + 1)],
                                       kT[rows, CH * c:CH * (c + 1)]).then_inc(s_kM, 1)
                        done += 1
                        pool.wait_ge(s_kM, done)
                    if c == NC - 1:
                        if g >= 2:
                            pool.wait_ge(s_av, N0 * (g - 1))
                        gv = qkv[:, :, 2 * D + 32 * g:2 * D + 32 * (g + 1)].rearrange("p n (h d) -> p n h d", d=D0)
                        g_.tensor_copy(stagev[:, g % 2, :, :, 0:D0], gv).then_inc(s_stagev, 1)
                        pool.wait_ge(s_stagev, g + 1)
            pool.wait_ge(s_g1, 3)
            link(g_.memset(z[:], 0.0))
            for step in SEQ1:
                if step[0] == "proj" and step[3] == 2:
                    _, h, n, _j = step
                    m = NT * h + n
                    wait_read(pool, ring1, step)
                    if h and n == 0:
                        pool.wait_ge(s_m1, NC * h)
                    if h >= 2 and n == 0:
                        pool.wait_ge(s_av1, U1 * (h - 1))
                    t = gt[:, m % 2]
                    link(g_.tensor_tensor(gs[:], t[:, :, 0:2, :], t[:, :, 2:4, :], ALU.add))
                    link(g_.tensor_tensor(gsum[:], gs[:, :, 0, :], gs[:, :, 1, :], ALU.add))
                    g_.tensor_tensor(h_qk[:, :, n, :], gsum[:, 0:2, :], t[:, 0:2, 4, :], ALU.add)
                    g_.tensor_tensor(h_v[:, h % 2, n, :], gsum[:, 2, :], t[:, 2, 4, :], ALU.add).then_inc(s_gadd, 1)
                elif step[0] == "F":
                    mc = step[1]
                    h, c = mc // NC, mc % NC
                    wait_read(pool, ring1, step)
                    tiles = slice(TPC * c, TPC * (c + 1))
                    g_.tensor_tensor(onm[:], on[:].unsqueeze(2).to_broadcast([P, TPC, E1, D1]),
                                     maskd[:, tiles, h, :].unsqueeze(3).to_broadcast([P, TPC, E1, D1]),
                                     ALU.mult).then_inc(s_z, 1)
                    pool.wait_ge(s_z, 2 * mc + 1)
                    g_.tensor_tensor(z[:, tiles], z[:, tiles], onm[:], ALU.add).then_inc(s_z, 1)
                    pool.wait_ge(s_z, 2 * mc + 2)


_INPUTS = {
    "x": "L0_attn_x", "qnw": "L0_attn_q_norm_w", "knw": "L0_attn_k_norm_w", "wre": "L0_ffn_w_freq_real",
    "wim": "L0_ffn_w_freq_imag", "bias0": "L0_ffn_bias", "lbq": "L1_attn_bq", "lbk": "L1_attn_bk",
    "lbv": "L1_attn_bv", "lbo": "L1_attn_bo", "stdp": "L1_attn_stdp", "Ws": "L1_ffn_Ws", "Wd": "L1_ffn_Wd",
    "Wq": "L1_ffn_Wq", "Wkv": "L1_ffn_Wkv",
}
_TRANSPOSED = {"wqkvT": "L0_attn_w_qkv", "wprojT": "L0_attn_w_proj", "lWq": "L1_attn_Wq", "lWk": "L1_attn_Wk",
               "lWv": "L1_attn_Wv", "lWo": "L1_attn_Wo"}


def constants():
    f32 = np.float32
    freqs = (f32(32.0) ** (-np.arange(0, D0, 2, dtype=f32) / f32(D0))).astype(f32)
    ang = (np.arange(T, dtype=f32)[:, None] * freqs[None, :]).astype(f32).astype(np.float64)
    a = 2 * np.pi * (np.outer(np.arange(D), np.arange(D)) % D) / D
    i, j = np.arange(P)[:, None], np.arange(P)[None, :]
    return {
        "ident": np.eye(P, dtype=f32),
        "rope": np.stack([np.cos(ang), np.sin(ang)], 1).astype(f32),
        "masks": np.stack([np.where(j > i, NEG, 0.0), np.where(i > j, NEG, 0.0)]).astype(f32),
        "dft": np.stack([np.cos(a), np.sin(a)]).astype(f32),
        "blockm": (i // D0 == j // D0).astype(f32),
        "fold": np.concatenate([np.eye(D1), np.eye(D1)]).astype(f32),
    }


def kernel(**inputs):
    import concourse.bacc as _bacc
    from concourse.bass_utils import run_bass_kernel_spmd as _run

    arrays = {k: np.ascontiguousarray(inputs[v]) for k, v in _INPUTS.items()}
    arrays["x"] = arrays["x"].reshape(T, D)
    arrays |= {k: np.ascontiguousarray(np.asarray(inputs[v]).T) for k, v in _TRANSPOSED.items()}
    wo = np.asarray(inputs["L1_ffn_Wo"]).reshape(D1, E1, D).transpose(1, 0, 2)
    arrays["Wo"] = np.ascontiguousarray(wo).reshape(E1 * D1, D)
    arrays |= constants()
    nc = _bacc.Bacc("TRN2", target_bir_lowering=False, num_devices=1)
    aps = {k: nc.dram_tensor(f"in_{k}", a.shape, mybir.dt.from_np(a.dtype), kind="ExternalInput").ap()
           for k, a in arrays.items()}
    aps["out"] = nc.dram_tensor("out_0", (T, D), F32, kind="ExternalOutput").ap()
    build(nc, aps)
    r = _run(nc, [{f"in_{k}": a for k, a in arrays.items()}], core_ids=[0])
    return r.results[0]["out_0"].reshape(1, T, D)
```

```python
from contextlib import ExitStack

import numpy as np

import concourse.bass as bass
from concourse import mybir

F32 = mybir.dt.float32
F32R = mybir.dt.float32r
BF16 = mybir.dt.bfloat16
ALU = mybir.AluOpType
ACT = mybir.ActivationFunctionType
AX = mybir.AxisListType

P = 128
T = 2048
NT = T // P
D = 128
CH = 512
NC = T // CH
TPC = CH // P
H0, D0 = 16, 8
GH = 4
NG = H0 // GH
H1, E1, D1 = 8, 5, 64
TOP = 3
LN_EPS = 1e-5
RMS_EPS = 1e-6
NEG = -1e30
NP0, NP1 = 6, 5
NS = 2
M1 = NT // 2
U1 = NC * M1
ACC = 6
RING = (4, 5, 7)
MAX0 = (-1.5, 6.0, 21.0, 44.0)
PROJ1 = (2.05, 20.5)
STAGE1 = (2.2, 3.0, 3.7)
SHARE = 704
MAX1 = 1.6


def preparation0():
    out, late = [], None
    for g in range(NG):
        out += [(("stagek", g), 3), (("k", g, 0), 1), (("k", g, 1), 1)]
        if late:
            out.append((late, 1))
        out += [(("stageq", g), 3), (("q", g, 0), 1)]
        if g == 0:
            out += [(("rest", 0), 1), (("rest", 1), 1)]
        late = None
        for c in range(NC):
            if c + 1 < NC:
                out.append((("q", g, c + 1), 1))
            if c + 2 < NC:
                out.append((("k", g, c + 2), 1))
            items = []
            for i in range(TPC):
                for b in range(c + 1):
                    n = min(GH, TPC // (i + 1)) if b == c else 1
                    items += [(("max", g, c, i, b, h, n), 1) for h in range(0, GH, n)]
            if late:
                items.insert(5, (late, 1))
            out += items + [(("m", g, c), 0.5)]
            late = ("q2", g, c)
    return out + [(late, 1)]


def preparation1():
    out = []
    for h in range(H1):
        u = U1 * h
        out.append((u - U1 - 4, ("w", h)))
        start, step = u - U1 + PROJ1[0], (PROJ1[1] - PROJ1[0]) / NT
        for n in range(NT):
            if h == 0 and n == 0:
                out.append((start, ("gates",)))
            out += [(start + step * (n + j / 3), ("proj", h, n, j)) for j in range(3)]
        for c in range(NC):
            end = start + step * TPC * (c + 1)
            out += [(end + STAGE1[0], ("hi", h, c)), (end + STAGE1[1], ("lo", h, c))]
            out += [(end + STAGE1[2] + 0.3 * w, ("t", h, c, w)) for w in range(3)]
        for c in range(NC):
            end = u + M1 * c - MAX1
            start = end - M1 if c > 1 else u - MAX1 + 0.4 if c else u - U1 + PROJ1[1] + STAGE1[2] + 0.9
            items = [("max", h, TPC * c + i, b) for i in range(TPC) for b in range(NC)]
            out += [(start + (end - start) * k / len(items), item) for k, item in enumerate(items)]
            out += [(end, ("m", h, c)), (end + 1, ("q2", h, c))]
    return sorted(out, key=lambda p: p[0])


def paced(preparation, units):
    places = {("q2", 0, c): MAX0[c] for c in range(NC)}
    places |= {("q2", g, NC - 1): units * g + MAX0[-1] for g in range(1, NG)}
    at, knots, costs = 0.0, [(0.0, -30.0)], []
    for step, cost in preparation:
        if step in places:
            knots.append((at, places[step]))
        costs.append(at)
        at += cost
    return [(float(np.interp(a, *zip(*knots))), step) for a, (step, _) in zip(costs, preparation)]


def merge(preparation, units, foreground):
    seq, i = [], 0
    for u in range(2 * units):
        while i < len(preparation) and preparation[i][0] < u / 2:
            seq.append(preparation[i][1])
            i += 1
        seq += foreground(u // 2, u % 2)
    assert i == len(preparation)
    return seq


class Ring:

    def __init__(self, seq, by_dve, by_act):
        self.turn, self.read, self.by_act, self.order = {}, {}, by_act, []
        counts = {True: 0, False: 0}
        for step in seq:
            if step[0] in by_dve + by_act:
                a = step[0] in by_act
                counts[a] += 1
                self.turn[step], self.read[step] = len(self.order), counts[a]
                self.order.append(step)

    def bank(self, step):
        return RING[self.turn[step] % len(RING)]


def build(nc, A):
    ctx = ExitStack()
    with ctx:
        def sem(name):
            return ctx.enter_context(nc.semaphore(name))

        def sbuf(stack, name, shape, dt=F32):
            return stack.enter_context(nc.sbuf_tensor(name, shape, dt))

        ps = ctx.enter_context(nc.psum_tensor("ps", [P, 8, CH], F32))

        x = sbuf(ctx, "x", [P, NT, D])
        ident = sbuf(ctx, "ident", [P, P])
        eps = sbuf(ctx, "eps", [P, 2])
        stats = sbuf(ctx, "stats", [P, NT, 6])
        meanvar = sbuf(ctx, "meanvar", [P, NT, 2])
        std = sbuf(ctx, "std", [P, NT])
        rstd = sbuf(ctx, "rstd", [P, NT])
        power = sbuf(ctx, "power", [P, TPC])
        oT = sbuf(ctx, "oT", [P, 2, CH])

        fold = sbuf(ctx, "fold", [P, D1])
        ones = sbuf(ctx, "ones", [P, 1])
        wgate = sbuf(ctx, "wgate", [P, 2, H1 * E1])
        wout = sbuf(ctx, "wout", [P, 3, D])
        wlin = sbuf(ctx, "wlin", [P, 4, D])
        blin = sbuf(ctx, "blin", [P, 3, D])
        bqcol = sbuf(ctx, "bqcol", [P, 1])
        stdp = sbuf(ctx, "stdp", [P, 3, H0])
        blockm = sbuf(ctx, "blockm", [P, D])
        bd = sbuf(ctx, "bd", [P, 2, D])
        bsum = sbuf(ctx, "bsum", [P, H0])
        lden = sbuf(ctx, "lden", [P, 2, TPC, H0])

        l0 = ExitStack()
        s0 = lambda name, shape, dt=F32: sbuf(l0, name, shape, dt)
        identb = s0("identb", [P, P], BF16)
        masksb = s0("masksb", [P, 2, P], BF16)
        wqkv = s0("wqkv", [P, 3 * D])
        wproj = s0("wproj", [P, D])
        normw = s0("normw", [P, 2, D0])
        rope = s0("rope", [P, NT, 2, D0 // 2])
        mix = s0("mix", [P, P])
        bias0 = s0("bias0", [P, D])
        ms = s0("ms", [P, NT, 2 * H0])
        mxp = s0("mxp", [P, TPC, GH, NC])
        mx = s0("mx", [P, TPC, GH])
        rden = s0("rden", [P, TPC, GH])
        stageq = s0("stageq", [P, NT, GH, 32])
        stagek = s0("stagek", [P, NT, GH, 32])
        stagev = s0("stagev", [P, 2, NT, GH, 32])
        qT = s0("qT", [P, 2, T], F32R)
        early = ExitStack()
        se = lambda name, shape, dt=F32: sbuf(early, name, shape, dt)
        masks = se("masks", [P, 2, P])
        dft = se("dft", [P, 2, P])
        ndft = se("ndft", [P, P])
        wfreq = se("wfreq", [P, 2, P])
        ab = se("ab", [P, 2, P])
        early.close()
        pbuf0 = s0("pbuf0", [P, NP0, 2, CH])
        xn = s0("xn", [P, NT, D])
        xnT = s0("xnT", [P, T])
        linear = ExitStack()
        lt = sbuf(linear, "lt", [P, 2, 2, CH])
        aT = sbuf(linear, "aT", [P, T])
        a_n = sbuf(linear, "a_n", [P, NT, D])
        linear.close()
        qkv = s0("qkv", [P, NT, 3 * D])
        linear = ExitStack()
        qfT = sbuf(linear, "qfT", [P, T])
        kf = sbuf(linear, "kf", [P, NT, D])
        vf = sbuf(linear, "vf", [P, NT, D + 2])
        linear.close()
        kM0 = s0("kM0", [P, GH, T], F32R)
        rotating = ExitStack()
        tmp = sbuf(rotating, "tmp", [P, NT, 2 * H0, D0])
        rotating.close()
        kM1 = s0("kM1", [P, GH, T], F32R)
        kM = (kM0, kM1)
        l0.close()

        l1 = ExitStack()
        s1 = lambda name, shape, dt=F32: sbuf(l1, name, shape, dt)
        z = s1("z", [P, NT, E1, D1])
        xh = s1("xh", [P, T], F32R)
        xl = s1("xl", [P, T], F32R)
        gate = s1("gate", [P, NT, 2, H1, E1])
        maskd = s1("maskd", [P, NT, H1, E1])
        wraw = s1("wraw", [P, 3, E1 * D1])
        wh = s1("wh", [P, 3, E1 * D1], F32R)
        wl = s1("wl", [P, 3, E1 * D1], F32R)
        final = ExitStack()
        zT = sbuf(final, "zT", [P, 2, 3, P])
        final.close()
        gt = s1("gt", [P, 2, 3, E1, D1])
        gs = s1("gs", [P, 3, 2, D1])
        gsum = s1("gsum", [P, 3, D1])
        h_qk = s1("h_qk", [P, 2, NT, D1])
        h_v = s1("h_v", [P, 2, NT, D1])
        ranking = ExitStack()
        sr = lambda name, shape, dt=F32: sbuf(ranking, name, shape, dt)
        beats = sr("beats", [P, 2, NT, H1, E1 * (E1 - 1) // 2])
        rank = sr("rank", [P, 2, NT, H1, E1])
        sig = sr("sig", [P, 2, NT, H1, E1])
        ranking.close()
        pbuf1 = s1("pbuf1", [P, NP1, 2, CH])
        den = s1("den", [P, 2, 2, CH])
        on = s1("on", [P, TPC, D1])
        onm = s1("onm", [P, TPC, E1, D1])
        rd1 = s1("rd1", [P, TPC])
        mxp1 = s1("mxp1", [P, TPC, NC])
        mx1 = s1("mx1", [P, TPC])
        sk1 = s1("sk1", [P, TPC, P])
        sk2 = s1("sk2", [P, TPC, D1])
        sq1 = s1("sq1", [P, TPC, P])
        sq2 = s1("sq2", [P, TPC, P])
        k1T = s1("k1T", [P, 2, T], F32R)
        k2T = s1("k2T", [P, 2, T], F32R)
        q1T = s1("q1T", [P, 2, T], F32R)
        q2T = s1("q2T", [P, 2, T], F32R)
        l1.close()

        s_load = sem("s_load")
        s_load1 = sem("s_load1")
        s_w = sem("s_w")
        s_out = sem("s_out")
        s_const = sem("s_const")
        s_pconst = sem("s_pconst")
        s_dve = sem("s_dve")
        s_pool = sem("s_pool")
        s_mv = sem("s_mv")
        s_std = sem("s_std")
        s_rstd = sem("s_rstd")
        s_xn = sem("s_xn")
        s_tp = sem("s_tp")
        s_xnT = sem("s_xnT")
        s_qkv = sem("s_qkv")
        s_qkvev = sem("s_qkvev")
        s_ms = sem("s_ms")
        s_rms = sem("s_rms")
        s_roped = sem("s_roped")
        s_stagek = sem("s_stagek")
        s_stageq = sem("s_stageq")
        s_stagev = sem("s_stagev")
        s_turn0 = sem("s_turn0")
        s_read0d = sem("s_read0d")
        s_read0a = sem("s_read0a")
        s_turn1 = sem("s_turn1")
        s_read1d = sem("s_read1d")
        s_read1a = sem("s_read1a")
        s_m = sem("s_m")
        s_sc = sem("s_sc")
        s_exp = sem("s_exp")
        s_av = sem("s_av")
        s_oT = sem("s_oT")
        s_pj = sem("s_pj")
        s_res = sem("s_res")
        s_mixw = sem("s_mixw")
        s_mixc = sem("s_mixc")
        s_gaddv = sem("s_gaddv")
        s_xl = sem("s_xl")
        s_sig = sem("s_sig")
        s_rank = sem("s_rank")
        s_lin = sem("s_lin")
        s_lind = sem("s_lind")
        s_lina = sem("s_lina")
        s_lden = sem("s_lden")
        s_at = sem("s_at")
        s_aT = sem("s_aT")
        s_lq = sem("s_lq")
        s_g1 = sem("s_g1")
        s_g2 = sem("s_g2")
        s_wh = sem("s_wh")
        s_gadd = sem("s_gadd")
        s_hi1 = sem("s_hi1")
        s_st1 = sem("s_st1")
        s_m1 = sem("s_m1")
        s_sc1 = sem("s_sc1")
        s_exp1 = sem("s_exp1")
        s_av1 = sem("s_av1")
        s_den1 = sem("s_den1")
        s_den1p = sem("s_den1p")
        s_den1s = sem("s_den1s")
        s_oT1 = sem("s_oT1")
        s_z = sem("s_z")

        STEPS0 = [(c, jt) for c in range(NC) for jt in range(TPC * (c + 1))]
        N0 = len(STEPS0)
        LAST0 = [TPC * (c + 1) * (c + 2) // 2 for c in range(NC)]

        def foreground0(u, half):
            if half == 0:
                return [("S", u)] if u < 2 * N0 * NG else []
            seq = []
            k = u // 2 - 2
            if u % 2 == 0 and 0 <= k < N0 * NG:
                seq.append(("V", k))
                if k % N0 + 1 in LAST0:
                    seq.append(("O", k // N0, LAST0.index(k % N0 + 1)))
            k = u // 2 - 4
            if u % 2 and 0 <= k < N0 * NG and k % N0 + 1 in LAST0:
                seq.append(("F", k // N0, LAST0.index(k % N0 + 1)))
            return seq

        def foreground1(u, half):
            if half == 0:
                return [("S", u)] if u < U1 * H1 else []
            seq = []
            if 0 <= u - 2 < U1 * H1:
                seq += [("V", u - 2), ("D", u - 2)]
                if (u - 1) % M1 == 0:
                    seq.append(("O", (u - 1) // M1 - 1))
            if 0 <= u - 4 < U1 * H1 and (u - 3) % M1 == 0:
                seq.append(("F", (u - 3) // M1 - 1))
            return seq

        after0 = []
        for c in range(NC):
            u = 2 * (N0 * (NG - 1) + LAST0[c] + 3) + 1
            for i, kind in enumerate(("at", "pj", "sd", "ln", "lt", "mix", "sd2", "ln2", "lt2")):
                after0.append((u + 1.8 + 1.6 * i, (kind, c)))
            u += 1.8 + 1.6 * 9
            i = 3 * c
            for a, step in enumerate((("lin", i), ("lin", i + 1), ("ex", i), ("el", i), ("lin", i + 2), ("ex", i + 1),
                                      ("el", i + 1), ("ex", i + 2), ("el", i + 2))):
                after0.append((u + 0.8 * a, step))
        after1 = []
        for n in range(NT):
            u = U1 * (H1 - 1) + M1 * (n // TPC + 1) + 3
            after1 += [(u + 3 + n % TPC, ("zt", n)), (u + 4.5 + n % TPC, ("y", n))]
        by_place = lambda steps: sorted(steps, key=lambda p: p[0])
        SEQ0 = merge(by_place(paced(preparation0(), 2 * N0) + after0), 2 * N0 * NG + 36, foreground0)
        NORM = {step: i for i, step in enumerate(
            [s for s in SEQ0 if s[0] in ("sd", "sd2")] + [("sd3", c) for c in range(NC)])}
        assert [s for s in SEQ0 if s[0] in ("pj", "mix")] == [
            ({"sd": "pj", "sd2": "mix"}[s[0]], s[1]) for s in NORM if s[0] != "sd3"]
        SEQ1 = merge(by_place(preparation1() + after1), U1 * H1 + 16, foreground1)
        ring0 = Ring(SEQ0, ("max", "F", "pj", "mix", "lin"), ("k", "q", "q2", "at", "lt", "lt2"))
        ring1 = Ring(SEQ1, ("proj", "max", "F", "y"), ("t", "q2", "zt"))

        def wait_read(eng, ring, step):
            a, d = (s_read0a, s_read0d) if ring is ring0 else (s_read1a, s_read1d)
            eng.wait_ge(a if step[0] in ring.by_act else d, ring.read[step])

        def wait_turn(eng, ring, step):
            eng.wait_ge(s_turn0 if ring is ring0 else s_turn1, ring.turn[step] + 1)

        def diag(c, jt):
            return max(0, P * (jt - TPC * c))

        def wait_experts(eng, m):
            if m < NT and m % 2:
                eng.wait_ge(s_gaddv, (m + 1) // 2)
            else:
                eng.wait_ge(s_gadd, m // 2 + 1 if m < NT else m - NT // 2 + 1)

        PAIRS = {r: slice((r - 1) * (2 * E1 - r) // 2, r * (2 * E1 - r - 1) // 2) for r in range(1, E1)}

        def ranks(eng, order_after, a):
            rk = rank[:, a]
            for e in range(E1):
                ins = eng.memset(rk[:, :, :, e:e + 1], float(e))
            order_after(ins)
            for r in range(1, E1):
                lo, hi = slice(0, E1 - r), slice(r, E1)
                b = beats[:, a, :, :, PAIRS[r]]
                order_after(eng.tensor_tensor(rk[:, :, :, lo], rk[:, :, :, lo], b, ALU.add))
                ins = eng.tensor_tensor(rk[:, :, :, hi], rk[:, :, :, hi], b, ALU.subtract)
                if r < E1 - 1:
                    order_after(ins)
            return ins

        first, rest = slice(0, GH), slice(GH, H0)

        def heads(i, hs):
            n = hs.stop - hs.start
            hh = slice(H0 * i + hs.start, H0 * i + hs.stop)
            a = qkv[:, :, 0:2 * D].rearrange("p n (h d) -> p n h d", d=D0)[:, :, hh, :]
            w = normw[:, i, :].unsqueeze(1).unsqueeze(1).to_broadcast([P, NT, n, D0])
            cos, sin = (rope[:, :, r, :].unsqueeze(2).to_broadcast([P, NT, n, D0 // 2]) for r in range(2))
            return a, ms[:, :, hh], tmp[:, :, hh, :], w, cos, sin

        def norm_and_rotate(eng, order_after, hs):
            half = D0 // 2
            parts = [heads(i, hs) for i in range(2)]
            for a, m, t, w, cos, sin in parts:
                ins = eng.tensor_tensor(a, a, m.unsqueeze(3).to_broadcast(list(a.shape)), ALU.mult)
            order_after(ins)
            for a, m, t, w, cos, sin in parts:
                ins = eng.tensor_tensor(a, a, w, ALU.mult)
            order_after(ins)
            for a, m, t, w, cos, sin in parts:
                eng.tensor_tensor(t[:, :, :, 0:half], a[:, :, :, 0:half], sin, ALU.mult)
                ins = eng.tensor_tensor(t[:, :, :, half:D0], a[:, :, :, half:D0], sin, ALU.mult)
            order_after(ins)
            for a, m, t, w, cos, sin in parts:
                eng.tensor_tensor(a[:, :, :, 0:half], a[:, :, :, 0:half], cos, ALU.mult)
                ins = eng.tensor_tensor(a[:, :, :, half:D0], a[:, :, :, half:D0], cos, ALU.mult)
            order_after(ins)
            for a, m, t, w, cos, sin in parts:
                eng.tensor_tensor(a[:, :, :, 0:half], a[:, :, :, 0:half], t[:, :, :, half:D0], ALU.subtract)
                ins = eng.tensor_tensor(a[:, :, :, half:D0], a[:, :, :, half:D0], t[:, :, :, 0:half], ALU.add)
            return ins

        block = ctx.enter_context(nc.Block())

        @block.sync
        def _(sp):
            sp.dma_start(x[:], A["x"].rearrange("(n p) d -> p n d", p=P)).then_inc(s_load, 16)
            sp.dma_start(ident[:], A["ident"]).then_inc(s_load, 16)
            sp.dma_start(wqkv[:], A["wqkvT"]).then_inc(s_load, 16)
            sp.dma_start(normw[:, 0, :], A["qnw"].partition_broadcast(P)).then_inc(s_load, 16)
            sp.dma_start(normw[:, 1, :], A["knw"].partition_broadcast(P)).then_inc(s_load, 16)
            sp.dma_start(rope[:], A["rope"].rearrange("(n p) a f -> p n a f", p=P)).then_inc(s_load, 16)
            sp.dma_start(masks[:], A["masks"].rearrange("a p q -> p a q")).then_inc(s_load, 16)
            sp.dma_start(wproj[:], A["wprojT"]).then_inc(s_load, 16)
            sp.dma_start(dft[:], A["dft"].rearrange("a p q -> p a q")).then_inc(s_load, 16)
            sp.dma_start(wfreq[:, 0, :], A["wre"]).then_inc(s_load, 16)
            sp.dma_start(wfreq[:, 1, :], A["wim"]).then_inc(s_load, 16)
            sp.dma_start(bias0[:], A["bias0"].partition_broadcast(P)).then_inc(s_load, 16)
            for i, name in enumerate(["lWq", "lWk", "lWv", "lWo"]):
                sp.dma_start(wlin[:, i, :], A[name]).then_inc(s_load1, 16)
            for i, name in enumerate(["lbk", "lbv", "lbo"]):
                sp.dma_start(blin[:, i, :], A[name].partition_broadcast(P)).then_inc(s_load1, 16)
            sp.dma_start(bqcol[:], A["lbq"].rearrange("(p a) -> p a", a=1)).then_inc(s_load1, 16)
            sp.dma_start(stdp[:, 0, :], A["stdp"].partition_broadcast(P)).then_inc(s_load1, 16)
            sp.dma_start(blockm[:], A["blockm"]).then_inc(s_load1, 16)
            sp.dma_start(wgate[:, 0, :], A["Ws"]).then_inc(s_load1, 16)
            sp.dma_start(wgate[:, 1, :], A["Wd"]).then_inc(s_load1, 16)
            for i in range(3):
                r = min(P, E1 * D1 - P * i)
                sp.dma_start(wout[0:r, i, :], A["Wo"][P * i:P * i + r, :]).then_inc(s_load1, 16)
            sp.dma_start(fold[:], A["fold"]).then_inc(s_load1, 16)
            sp.wait_ge(s_res, NC)
            for h in range(H1):
                if h:
                    sp.wait_ge(s_wh, h)
                c0 = h * E1 * D1
                sp.dma_start(wraw[:, 0, :], A["Wq"][:, c0:c0 + E1 * D1]).then_inc(s_w, 16)
                for i in range(2):
                    c1 = i * H1 * E1 * D1 + c0
                    sp.dma_start(wraw[:, 1 + i, :], A["Wkv"][:, c1:c1 + E1 * D1]).then_inc(s_w, 16)
            out_v = A["out"].rearrange("(n p) d -> p n d", p=P)
            for c in range(NC):
                wait_read(sp, ring1, ("y", TPC * (c + 1) - 1))
                sp.dma_start(out_v[:, TPC * c:TPC * (c + 1), :], x[:, TPC * c:TPC * (c + 1), :]).then_inc(s_out, 16)
            sp.wait_ge(s_out, 16 * NC)

        @block.tensor
        def _(pe):
            def transpose_tiles(src, ready, count):
                for c in range(NC):
                    pe.wait_ge(ready, count(c))
                    for i in range(TPC):
                        n = TPC * c + i
                        mm = pe.transpose(ps[:, c, P * i:P * (i + 1)], src[:, n, :], ident[:])
                    mm.then_inc(s_tp, 1)

            pe.wait_ge(s_load, 16 * 12)
            transpose_tiles(xn, s_xn, lambda c: c + 1)
            for n in range(NT):
                pe.wait_ge(s_xnT, n // TPC + 1)
                if n >= 4:
                    pe.wait_ge(s_qkvev, n - 3)
                pe.matmul(ps[:, 4 + n % 4, 0:3 * D], xnT[:, P * n:P * (n + 1)], wqkv[:],
                          start=True, stop=True).then_inc(s_qkv, 1)
            pe.wait_ge(s_qkvev, NT)

            pe.wait_ge(s_const, 1)
            pe.matmul(ps[:, 0, 0:P], wfreq[:, 0, :], dft[:, 0, :], start=True, stop=False)
            pe.matmul(ps[:, 0, 0:P], wfreq[:, 1, :], dft[:, 1, :], start=False, stop=True)
            pe.matmul(ps[:, 1, 0:P], wfreq[:, 1, :], dft[:, 0, :], start=True, stop=False)
            pe.matmul(ps[:, 1, 0:P], wfreq[:, 0, :], ndft[:], start=False, stop=True).then_inc(s_mixw, 1)
            pe.wait_ge(s_mixc, 1)
            pe.matmul(ps[:, 2, 0:P], ab[:, 0, :], dft[:, 0, :], start=True, stop=False)
            pe.matmul(ps[:, 2, 0:P], ab[:, 1, :], ndft[:], start=False, stop=True).then_inc(s_mixw, 1)
            pe.wait_ge(s_mixc, 2)

            def take(ring, step):
                turn = ring.turn[step]
                if turn >= len(RING):
                    wait_read(pe, ring, ring.order[turn - len(RING)])
                return ring.bank(step)

            def chunk_transposes(ring, step, src, rows=P):
                b = take(ring, step)
                for i in range(TPC):
                    mm = pe.transpose(ps[0:rows, b, P * i:P * (i + 1)], src(i), ident[:])
                return mm

            for step in SEQ0:
                kind = step[0]
                if kind == "k":
                    _, g, c = step
                    pe.wait_ge(s_stagek, g + 1)
                    chunk_transposes(ring0, step, lambda i: stagek[:, TPC * c + i, :, :].rearrange(
                        "p h r -> p (h r)")).then_inc(s_turn0, 1)
                elif kind in ("q", "q2"):
                    _, g, c = step
                    pe.wait_ge(s_stageq, g + 1)
                    if kind == "q2":
                        pe.wait_ge(s_m, NC * g + c + 1)
                    chunk_transposes(ring0, step, lambda i: stageq[:, TPC * c + i, :, :].rearrange(
                        "p h r -> p (h r)")).then_inc(s_turn0, 1)
                elif kind == "max":
                    _, g, c, i, b, h, n = step
                    bank = take(ring0, step)
                    wait_read(pe, ring0, ("q", g, c))
                    wait_read(pe, ring0, ("k", g, b))
                    w = P * (i + 1) if b == c else CH
                    for a in range(n):
                        it = TPC * c + i
                        mm = pe.matmul(ps[:, bank, w * a:w * (a + 1)], qT[:, g % 2, P * it:P * (it + 1)],
                                       kM[g % 2][:, h + a, CH * b:CH * b + w], start=True, stop=b < c)
                        if b == c:
                            mm = pe.matmul(ps[:, bank, w * (a + 1) - P:w * (a + 1)], identb[:], masksb[:, 0, :],
                                           start=False, stop=True)
                    mm.then_inc(s_turn0, 1)
                elif kind == "S":
                    u = step[1]
                    g, (c, jt) = u // (2 * N0), STEPS0[u // 2 % N0]
                    off = diag(c, jt)
                    if u >= NS:
                        pe.wait_ge(s_exp, u - NS + 1)
                    wait_read(pe, ring0, ("q2", g, c))
                    wait_read(pe, ring0, ("k", g, c))
                    for i in range(2):
                        h = 2 * (u % 2) + i
                        b = 2 * (u % NS) + i
                        mm = pe.matmul(ps[:, b, off:CH], kM[g % 2][:, h, P * jt:P * (jt + 1)],
                                       qT[:, g % 2, CH * c + off:CH * (c + 1)], start=True, stop=jt < TPC * c)
                        if jt >= TPC * c:
                            mm = pe.matmul(ps[:, b, off:off + P], identb[:], masksb[:, 1, :], start=False, stop=True)
                    mm.then_inc(s_sc, 1)
                elif kind == "V":
                    k = step[1]
                    g, (c, jt) = k // N0, STEPS0[k % N0]
                    off = diag(c, jt)
                    pe.wait_ge(s_stagev, g + 1)
                    pe.wait_ge(s_exp, 2 * k + 2)
                    if jt == 0 and g * NC + c:
                        pe.wait_ge(s_oT, g * NC + c)
                    for h in range(GH):
                        u = 2 * k + h // 2
                        mm = pe.matmul(ps[32 * h:32 * h + 32, ACC, off:CH], stagev[:, g % 2, jt, h, :],
                                       pbuf0[:, u % NP0, h % 2, off:CH], start=jt == 0, stop=jt == TPC * (c + 1) - 1,
                                       tile_position=(0, 32 * h))
                    mm.then_inc(s_av, 1)
                elif kind == "F":
                    _, g, c = step
                    m = g * NC + c
                    pe.wait_ge(s_oT, m + 1)
                    chunk_transposes(ring0, step,
                                     lambda i: oT[:, m % 2, P * i:P * (i + 1)]).then_inc(s_turn0, 1)
                elif kind in ("at", "lt", "lt2"):
                    c = step[1]
                    if kind == "at":
                        wait_read(pe, ring0, ("F", NG - 1, c))
                    else:
                        pe.wait_ge(s_xn, NC + NORM["sd" if kind == "lt" else "sd2", c] + 1)
                    chunk_transposes(ring0, step, lambda i: xn[:, TPC * c + i, :]).then_inc(s_turn0, 1)
                elif kind == "lin":
                    i = step[1]
                    b = take(ring0, step)
                    wait_read(pe, ring0, ("lt2", i // 3))
                    pe.wait_ge(s_load1, 16 * 16)
                    if i % 3 == 0:
                        mm = pe.matmul(ps[:, b, :], wlin[:, 0, :], xnT[:, CH * (i // 3):CH * (i // 3 + 1)],
                                       start=True, stop=True)
                    else:
                        for a in range(2):
                            n = TPC * (i // 3) + 2 * (i % 3 - 1) + a
                            mm = pe.matmul(ps[:, b, 2 * D * a:2 * D * (a + 1)], xnT[:, P * n:P * (n + 1)],
                                           wlin[:, 1:3, :].rearrange("p a d -> p (a d)"), start=True, stop=True)
                    mm.then_inc(s_turn0, 1)
                elif kind in ("pj", "mix"):
                    c = step[1]
                    b = take(ring0, step)
                    wait_read(pe, ring0, ("at" if kind == "pj" else "lt", c))
                    for i in range(TPC):
                        n = TPC * c + i
                        mm = pe.matmul(ps[:, b, P * i:P * (i + 1)], xnT[:, P * n:P * (n + 1)],
                                       (wproj if kind == "pj" else mix)[:], start=True, stop=True)
                    mm.then_inc(s_turn0, 1)
            items = 3 * NC
            pe.wait_ge(s_lind, items)
            for n in range(NT):
                mm = pe.matmul(ps[:, 4, 0:D + 2], kf[:, n, :], vf[:, n, :], start=n == 0, stop=n == NT - 1)
            mm.then_inc(s_lin, 1)
            pe.wait_ge(s_lind, items + 1)

            def numerators(c):
                if c >= 1:
                    pe.wait_ge(s_lden, c)
                for i in range(TPC):
                    n = TPC * c + i
                    pe.matmul(ps[:, c, P * i:P * (i + 1)], qfT[:, P * n:P * (n + 1)], bd[:, 0, :],
                              start=True, stop=True)
                    mm = pe.matmul(ps[:, 5, H0 * i:H0 * (i + 1)], qfT[:, P * n:P * (n + 1)], bsum[:],
                                   start=True, stop=True)
                mm.then_inc(s_lin, 1)

            def output(c):
                pe.wait_ge(s_lind, items + 2 + c)
                for i in range(TPC):
                    mm = pe.transpose(ps[:, c, P * i:P * (i + 1)], a_n[:, TPC * c + i, :], ident[:])
                mm.then_inc(s_at, 1)
                pe.wait_ge(s_aT, c + 1)
                if c >= 2:
                    pe.wait_ge(s_res, NC + c - 1)
                for i in range(TPC):
                    n = TPC * c + i
                    mm = pe.matmul(ps[:, 6 + c % 2, P * i:P * (i + 1)], aT[:, P * n:P * (n + 1)], wlin[:, 3, :],
                                   start=True, stop=True)
                mm.then_inc(s_pj, 1)

            def transposes3(c):
                pe.wait_ge(s_xn, NC + NORM["sd3", c] + 1)
                for i in range(TPC):
                    mm = pe.transpose(ps[:, c, P * i:P * (i + 1)], xn[:, TPC * c + i, :], ident[:])
                mm.then_inc(s_tp, 1)

            def logits(c):
                pe.wait_ge(s_xnT, NC + c + 1)
                for i in range(TPC):
                    n = TPC * c + i
                    mm = pe.matmul(ps[:, 4 + c, 80 * i:80 * (i + 1)], xnT[:, P * n:P * (n + 1)],
                                   wgate[:, :, :].rearrange("p a f -> p (a f)"), start=True, stop=True)
                mm.then_inc(s_g1, 1)

            for c in range(NC + 1):
                if c < NC:
                    numerators(c)
                if c:
                    output(c - 1)
                if c >= 3:
                    transposes3(c - 3)
            transposes3(2)
            logits(0)
            transposes3(3)
            for c in range(1, NC):
                logits(c)
            pe.wait_ge(s_g2, NC)
            for step in SEQ1:
                kind = step[0]
                if kind == "proj":
                    _, h, n, j = step
                    bank = take(ring1, step)
                    pe.wait_ge(s_wh, h + 1)
                    pe.wait_ge(s_xl, n // TPC + 1)
                    o, t = ps[:, bank, 0:E1 * D1], slice(P * n, P * (n + 1))
                    pe.matmul(o, xh[:, t], wh[:, j, :], start=True, stop=False)
                    pe.matmul(o, xh[:, t], wl[:, j, :], start=False, stop=False)
                    pe.matmul(o, xl[:, t], wh[:, j, :], start=False, stop=True).then_inc(s_turn1, 1)
                elif kind == "t":
                    _, h, c, w = step
                    pe.wait_ge(s_st1, NC * h + c + 1)
                    src = (sk1, sk2, sq1)[w]
                    chunk_transposes(ring1, step, lambda i: src[:, i, :], D1 if w == 1 else P).then_inc(s_turn1, 1)
                elif kind == "max":
                    _, h, it, b = step
                    bank = take(ring1, step)
                    wait_read(pe, ring1, ("t", h, NC - 1, 2))
                    pe.matmul(ps[:, bank, :], q1T[:, h % 2, P * it:P * (it + 1)],
                              k1T[:, h % 2, CH * b:CH * (b + 1)], start=True, stop=True).then_inc(s_turn1, 1)
                elif kind == "q2":
                    _, h, c = step
                    pe.wait_ge(s_m1, NC * h + c + 1)
                    chunk_transposes(ring1, step, lambda i: sq2[:, i, 0:D1 + 1], D1 + 1).then_inc(s_turn1, 1)
                elif kind == "S":
                    u = step[1]
                    h, c, m = u // U1, u % U1 // M1, u % M1
                    if u >= NS:
                        pe.wait_ge(s_exp1, u - NS + 1)
                    wait_read(pe, ring1, ("q2", h, c))
                    for i in range(2):
                        b = 2 * (u % NS) + i
                        t = slice(P * (2 * m + i), P * (2 * m + i + 1))
                        q = slice(CH * c, CH * (c + 1))
                        pe.matmul(ps[:, b, :], k1T[:, h % 2, t], q1T[:, h % 2, q], start=True, stop=False)
                        mm = pe.matmul(ps[:, b, :], k2T[0:D1 + 1, h % 2, t], q2T[0:D1 + 1, h % 2, q],
                                       start=False, stop=True)
                    mm.then_inc(s_sc1, 1)
                elif kind == "V":
                    u = step[1]
                    h, c, m = u // U1, u % U1 // M1, u % M1
                    pe.wait_ge(s_exp1, u + 1)
                    if m == 0 and h * NC + c:
                        pe.wait_ge(s_oT1, h * NC + c)
                    for i in range(2):
                        mm = pe.matmul(ps[64 * i:64 * i + 64, ACC, :], h_v[:, h % 2, 2 * m + i, :],
                                       pbuf1[:, u % NP1, i, :], start=m == 0, stop=m == M1 - 1,
                                       tile_position=(0, 64 * i))
                    mm.then_inc(s_av1, 1)
                elif kind == "F":
                    m = step[1]
                    bank = take(ring1, step)
                    pe.wait_ge(s_oT1, m + 1)
                    pe.wait_ge(s_den1s, m + 1)
                    for i in range(TPC):
                        t = slice(P * i, P * (i + 1))
                        pe.matmul(ps[:, bank, D1 * i:D1 * (i + 1)], oT[:, m % 2, t], fold[:],
                                  start=i == 0, stop=True, skip_group_check=True)
                    for i in range(TPC):
                        t = slice(P * i, P * (i + 1))
                        o = ps[:, bank, TPC * D1 + i:TPC * D1 + i + 1]
                        mm = pe.matmul(o, den[:, m % 2, 0, t], ones[:], start=False, stop=True, skip_group_check=True)
                    mm.then_inc(s_turn1, 1)
                elif kind == "zt":
                    n = step[1]
                    bank = take(ring1, step)
                    pe.wait_ge(s_z, 2 * (NC * (H1 - 1) + n // TPC + 1))
                    for i in range(3):
                        r = min(P, E1 * D1 - P * i)
                        mm = pe.transpose(ps[0:r, bank, P * i:P * (i + 1)],
                                          z[:, n, :, :].rearrange("p e d -> p (e d)")[:, P * i:P * i + r], ident[:])
                    mm.then_inc(s_turn1, 1)
                elif kind == "y":
                    n = step[1]
                    bank = take(ring1, step)
                    wait_read(pe, ring1, ("zt", n))
                    for i in range(3):
                        r = min(P, E1 * D1 - P * i)
                        mm = pe.matmul(ps[:, bank, 0:D], zT[0:r, n % 2, i, :], wout[0:r, i, :],
                                       start=i == 0, stop=i == 2)
                    mm.then_inc(s_turn1, 1)


        @block.scalar
        def _(act):
            msg = ms[:].rearrange("p n (a h) -> p n a h", a=2)

            act.wait_ge(s_mv, 1)
            nc.scalar.activation(std[:], meanvar[:, :, 1], ACT.Sqrt, bias=eps[:, 0:1]).then_inc(s_std, 1)
            for c in range(NC):
                act.wait_ge(s_tp, c + 1)
                nc.scalar.activation(xnT[:, CH * c:CH * (c + 1)], ps[:, c, :], ACT.Copy).then_inc(s_xnT, 1)
            for n in range(NT):
                act.wait_ge(s_qkv, n + 1)
                nc.scalar.activation(qkv[:, n, :], ps[:, 4 + n % 4, 0:3 * D], ACT.Copy).then_inc(s_qkvev, 1)
            act.wait_ge(s_ms, 1)
            nc.scalar.activation(msg[:, :, :, 0:GH], msg[:, :, :, 0:GH], ACT.Sqrt, bias=eps[:, 1:2],
                                 scale=1.0 / D0).then_inc(s_rms, 1)
            act.wait_ge(s_mixw, 1)
            nc.scalar.activation(ab[:], ps[:, 0:2, 0:P], ACT.Copy).then_inc(s_mixc, 1)
            act.wait_ge(s_mixw, 2)
            nc.scalar.activation(mix[:], ps[:, 2, 0:P], ACT.Copy, scale=1.0 / D).then_inc(s_mixc, 1)

            act.wait_ge(s_load1, 16 * 16)
            nc.scalar.activation(stdp[:, 1, :], stdp[:, 0, :], ACT.Exp, scale=-1.0).then_inc(s_lina, 1)
            act.wait_ge(s_pconst, 1)
            for step in SEQ0:
                kind = step[0]
                if kind in ("k", "q", "q2"):
                    _, g, c = step
                    wait_turn(act, ring0, step)
                    if g >= 2:
                        act.wait_ge(s_sc, 2 * N0 * (g - 1))
                    b = ring0.bank(step)
                    if kind == "k":
                        if g == 1:
                            act.wait_ge(s_pconst, 2)
                        for h in range(GH):
                            rows = slice(32 * h, 32 * h + 32)
                            ins = nc.scalar.activation(kM[g % 2][rows, h, CH * c:CH * (c + 1)], ps[rows, b, :],
                                                       ACT.Copy)
                        ins.then_inc(s_read0a, 1)
                    else:
                        nc.scalar.activation(qT[:, g % 2, CH * c:CH * (c + 1)], ps[:, b, :],
                                             ACT.Copy).then_inc(s_read0a, 1)
                elif kind == "S":
                    u = step[1]
                    off = diag(*STEPS0[u // 2 % N0])
                    act.wait_ge(s_sc, u + 1)
                    if u >= NP0:
                        act.wait_ge(s_av, (u - NP0) // 2 + 1)
                    b = 2 * (u % NS)
                    nc.scalar.activation(pbuf0[:, u % NP0, :, off:CH], ps[:, b:b + 2, off:CH], ACT.Exp,
                                         scale=float(D0) ** -0.5).then_inc(s_exp, 1)
                elif kind == "O":
                    _, g, c = step
                    m = g * NC + c
                    act.wait_ge(s_av, N0 * g + LAST0[c])
                    if m >= 2:
                        wait_turn(act, ring0, ("F", (m - 2) // NC, (m - 2) % NC))
                    nc.scalar.activation(oT[:, m % 2, :], ps[:, ACC, :], ACT.Copy).then_inc(s_oT, 1)
                elif step == ("rest", 0):
                    act.wait_ge(s_ms, 2)
                    nc.scalar.activation(msg[:, :, :, GH:], msg[:, :, :, GH:], ACT.Sqrt, bias=eps[:, 1:2],
                                         scale=1.0 / D0).then_inc(s_rms, 1)
                elif kind in ("at", "lt", "lt2"):
                    c = step[1]
                    wait_turn(act, ring0, step)
                    nc.scalar.activation(xnT[:, CH * c:CH * (c + 1)], ps[:, ring0.bank(step), :],
                                         ACT.Copy).then_inc(s_read0a, 1)
                elif kind == "ex":
                    i = step[1]
                    if i % 3 == 0:
                        wait_read(act, ring0, ("lin", i))
                    else:
                        act.wait_ge(s_lq, i - i // 3)
                    w = 2 * D if i % 3 else CH
                    nc.scalar.activation(lt[:, i % 2, 0, 0:w], lt[:, i % 2, 0, 0:w], ACT.Exp).then_inc(s_lina, 1)
            def tokens(c):
                act.wait_ge(s_tp, NC + c + 1)
                q = slice(CH * c, CH * (c + 1))
                nc.scalar.activation(xh[:, q], ps[:, c, :], ACT.Copy)
                nc.scalar.activation(xnT[:, q], ps[:, c, :], ACT.Copy).then_inc(s_xnT, 1)

            for c in range(NC + 1):
                if c < NC:
                    act.wait_ge(s_at, c + 1)
                    nc.scalar.activation(aT[:, CH * c:CH * (c + 1)], ps[:, c, :], ACT.Copy).then_inc(s_aT, 1)
                if c >= 3:
                    tokens(c - 3)
            tokens(2)
            tokens(3)
            act.wait_ge(s_xl, NC)
            for c in range(NC):
                act.wait_ge(s_g1, c + 1)
                nc.scalar.activation(sig[:, :, TPC * c:TPC * (c + 1)].rearrange("p a n h e -> p a n (h e)"),
                                     ps[:, 4 + c, 0:80 * TPC].rearrange("p (n a f) -> p a n f", n=TPC, a=2), ACT.Exp,
                                     scale=-1.0).then_inc(s_g2, 1)
            for step in SEQ1:
                kind = step[0]
                if kind == "hi":
                    _, h, c = step
                    tiles = slice(TPC * c, TPC * (c + 1))
                    wait_experts(act, NT * h + TPC * (c + 1) - 1)
                    if h == 0:
                        wait_experts(act, TPC * (c + 1) - 2)
                    if h or c:
                        wait_turn(act, ring1, ("t", h, c - 1, 2) if c else ("t", h - 1, NC - 1, 2))
                    nc.scalar.activation(sk1[:].rearrange("p n (a d) -> p n a d", a=2).bitcast(F32R),
                                         h_qk[:, 1, tiles, :].unsqueeze(2).to_broadcast([P, TPC, 2, D1]), ACT.Copy)
                    nc.scalar.activation(sq1[:, :, 0:D1].bitcast(F32R), h_qk[:, 0, tiles, :],
                                         ACT.Copy).then_inc(s_hi1, 1)
                elif kind == "t":
                    _, h, c, w = step
                    wait_turn(act, ring1, step)
                    if h >= 2:
                        act.wait_ge(s_sc1, U1 * (h - 1))
                    rows, q = slice(0, D1 if w == 1 else P), slice(CH * c, CH * (c + 1))
                    if w == 2:
                        nc.scalar.activation(q2T[0:D1, h % 2, q], ps[0:D1, ring1.bank(step), :], ACT.Copy)
                    nc.scalar.activation((k1T, k2T, q1T)[w][rows, h % 2, q],
                                         ps[rows, ring1.bank(step), :], ACT.Copy).then_inc(s_read1a, 1)
                elif kind == "q2":
                    _, h, c = step
                    wait_turn(act, ring1, step)
                    nc.scalar.activation(q2T[D1:D1 + 1, h % 2, CH * c:CH * (c + 1)],
                                         ps[D1:D1 + 1, ring1.bank(step), :], ACT.Copy).then_inc(s_read1a, 1)
                elif kind == "S":
                    u = step[1]
                    act.wait_ge(s_sc1, u + 1)
                    if u >= NP1:
                        act.wait_ge(s_av1, u - NP1 + 1)
                        act.wait_ge(s_den1, u - NP1 + 1)
                        act.wait_ge(s_den1p, u - NP1 + 1)
                    b = 2 * (u % NS)
                    nc.scalar.activation(pbuf1[:, u % NP1, :, :], ps[:, b:b + 2, :], ACT.Exp,
                                         scale=float(D1) ** -0.5).then_inc(s_exp1, 1)
                elif kind == "O":
                    m = step[1]
                    act.wait_ge(s_av1, M1 * (m + 1))
                    if m >= 2:
                        wait_turn(act, ring1, ("F", m - 2))
                    nc.scalar.activation(oT[:, m % 2, :], ps[:, ACC, :], ACT.Copy).then_inc(s_oT1, 1)
                elif kind == "zt":
                    n = step[1]
                    b = ring1.bank(step)
                    wait_turn(act, ring1, step)
                    if n >= 2:
                        wait_turn(act, ring1, ("y", n - 2))
                    nc.scalar.activation(zT[:, n % 2, 0:2, :].rearrange("p a t -> p (a t)"), ps[:, b, 0:2 * P],
                                         ACT.Copy)
                    nc.scalar.activation(zT[0:64, n % 2, 2, :], ps[0:64, b, 2 * P:3 * P], ACT.Copy).then_inc(s_read1a, 1)

        @block.vector
        def _(dve):
            v = nc.vector
            order = [0]

            def link(ins):
                order[0] += 1
                ins.then_inc(s_dve, 1)
                dve.wait_ge(s_dve, order[0])

            def statistics(first, count):
                for n in range(first, first + count):
                    ins = v.bn_stats(stats[:, n, :], x[:, n, :])
                link(ins)
                for n in range(first, first + count):
                    ins = v.bn_aggr(meanvar[:, n, :], stats[:, n, :])
                ins.then_inc(s_mv, 1)

            def norm(first, count):
                for n in range(first, first + count):
                    ins = v.tensor_scalar(xn[:, n, :], x[:, n, :], meanvar[:, n, 0:1], rstd[:, n:n + 1],
                                          ALU.subtract, ALU.mult)
                    if n % TPC == TPC - 1:
                        ins.then_inc(s_xn, 1)

            v.memset(eps[:, 0:1], LN_EPS)
            v.memset(eps[:, 1:2], RMS_EPS)
            v.memset(ones[:], 1.0)
            dve.wait_ge(s_load, 16 * 12)
            statistics(0, NT)
            dve.wait_ge(s_std, 1)
            link(v.reciprocal(rstd[:], std[:]))
            norm(0, NT)
            v.tensor_copy(identb[:], ident[:])
            v.tensor_copy(masksb[:], masks[:])
            v.tensor_scalar(ndft[:], dft[:, 1, :], -1.0, None, ALU.mult).then_inc(s_const, 1)

            dve.wait_ge(s_qkvev, NT)
            def squares(hs):
                for i in range(2):
                    a, _, t, _, _, _ = heads(i, hs)
                    ins = v.tensor_tensor(t, a, a, ALU.mult)
                link(ins)
                for i in range(2):
                    _, m, t, _, _, _ = heads(i, hs)
                    ins = v.tensor_reduce(m, t, AX.X, ALU.add)
                ins.then_inc(s_ms, 1)

            squares(first)
            dve.wait_ge(s_rms, 1)
            for i in range(2):
                m = heads(i, first)[1]
                ins = v.reciprocal(m, m)
            link(ins)
            link(norm_and_rotate(v, link, first))
            dve.wait_ge(s_pconst, 1)

            for step in SEQ0:
                kind = step[0]
                if kind == "stagek":
                    g = step[1]
                    if g:
                        dve.wait_ge(s_roped, 1)
                        wait_turn(dve, ring0, ("k", g - 1, NC - 1))
                    gk = qkv[:, :, D + 32 * g:D + 32 * (g + 1)].rearrange("p n (h d) -> p n h d", d=D0)
                    v.tensor_copy(stagek[:, :, :, D0:2 * D0].bitcast(F32R), gk)
                    link(v.tensor_copy(stagek[:, :, :, 0:D0].bitcast(F32R), gk))
                    v.tensor_tensor(stagek[:, :, :, 2 * D0:3 * D0], gk, stagek[:, :, :, 0:D0],
                                    ALU.subtract).then_inc(s_stagek, 1)
                elif step == ("rest", 0):
                    squares(rest)
                elif step == ("rest", 1):
                    dve.wait_ge(s_rms, 2)
                    for i in range(2):
                        m = heads(i, rest)[1]
                        ins = v.reciprocal(m, m)
                    ins.then_inc(s_ms, 1)
                elif kind == "stageq":
                    g = step[1]
                    if g:
                        wait_turn(dve, ring0, ("q2", g - 1, NC - 1))
                    gq = qkv[:, :, 32 * g:32 * (g + 1)].rearrange("p n (h d) -> p n h d", d=D0)
                    v.tensor_copy(stageq[:, :, :, 2 * D0:3 * D0].bitcast(F32R), gq)
                    v.tensor_copy(stageq[:, :, :, 0:D0].bitcast(F32R), gq)
                    link(v.memset(stageq[:, :, :, 24:25], 0.0))
                    v.tensor_tensor(stageq[:, :, :, D0:2 * D0], gq, stageq[:, :, :, 0:D0],
                                    ALU.subtract).then_inc(s_stageq, 1)
                elif kind == "max":
                    _, g, c, i, b, h, n = step
                    wait_turn(dve, ring0, step)
                    w = P * (i + 1) if b == c else CH
                    v.tensor_reduce(mxp[:, i, h:h + n, b],
                                    ps[:, ring0.bank(step), 0:w * n].rearrange("p (h k) -> p h k", h=n),
                                    AX.X, ALU.max).then_inc(s_read0d, 1)
                    last = step
                elif kind == "m":
                    _, g, c = step
                    wait_read(dve, ring0, last)
                    if g or c:
                        dve.wait_ge(s_m, NC * g + c)
                    link(v.tensor_reduce(mx[:], mxp[:, :, :, 0:c + 1], AX.X, ALU.max))
                    v.tensor_scalar(stageq[:, TPC * c:TPC * (c + 1), :, 24:25].bitcast(F32R), mx[:].unsqueeze(3),
                                    -1.0, None, ALU.mult).then_inc(s_m, 1)
                elif kind == "F":
                    _, g, c = step
                    wait_turn(dve, ring0, step)
                    if g or c:
                        wait_read(dve, ring0, ("F", g, c - 1) if c else ("F", g - 1, NC - 1))
                    o = ps[:, ring0.bank(step), :].rearrange("p (n h r) -> p n h r", n=TPC, h=GH)
                    link(v.reciprocal(rden[:].unsqueeze(3), o[:, :, :, D0:D0 + 1]))
                    dst = xn[:, TPC * c:TPC * (c + 1), 32 * g:32 * (g + 1)].rearrange("p n (h d) -> p n h d", d=D0)
                    v.tensor_tensor(dst, o[:, :, :, 0:D0], rden[:].unsqueeze(3).to_broadcast([P, TPC, GH, D0]),
                                    ALU.mult).then_inc(s_read0d, 1)
                elif kind in ("pj", "mix"):
                    c = step[1]
                    xc = x[:, TPC * c:TPC * (c + 1), :]
                    wait_turn(dve, ring0, step)
                    v.tensor_tensor(xc, ps[:, ring0.bank(step), :].rearrange("p (n d) -> p n d", n=TPC), xc,
                                    ALU.add).then_inc(s_read0d, 1)
                    wait_read(dve, ring0, step)
                    if kind == "mix":
                        v.tensor_tensor(xc, xc, bias0[:].unsqueeze(1).to_broadcast([P, TPC, D]),
                                        ALU.add).then_inc(s_res, 1)
                        dve.wait_ge(s_res, c + 1)
                    statistics(TPC * c, TPC)
                elif kind in ("ln", "ln2"):
                    c = step[1]
                    wait_read(dve, ring0, ("at" if kind == "ln" else "lt", c))
                    dve.wait_ge(s_rstd, NORM["sd" + kind[2:], c] + 1)
                    norm(TPC * c, TPC)
                elif kind == "lin":
                    i = step[1]
                    wait_turn(dve, ring0, step)
                    if i == 0:
                        dve.wait_ge(s_stagev, NG)
                        dve.wait_ge(s_sc, 2 * N0 * (NG - 1))
                        dve.wait_ge(s_load1, 16 * 16)
                        v.memset(vf[:, :, D:D + 1], 1.0)
                        v.memset(vf[:, :, D + 1:D + 2], 0.0)
                    if i >= 2:
                        dve.wait_ge(s_lind, i - 1)
                    b = ring0.bank(step)
                    if i % 3 == 0:
                        v.tensor_scalar(lt[:, i % 2, 0, :], ps[:, b, :], bqcol[:, 0:1], 0.0, ALU.add, ALU.min)
                        v.tensor_scalar(lt[:, i % 2, 1, :], ps[:, b, :], bqcol[:, 0:1], 0.0, ALU.add,
                                        ALU.max).then_inc(s_read0d, 1)
                        continue
                    n = TPC * (i // 3) + 2 * (i % 3 - 1)
                    kv = ps[:, b, :].rearrange("p (n a d) -> p n a d", n=2, a=2)
                    z0, z1 = (lt[:, i % 2, a, 0:2 * D].rearrange("p (n d) -> p n d", n=2) for a in range(2))
                    bk, bv = (blin[:, a, :].unsqueeze(1).to_broadcast([P, 2, D]) for a in range(2))
                    v.tensor_tensor(z1, kv[:, :, 0, :], bk, ALU.add)
                    v.tensor_tensor(vf[:, n:n + 2, 0:D], kv[:, :, 1, :], bv, ALU.add).then_inc(s_read0d, 1)
                    wait_read(dve, ring0, step)
                    link(v.tensor_scalar(z0, z1, 0.0, None, ALU.min))
                    v.tensor_scalar(z1, z1, 0.0, None, ALU.max).then_inc(s_lq, 1)
                elif kind == "el":
                    i = step[1]
                    dve.wait_ge(s_lina, i + 2)
                    if i % 3 == 0:
                        wait_read(dve, ring0, ("lin", i))
                        c = i // 3
                        out, z0, z1 = qfT[:, CH * c:CH * (c + 1)], lt[:, i % 2, 0, :], lt[:, i % 2, 1, :]
                    else:
                        dve.wait_ge(s_lq, i - i // 3)
                        n = TPC * (i // 3) + 2 * (i % 3 - 1)
                        out = kf[:, n:n + 2, :]
                        z0, z1 = (lt[:, i % 2, a, 0:2 * D].rearrange("p (n d) -> p n d", n=2) for a in range(2))
                    v.tensor_tensor(out, z0, z1, ALU.add).then_inc(s_lind, 1)

            link(v.tensor_scalar(stdp[:, 1, :], stdp[:, 1, :], 1.0, None, ALU.add))
            link(v.reciprocal(stdp[:, 2, :], stdp[:, 1, :]))
            link(v.tensor_tensor(bd[:, 1, :].rearrange("p (h d) -> p h d", d=D0),
                                 blockm[:].rearrange("p (h d) -> p h d", d=D0),
                                 stdp[:, 2, :].unsqueeze(2).to_broadcast([P, H0, D0]), ALU.mult))
            items = 3 * NC
            dve.wait_ge(s_lin, 1)
            v.tensor_tensor(bd[:, 0, :], ps[:, 4, 0:D], bd[:, 1, :], ALU.mult)
            v.tensor_scalar(bsum[:], blockm[:].rearrange("p (h d) -> p h d", d=D0)[:, :, 0], ps[:, 4, D:D + 1], None,
                            ALU.mult).then_inc(s_lind, 1)
            dve.wait_ge(s_lind, items + 1)

            def quotients(c):
                dve.wait_ge(s_lin, 2 + c)
                ld = lden[:, c % 2]
                v.tensor_scalar(ld, ps[:, 5, 0:TPC * H0].rearrange("p (n h) -> p n h", n=TPC), 1e-6, None,
                                ALU.add).then_inc(s_lden, 1)
                dve.wait_ge(s_lden, c + 1)
                link(v.reciprocal(ld, ld))
                v.tensor_tensor(a_n[:, TPC * c:TPC * (c + 1), :].rearrange("p n (h d) -> p n h d", d=D0),
                                ps[:, c, :].rearrange("p (n h d) -> p n h d", n=TPC, h=H0),
                                ld.unsqueeze(3).to_broadcast([P, TPC, H0, D0]), ALU.mult).then_inc(s_lind, 1)

            def residual(c):
                dve.wait_ge(s_pj, c + 1)
                xc = x[:, TPC * c:TPC * (c + 1), :]
                ins = v.tensor_tensor(xc, ps[:, 6 + c % 2, :].rearrange("p (n d) -> p n d", n=TPC), xc, ALU.add)
                ins.then_inc(s_res, 1)
                dve.wait_ge(s_res, NC + c + 1)
                link(v.tensor_tensor(xc, xc, blin[:, 2, :].unsqueeze(1).to_broadcast([P, TPC, D]), ALU.add))
                statistics(TPC * c, TPC)

            for c in range(NC + 1):
                if c < NC:
                    quotients(c)
                if c:
                    residual(c - 1)
                if c >= 2:
                    dve.wait_ge(s_rstd, NORM["sd3", c - 2] + 1)
                    norm(TPC * (c - 2), TPC)
            dve.wait_ge(s_rstd, NORM["sd3", NC - 1] + 1)
            norm(TPC * (NC - 1), TPC)

            dve.wait_ge(s_g2, NC)
            v.memset(sq2[:], 0.0)
            link(v.memset(k2T[D1:D1 + 1, :, :].bitcast(F32), 1.0))

            def gates():
                sigs = sig[:].rearrange("p a n h e -> p (a n h) e")
                link(v.tensor_scalar(sig[:], sig[:], 1.0, None, ALU.add))
                link(v.reciprocal(sig[:], sig[:]))
                for r in range(1, E1):
                    ins = v.tensor_tensor(beats[:].rearrange("p a n h e -> p (a n h) e")[:, :, PAIRS[r]],
                                          sigs[:, :, r:E1], sigs[:, :, 0:E1 - r], ALU.is_gt)
                ins.then_inc(s_sig, 1)
                dve.wait_ge(s_sig, 1)
                link(ranks(v, link, 1))
                dve.wait_ge(s_rank, 1)
                link(v.tensor_scalar(rank[:], rank[:], TOP - 0.5, None, ALU.is_lt))
                v.tensor_copy(maskd[:], rank[:, 1])
                for i, a in enumerate((1, 0)):
                    ins = v.tensor_tensor(gate[:, :, i, :, :], sig[:, a], rank[:, a], ALU.mult)
                link(ins)

            for step in SEQ1:
                kind = step[0]
                if kind == "gates":
                    gates()
                elif kind == "w":
                    h = step[1]
                    dve.wait_ge(s_w, 48 * (h + 1))
                    if h:
                        wait_turn(dve, ring1, ("proj", h - 1, NT - 1, 2))
                    link(v.tensor_copy(wh[:], wraw[:]))
                    v.tensor_tensor(wl[:], wraw[:], wh[:].bitcast(F32), ALU.subtract).then_inc(s_wh, 1)
                elif kind == "proj":
                    _, h, n, j = step
                    m = NT * h + n
                    wait_turn(dve, ring1, step)
                    if m >= 2:
                        wait_experts(dve, m - 2)
                    v.tensor_tensor(gt[:, m % 2, j], ps[:, ring1.bank(step), 0:E1 * D1].rearrange(
                        "p (e d) -> p e d", e=E1), gate[:, n, min(j, 1), h, :].unsqueeze(2).to_broadcast([P, E1, D1]),
                        ALU.mult).then_inc(s_read1d, 1)
                    if m < NT and m % 2 and j == 2:
                        wait_read(dve, ring1, step)
                        g = gt[:, m % 2].rearrange("p j e d -> p j d e")
                        v.tensor_reduce(h_qk[:, :, n, :], g[:, 0:2], AX.X, ALU.add)
                        v.tensor_reduce(h_v[:, 0, n, :], g[:, 2], AX.X, ALU.add).then_inc(s_gaddv, 1)
                elif kind == "lo":
                    _, h, c = step
                    tiles = slice(TPC * c, TPC * (c + 1))
                    dve.wait_ge(s_hi1, NC * h + c + 1)
                    v.tensor_tensor(sk2[:, :, 0:D1], h_qk[:, 1, tiles, :], sk1[:, :, 0:D1], ALU.subtract)
                    v.tensor_tensor(sq1[:, :, D1:P], h_qk[:, 0, tiles, :], sq1[:, :, 0:D1],
                                    ALU.subtract).then_inc(s_st1, 1)
                elif kind == "max":
                    _, h, it, b = step
                    wait_turn(dve, ring1, step)
                    v.tensor_reduce(mxp1[:, it % TPC, b:b + 1], ps[:, ring1.bank(step), :],
                                    AX.X, ALU.max).then_inc(s_read1d, 1)
                    last = step
                elif kind == "m":
                    _, h, c = step
                    wait_read(dve, ring1, last)
                    if h or c:
                        dve.wait_ge(s_m1, NC * h + c)
                    if c:
                        wait_turn(dve, ring1, ("q2", h, c - 1))
                    elif h:
                        wait_turn(dve, ring1, ("q2", h - 1, NC - 1))
                    link(v.tensor_reduce(mx1[:], mxp1[:], AX.X, ALU.max))
                    v.tensor_scalar(sq2[:, :, D1:D1 + 1].bitcast(F32R), mx1[:].unsqueeze(2), -1.0, None,
                                    ALU.mult).then_inc(s_m1, 1)
                elif kind == "D":
                    u = step[1]
                    mc, m = u // M1, u % M1
                    dve.wait_ge(s_exp1, u + 1)
                    w, dn = (a.rearrange("p a q -> p (a q)")[:, 0:SHARE]
                             for a in (pbuf1[:, u % NP1, :, :], den[:, mc % 2, :, :]))
                    if m == 0:
                        if mc >= 2:
                            wait_turn(dve, ring1, ("F", mc - 2))
                        v.tensor_copy(dn, w).then_inc(s_den1, 1)
                    else:
                        dve.wait_ge(s_den1, u)
                        v.tensor_tensor(dn, dn, w, ALU.add).then_inc(s_den1, 1)
                elif kind == "F":
                    m = step[1]
                    wait_turn(dve, ring1, step)
                    if m:
                        dve.wait_ge(s_z, 2 * m - 1)
                        wait_read(dve, ring1, ("F", m - 1))
                    b = ring1.bank(step)
                    link(v.reciprocal(rd1[:], ps[:, b, TPC * D1:TPC * (D1 + 1)]))
                    v.tensor_tensor(on[:], ps[:, b, 0:TPC * D1].rearrange("p (n d) -> p n d", n=TPC),
                                    rd1[:].unsqueeze(2).to_broadcast([P, TPC, D1]), ALU.mult).then_inc(s_read1d, 1)
                elif kind == "y":
                    n = step[1]
                    wait_turn(dve, ring1, step)
                    v.tensor_tensor(x[:, n, :], ps[:, ring1.bank(step), 0:D], x[:, n, :],
                                    ALU.add).then_inc(s_read1d, 1)

        @block.gpsimd
        def _(pool):
            g_ = nc.gpsimd
            order = [0]

            def link(ins):
                order[0] += 1
                ins.then_inc(s_pool, 1)
                pool.wait_ge(s_pool, order[0])

            g_.memset(stageq[:, :, :, 24:32], 0.0)
            g_.memset(stagek[:, :, :, 24:25], 1.0)
            g_.memset(stagek[:, :, :, 25:32], 0.0)
            g_.memset(stagev[:, :, :, :, D0:D0 + 1].rearrange("p b n h r -> p (b n h) r"), 1.0)
            g_.memset(stagev[:, :, :, :, D0 + 1:32].rearrange("p b n h r -> p (b n h) r"), 0.0)
            g_.memset(power[:], -0.5)
            g_.memset(kM0[:].bitcast(F32), 0.0).then_inc(s_pconst, 1)
            pool.wait_ge(s_pconst, 1)
            pool.wait_ge(s_qkvev, NT)
            def deviation(step):
                tiles = slice(TPC * step[1], TPC * (step[1] + 1))
                pool.wait_ge(s_mv, 2 + NORM[step])
                link(g_.tensor_scalar(rstd[:, tiles], meanvar[:, tiles, 1], LN_EPS, None, ALU.add))
                g_.tensor_tensor(rstd[:, tiles], rstd[:, tiles], power[:], ALU.pow).then_inc(s_rstd, 1)

            for step in SEQ0:
                if step == ("rest", 1):
                    pool.wait_ge(s_ms, 3)
                    norm_and_rotate(g_, link, rest).then_inc(s_roped, 1)
                    pool.wait_ge(s_roped, 1)
                    g_.memset(kM1[:].bitcast(F32), 0.0).then_inc(s_pconst, 1)
                    pool.wait_ge(s_pconst, 2)
                elif step[0] == "stagek":
                    g = step[1]
                    if g >= 2:
                        pool.wait_ge(s_av, N0 * (g - 1))
                    gv = qkv[:, :, 2 * D + 32 * g:2 * D + 32 * (g + 1)].rearrange("p n (h d) -> p n h d", d=D0)
                    g_.tensor_copy(stagev[:, g % 2, :, :, 0:D0], gv).then_inc(s_stagev, 1)
                    pool.wait_ge(s_stagev, g + 1)
                elif step[0] in ("sd", "sd2"):
                    deviation(step)
            for c in range(NC):
                deviation(("sd3", c))
            for c in range(NC):
                pool.wait_ge(s_xnT, NC + c + 1)
                q = slice(CH * c, CH * (c + 1))
                g_.tensor_tensor(xl[:, q], xnT[:, q], xh[:, q].bitcast(F32), ALU.subtract).then_inc(s_xl, 1)
            pool.wait_ge(s_xl, NC)
            pool.wait_ge(s_g2, NC)
            pool.wait_ge(s_sig, 1)
            ranks(g_, link, 0).then_inc(s_rank, 1)
            link(g_.memset(z[:], 0.0))
            for step in SEQ1:
                if step[0] == "proj" and step[3] == 2:
                    _, h, n, _j = step
                    m = NT * h + n
                    if m < NT and m % 2:
                        continue
                    wait_read(pool, ring1, step)
                    if h and n == 0:
                        pool.wait_ge(s_st1, NC * h)
                    if h >= 2 and n == 0:
                        pool.wait_ge(s_av1, U1 * (h - 1))
                    t = gt[:, m % 2]
                    link(g_.tensor_tensor(gs[:], t[:, :, 0:2, :], t[:, :, 2:4, :], ALU.add))
                    link(g_.tensor_tensor(gsum[:], gs[:, :, 0, :], gs[:, :, 1, :], ALU.add))
                    g_.tensor_tensor(h_qk[:, :, n, :], gsum[:, 0:2, :], t[:, 0:2, 4, :], ALU.add)
                    g_.tensor_tensor(h_v[:, h % 2, n, :], gsum[:, 2, :], t[:, 2, 4, :], ALU.add).then_inc(s_gadd, 1)
                elif step[0] == "D":
                    u = step[1]
                    mc, m = u // M1, u % M1
                    pool.wait_ge(s_exp1, u + 1)
                    w, dn = (a.rearrange("p a q -> p (a q)")[:, SHARE:]
                             for a in (pbuf1[:, u % NP1, :, :], den[:, mc % 2, :, :]))
                    if m == 0:
                        if mc >= 2:
                            wait_turn(pool, ring1, ("F", mc - 2))
                        g_.tensor_copy(dn, w).then_inc(s_den1p, 1)
                    else:
                        pool.wait_ge(s_den1p, u)
                        g_.tensor_tensor(dn, dn, w, ALU.add).then_inc(s_den1p, 1)
                    if m == M1 - 1:
                        pool.wait_ge(s_den1p, u + 1)
                        pool.wait_ge(s_den1, u + 1)
                        dn = den[:, mc % 2, 0, :]
                        g_.tensor_tensor(dn, dn, den[:, mc % 2, 1, :], ALU.add).then_inc(s_den1s, 1)
                elif step[0] == "F":
                    mc = step[1]
                    h, c = mc // NC, mc % NC
                    wait_read(pool, ring1, step)
                    tiles = slice(TPC * c, TPC * (c + 1))
                    g_.tensor_tensor(onm[:], on[:].unsqueeze(2).to_broadcast([P, TPC, E1, D1]),
                                     maskd[:, tiles, h, :].unsqueeze(3).to_broadcast([P, TPC, E1, D1]),
                                     ALU.mult).then_inc(s_z, 1)
                    pool.wait_ge(s_z, 2 * mc + 1)
                    g_.tensor_tensor(z[:, tiles], z[:, tiles], onm[:], ALU.add).then_inc(s_z, 1)
                    pool.wait_ge(s_z, 2 * mc + 2)


_INPUTS = {
    "x": "L0_attn_x", "qnw": "L0_attn_q_norm_w", "knw": "L0_attn_k_norm_w", "wre": "L0_ffn_w_freq_real",
    "wim": "L0_ffn_w_freq_imag", "bias0": "L0_ffn_bias", "lbq": "L1_attn_bq", "lbk": "L1_attn_bk",
    "lbv": "L1_attn_bv", "lbo": "L1_attn_bo", "stdp": "L1_attn_stdp", "Ws": "L1_ffn_Ws", "Wd": "L1_ffn_Wd",
    "Wq": "L1_ffn_Wq", "Wkv": "L1_ffn_Wkv",
}
_TRANSPOSED = {"wqkvT": "L0_attn_w_qkv", "wprojT": "L0_attn_w_proj", "lWq": "L1_attn_Wq", "lWk": "L1_attn_Wk",
               "lWv": "L1_attn_Wv", "lWo": "L1_attn_Wo"}


def constants():
    f32 = np.float32
    freqs = (f32(32.0) ** (-np.arange(0, D0, 2, dtype=f32) / f32(D0))).astype(f32)
    ang = (np.arange(T, dtype=f32)[:, None] * freqs[None, :]).astype(f32).astype(np.float64)
    a = 2 * np.pi * (np.outer(np.arange(D), np.arange(D)) % D) / D
    i, j = np.arange(P)[:, None], np.arange(P)[None, :]
    return {
        "ident": np.eye(P, dtype=f32),
        "rope": np.stack([np.cos(ang), np.sin(ang)], 1).astype(f32),
        "masks": np.stack([np.where(j > i, NEG, 0.0), np.where(i > j, NEG, 0.0)]).astype(f32),
        "dft": np.stack([np.cos(a), np.sin(a)]).astype(f32),
        "blockm": (i // D0 == j // D0).astype(f32),
        "fold": np.concatenate([np.eye(D1), np.eye(D1)]).astype(f32),
    }


def kernel(**inputs):
    import concourse.bacc as _bacc
    from concourse.bass_utils import run_bass_kernel_spmd as _run

    arrays = {k: np.ascontiguousarray(inputs[v]) for k, v in _INPUTS.items()}
    arrays["x"] = arrays["x"].reshape(T, D)
    arrays |= {k: np.ascontiguousarray(np.asarray(inputs[v]).T) for k, v in _TRANSPOSED.items()}
    wo = np.asarray(inputs["L1_ffn_Wo"]).reshape(D1, E1, D).transpose(1, 0, 2)
    arrays["Wo"] = np.ascontiguousarray(wo).reshape(E1 * D1, D)
    arrays |= constants()
    nc = _bacc.Bacc("TRN2", target_bir_lowering=False, num_devices=1)
    aps = {k: nc.dram_tensor(f"in_{k}", a.shape, mybir.dt.from_np(a.dtype), kind="ExternalInput").ap()
           for k, a in arrays.items()}
    aps["out"] = nc.dram_tensor("out_0", (T, D), F32, kind="ExternalOutput").ap()
    build(nc, aps)
    r = _run(nc, [{f"in_{k}": a for k, a in arrays.items()}], core_ids=[0])
    return r.results[0]["out_0"].reshape(1, T, D)
```
